# Optimizing a Trainium2 kernel written in Bass

```python
import numpy as np
import jax
import jax.numpy as jnp

def _softmax(x, axis=-1):
    return jax.nn.softmax(x, axis=axis)

def _gelu(x):
    return jax.nn.gelu(x, approximate=True)

def _silu(x):
    return jax.nn.silu(x)

def _sigmoid(x):
    return jax.nn.sigmoid(x)

def _layernorm(x, axis=-1, eps=1e-05):
    m = jnp.mean(x, axis=axis, keepdims=True)
    v = jnp.var(x, axis=axis, keepdims=True)
    return (x - m) / jnp.sqrt(v + eps)

def _scatter_add(tgt, idx, src, axis=0):
    return tgt.at[idx].add(src)

def _segment_sum(src, seg, n):
    return jax.ops.segment_sum(src, seg, n)
kernel_name = 'mk_seq_preln_d1_jaxref_r4_4fa99f'

def setup_inputs(seed: int=0):
    np.random.seed(seed)
    _w = jnp.asarray

    def _L0_attn_setup():
        import jax, jax.numpy as jnp
        import numpy as np
        N_HIDDEN = 512
        N_HEADS = 64
        EXPAND = 2
        D_STATE = 128
        D_CONV = 4
        CHUNK = 128
        DT_MIN = 0.001
        DT_MAX = 0.1
        INNER = EXPAND * N_HIDDEN
        HEAD_DIM = INNER // N_HEADS
        CONV_DIM = INNER + 2 * D_STATE
        D_IN_PROJ = 2 * INNER + 2 * D_STATE + N_HEADS
        EPS = 1e-06

        def _segsum(x):
            t = x.shape[-1]
            cs = jnp.cumsum(x, axis=-1)
            seg = cs[..., :, None] - cs[..., None, :]
            mask = jnp.tril(jnp.ones((t, t), dtype=bool))
            return jnp.where(mask, seg, -jnp.inf)

        def _ssd(x, dt, a, b_mat, c_mat, d, dt_bias):
            bsz, seq, h, p = x.shape
            dt = jnp.clip(jax.nn.softplus(dt + dt_bias), DT_MIN, DT_MAX)
            d_res = d.reshape(1, 1, h, 1) * x
            x_disc = x * dt[..., None]
            a_disc = a * dt
            ch = lambda t_: t_.reshape(bsz, seq // CHUNK, CHUNK, *t_.shape[2:])
            x_blk, b_blk, c_blk = (ch(x_disc), ch(b_mat), ch(c_mat))
            a_blk = jnp.transpose(ch(a_disc), (0, 3, 1, 2))
            a_cum = jnp.cumsum(a_blk, axis=-1)
            l_mat = jnp.exp(_segsum(a_blk))
            y_diag = jnp.einsum('bclhn,bcshn,bhcls,bcshp->bclhp', c_blk, b_blk, l_mat, x_blk)
            decay_states = jnp.exp(a_cum[..., -1:] - a_cum)
            states = jnp.einsum('bclhn,bhcl,bclhp->bchpn', b_blk, decay_states, x_blk)
            states = jnp.concatenate([jnp.zeros_like(states[:, :1]), states], axis=1)
            a_end = jnp.pad(a_cum[..., -1], ((0, 0), (0, 0), (1, 0)))
            decay_chunk = jnp.exp(_segsum(a_end))
            new_states = jnp.einsum('bhzc,bchpn->bzhpn', decay_chunk, states)
            states = new_states[:, :-1]
            y_off = jnp.einsum('bclhn,bchpn,bhcl->bclhp', c_blk, states, jnp.exp(a_cum))
            y = (y_diag + y_off).reshape(bsz, seq, h, p)
            return y + d_res
        key = jax.random.key(seed)
        ks = jax.random.split(key, 10)
        B, L = (2, 512)
        s = lambda fan_in: 1.0 / np.sqrt(fan_in)
        return {'x': jax.random.normal(ks[0], (B, L, N_HIDDEN), jnp.float32), 'W_in': jax.random.normal(ks[1], (N_HIDDEN, D_IN_PROJ), jnp.float32) * s(N_HIDDEN), 'b_in': jnp.zeros((D_IN_PROJ,), jnp.float32), 'conv_w': jax.random.normal(ks[2], (D_CONV, 1, CONV_DIM), jnp.float32) * s(D_CONV), 'conv_b': jnp.zeros((CONV_DIM,), jnp.float32), 'A_log': jnp.log(jnp.arange(1, N_HEADS + 1, dtype=jnp.float32)), 'dt_bias': jax.random.normal(ks[3], (N_HEADS,), jnp.float32) * 0.1, 'D_param': jnp.ones((N_HEADS,), jnp.float32), 'norm_w': jnp.ones((INNER,), jnp.float32), 'W_out': jax.random.normal(ks[4], (INNER, N_HIDDEN), jnp.float32) * s(INNER), 'b_out': jnp.zeros((N_HIDDEN,), jnp.float32)}
    _L0_attn_in = _L0_attn_setup()

    def _L0_ffn_setup():
        import jax, jax.numpy as jnp
        import numpy as np
        E = 32
        K = 4
        G = 4
        TG = 2
        H = 512
        F = 256
        FS = 512
        SCALE = 2.0
        B, S = (2, 256)
        N = B * S
        CAP = 2 * (N * K // E)

        def _gate(x, gate_w, gate_bias):
            logits = x @ gate_w.T
            scores = jax.nn.sigmoid(logits)
            sc = scores + gate_bias
            n = x.shape[0]
            grp = sc.reshape(n, G, E // G)
            group_scores = jax.lax.top_k(grp, 2)[0].sum(-1)
            _, gidx = jax.lax.top_k(group_scores, TG)
            gmask = jnp.zeros((n, G), sc.dtype).at[jnp.arange(n)[:, None], gidx].set(1.0)
            smask = jnp.repeat(gmask, E // G, axis=1)
            tmp = jnp.where(smask > 0, sc, 0.0)
            _, topk_idx = jax.lax.top_k(tmp, K)
            topk_w = jnp.take_along_axis(scores, topk_idx, axis=1)
            topk_w = topk_w / (topk_w.sum(-1, keepdims=True) + 1e-20)
            return (topk_idx, topk_w * SCALE)

        def _moe(x, topk_idx, topk_w, w1, w2, w3):
            n = x.shape[0]
            flat_e = topk_idx.reshape(-1)
            oh = jax.nn.one_hot(flat_e, E, dtype=jnp.int32)
            pos = (jnp.cumsum(oh, axis=0) * oh).sum(-1) - 1
            keep = pos < CAP
            slot = jnp.where(keep, pos, CAP)
            x_rep = jnp.repeat(x, K, axis=0)
            buf = jnp.zeros((E, CAP, H), x.dtype).at[flat_e, slot].set(x_rep, mode='drop')
            h = jax.nn.silu(jnp.einsum('ech,ehf->ecf', buf, w1)) * jnp.einsum('ech,ehf->ecf', buf, w3)
            ob = jnp.einsum('ecf,efh->ech', h, w2)
            y = ob[flat_e, jnp.minimum(slot, CAP - 1)]
            y = jnp.where(keep[:, None], y, 0.0)
            return (y.reshape(n, K, H) * topk_w[:, :, None]).sum(1)
        key = jax.random.key(seed)
        ks = jax.random.split(key, 9)
        w = 0.02
        return {'hidden_states': jax.random.normal(ks[0], (B, S, H), jnp.float32), 'gate_w': jax.random.normal(ks[1], (E, H), jnp.float32) * w, 'gate_bias': jax.random.normal(ks[2], (E,), jnp.float32) * w, 'w1': jax.random.normal(ks[3], (E, H, F), jnp.float32) * w, 'w2': jax.random.normal(ks[4], (E, F, H), jnp.float32) * w, 'w3': jax.random.normal(ks[5], (E, H, F), jnp.float32) * w, 'shared_gate': jax.random.normal(ks[6], (H, FS), jnp.float32) * w, 'shared_up': jax.random.normal(ks[7], (H, FS), jnp.float32) * w, 'shared_down': jax.random.normal(ks[8], (FS, H), jnp.float32) * w}
    _L0_ffn_in = _L0_ffn_setup()
    _d = {'L0_attn_x': _L0_attn_in['x'], 'L0_attn_W_in': _L0_attn_in['W_in'], 'L0_attn_b_in': _L0_attn_in['b_in'], 'L0_attn_conv_w': _L0_attn_in['conv_w'], 'L0_attn_conv_b': _L0_attn_in['conv_b'], 'L0_attn_A_log': _L0_attn_in['A_log'], 'L0_attn_dt_bias': _L0_attn_in['dt_bias'], 'L0_attn_D_param': _L0_attn_in['D_param'], 'L0_attn_norm_w': _L0_attn_in['norm_w'], 'L0_attn_W_out': _L0_attn_in['W_out'], 'L0_attn_b_out': _L0_attn_in['b_out'], 'L0_ffn_gate_w': _L0_ffn_in['gate_w'], 'L0_ffn_gate_bias': _L0_ffn_in['gate_bias'], 'L0_ffn_w1': _L0_ffn_in['w1'], 'L0_ffn_w2': _L0_ffn_in['w2'], 'L0_ffn_w3': _L0_ffn_in['w3'], 'L0_ffn_shared_gate': _L0_ffn_in['shared_gate'], 'L0_ffn_shared_up': _L0_ffn_in['shared_up'], 'L0_ffn_shared_down': _L0_ffn_in['shared_down']}
    _x0 = _d['L0_attn_x']
    _d['L0_attn_x'] = jax.random.normal(jax.random.fold_in(jax.random.key(seed), 1), (4, 512, 512), dtype=_x0.dtype)
    del _x0
    return _d

def reference(L0_attn_x, L0_attn_W_in, L0_attn_b_in, L0_attn_conv_w, L0_attn_conv_b, L0_attn_A_log, L0_attn_dt_bias, L0_attn_D_param, L0_attn_norm_w, L0_attn_W_out, L0_attn_b_out, L0_ffn_gate_w, L0_ffn_gate_bias, L0_ffn_w1, L0_ffn_w2, L0_ffn_w3, L0_ffn_shared_gate, L0_ffn_shared_up, L0_ffn_shared_down):

    def _L0_attn_ref(x, W_in, b_in, conv_w, conv_b, A_log, dt_bias, D_param, norm_w, W_out, b_out):
        import jax, jax.numpy as jnp
        import numpy as np
        N_HIDDEN = 512
        N_HEADS = 64
        EXPAND = 2
        D_STATE = 128
        D_CONV = 4
        CHUNK = 128
        DT_MIN = 0.001
        DT_MAX = 0.1
        INNER = EXPAND * N_HIDDEN
        HEAD_DIM = INNER // N_HEADS
        CONV_DIM = INNER + 2 * D_STATE
        D_IN_PROJ = 2 * INNER + 2 * D_STATE + N_HEADS
        EPS = 1e-06

        def _segsum(x):
            t = x.shape[-1]
            cs = jnp.cumsum(x, axis=-1)
            seg = cs[..., :, None] - cs[..., None, :]
            mask = jnp.tril(jnp.ones((t, t), dtype=bool))
            return jnp.where(mask, seg, -jnp.inf)

        def _ssd(x, dt, a, b_mat, c_mat, d, dt_bias):
            bsz, seq, h, p = x.shape
            dt = jnp.clip(jax.nn.softplus(dt + dt_bias), DT_MIN, DT_MAX)
            d_res = d.reshape(1, 1, h, 1) * x
            x_disc = x * dt[..., None]
            a_disc = a * dt
            ch = lambda t_: t_.reshape(bsz, seq // CHUNK, CHUNK, *t_.shape[2:])
            x_blk, b_blk, c_blk = (ch(x_disc), ch(b_mat), ch(c_mat))
            a_blk = jnp.transpose(ch(a_disc), (0, 3, 1, 2))
            a_cum = jnp.cumsum(a_blk, axis=-1)
            l_mat = jnp.exp(_segsum(a_blk))
            y_diag = jnp.einsum('bclhn,bcshn,bhcls,bcshp->bclhp', c_blk, b_blk, l_mat, x_blk)
            decay_states = jnp.exp(a_cum[..., -1:] - a_cum)
            states = jnp.einsum('bclhn,bhcl,bclhp->bchpn', b_blk, decay_states, x_blk)
            states = jnp.concatenate([jnp.zeros_like(states[:, :1]), states], axis=1)
            a_end = jnp.pad(a_cum[..., -1], ((0, 0), (0, 0), (1, 0)))
            decay_chunk = jnp.exp(_segsum(a_end))
            new_states = jnp.einsum('bhzc,bchpn->bzhpn', decay_chunk, states)
            states = new_states[:, :-1]
            y_off = jnp.einsum('bclhn,bchpn,bhcl->bclhp', c_blk, states, jnp.exp(a_cum))
            y = (y_diag + y_off).reshape(bsz, seq, h, p)
            return y + d_res
        B, L, _ = x.shape
        zxbcdt = x @ W_in + b_in
        z = zxbcdt[..., :INNER]
        xBC = zxbcdt[..., INNER:INNER + CONV_DIM]
        dt = zxbcdt[..., -N_HEADS:]
        xp = jnp.pad(xBC, ((0, 0), (D_CONV - 1, 0), (0, 0)))
        xBC = jax.lax.conv_general_dilated(xp, conv_w, window_strides=(1,), padding='VALID', dimension_numbers=('NWC', 'WIO', 'NWC'), feature_group_count=CONV_DIM) + conv_b
        xBC = jax.nn.silu(xBC)
        x_ssm = xBC[..., :INNER].reshape(B, L, N_HEADS, HEAD_DIM)
        b_mat = jnp.broadcast_to(xBC[..., INNER:INNER + D_STATE][:, :, None, :], (B, L, N_HEADS, D_STATE))
        c_mat = jnp.broadcast_to(xBC[..., INNER + D_STATE:][:, :, None, :], (B, L, N_HEADS, D_STATE))
        a = -jnp.exp(A_log)
        y = _ssd(x_ssm, dt, a, b_mat, c_mat, D_param, dt_bias)
        y = y.reshape(B, L, INNER)
        y = y * jax.nn.silu(z)
        y = y * jax.lax.rsqrt(jnp.mean(y * y, axis=-1, keepdims=True) + EPS) * norm_w
        return y @ W_out + b_out

    def _L0_ffn_ref(hidden_states, gate_w, gate_bias, w1, w2, w3, shared_gate, shared_up, shared_down):
        import jax, jax.numpy as jnp
        import numpy as np
        E = 32
        K = 4
        G = 4
        TG = 2
        H = 512
        F = 256
        FS = 512
        SCALE = 2.0
        B, S = (2, 256)
        N = B * S
        CAP = 2 * (N * K // E)

        def _gate(x, gate_w, gate_bias):
            logits = x @ gate_w.T
            scores = jax.nn.sigmoid(logits)
            sc = scores + gate_bias
            n = x.shape[0]
            grp = sc.reshape(n, G, E // G)
            group_scores = jax.lax.top_k(grp, 2)[0].sum(-1)
            _, gidx = jax.lax.top_k(group_scores, TG)
            gmask = jnp.zeros((n, G), sc.dtype).at[jnp.arange(n)[:, None], gidx].set(1.0)
            smask = jnp.repeat(gmask, E // G, axis=1)
            tmp = jnp.where(smask > 0, sc, 0.0)
            _, topk_idx = jax.lax.top_k(tmp, K)
            topk_w = jnp.take_along_axis(scores, topk_idx, axis=1)
            topk_w = topk_w / (topk_w.sum(-1, keepdims=True) + 1e-20)
            return (topk_idx, topk_w * SCALE)

        def _moe(x, topk_idx, topk_w, w1, w2, w3):
            n = x.shape[0]
            flat_e = topk_idx.reshape(-1)
            oh = jax.nn.one_hot(flat_e, E, dtype=jnp.int32)
            pos = (jnp.cumsum(oh, axis=0) * oh).sum(-1) - 1
            keep = pos < CAP
            slot = jnp.where(keep, pos, CAP)
            x_rep = jnp.repeat(x, K, axis=0)
            buf = jnp.zeros((E, CAP, H), x.dtype).at[flat_e, slot].set(x_rep, mode='drop')
            h = jax.nn.silu(jnp.einsum('ech,ehf->ecf', buf, w1)) * jnp.einsum('ech,ehf->ecf', buf, w3)
            ob = jnp.einsum('ecf,efh->ech', h, w2)
            y = ob[flat_e, jnp.minimum(slot, CAP - 1)]
            y = jnp.where(keep[:, None], y, 0.0)
            return (y.reshape(n, K, H) * topk_w[:, :, None]).sum(1)
        b, s, h = hidden_states.shape
        x = hidden_states.reshape(-1, h)
        topk_idx, topk_w = _gate(x, gate_w, gate_bias)
        out = _moe(x, topk_idx, topk_w, w1, w2, w3)
        shared = jax.nn.silu(x @ shared_gate) * (x @ shared_up) @ shared_down
        return (out + shared).reshape(b, s, h)
    x = L0_attn_x
    x = x + _L0_attn_ref(_layernorm(x, axis=-1), L0_attn_W_in, L0_attn_b_in, L0_attn_conv_w, L0_attn_conv_b, L0_attn_A_log, L0_attn_dt_bias, L0_attn_D_param, L0_attn_norm_w, L0_attn_W_out, L0_attn_b_out)
    x = x + _L0_ffn_ref(_layernorm(x, axis=-1), L0_ffn_gate_w, L0_ffn_gate_bias, L0_ffn_w1, L0_ffn_w2, L0_ffn_w3, L0_ffn_shared_gate, L0_ffn_shared_up, L0_ffn_shared_down)
    return x

_drawn_inputs = setup_inputs


def setup_inputs(seed=0):
    import zlib

    import numpy as np

    out = dict(_drawn_inputs(seed))
    spreads = {'L0_attn_b_in': (0.0, 0.1),
     'L0_attn_conv_b': (0.0, 0.1),
     'L0_attn_D_param': (1.0, 0.2),
     'L0_attn_norm_w': (1.0, 0.2),
     'L0_attn_b_out': (0.0, 0.1)}
    factors = {'L0_attn_dt_bias': 8.0,
     'L0_ffn_gate_w': 3.523,
     'L0_ffn_gate_bias': 6.1,
     'L0_ffn_w1': 3.415,
     'L0_ffn_w2': 3.338,
     'L0_ffn_w3': 3.35}
    for name, (base, spread) in spreads.items():
        noise = np.random.default_rng([zlib.crc32(name.encode()), seed]).standard_normal(out[name].shape)
        drawn = base * np.exp(spread * noise) if base else spread * noise
        out[name] = jnp.asarray(drawn.astype(out[name].dtype))
    for name, factor in factors.items():
        out[name] = (out[name] * factor).astype(out[name].dtype)
    return out
```

```python
from contextlib import ExitStack

import concourse.bass as bass
from concourse import mybir

ALU = mybir.AluOpType
ACT = mybir.ActivationFunctionType
AX = mybir.AxisListType
F32 = mybir.dt.float32
BF16 = mybir.dt.bfloat16
I32 = mybir.dt.int32
U32 = mybir.dt.uint32

P = 128
HID = 512
KH = HID // P
INNER = 1024
HEADS = 64
HD = INNER // HEADS
KI = INNER // P
CT = (INNER + 2 * P) // P
TAPS = 4
HALO = TAPS - 1
Z0, X0, B0, DT0 = 0, INNER, 2 * INNER, 2 * INNER + 2 * P
PROJ = DT0 + HEADS
TOKENS = 2048
CHUNKS = TOKENS // P
PER_SEQ = 4
LN_EPS, RMS_EPS = 1e-5, 1e-6
DT_MIN, DT_MAX = 1e-3, 1e-1
PIECES = 4
PH = HEADS // PIECES

EXPERTS = 32
GROUPS = 4
GE = EXPERTS // GROUPS
TOPK = 4
CAP = 128
F = 256
KF = F // P
FS = 512
KS = FS // P
ROUTED_SCALE = 2.0
IDC = 6


def wait(eng, sem, value):
    if isinstance(value, int) and value <= 0:
        return
    eng.wait_ge(sem, value)


class Own:

    def __init__(self, eng, sem, rate, n):
        self.eng, self.sem, self.rate, self.n, self.k = eng, sem, rate, n, 0

    def then(self, ins):
        self.k += 1
        ins.then_inc(self.sem, 1)
        self.eng.wait_ge(self.sem, self.rate * self.n + self.k)

    def close(self):
        assert self.k == self.rate, (self.k, self.rate)


class Chunk:

    def __init__(self, n, p, h):
        self.n, self.p, self.h = n, p, h


def run_steps(eng, step, loads_ahead=False):
    last = CHUNKS - 1

    def at(n):
        return Chunk(n, n % 2, n // 2) if 0 <= n <= last else None

    def peeled(n):
        step(at(n), at(n - 1), at(n + 2) if loads_ahead else at(n + 1))

    for n in range(3):
        peeled(n)
    with eng.Fori(1, 6 if loads_ahead else 7) as i:
        step(Chunk(2 * i + 1, 1, i), Chunk(2 * i, 0, i), Chunk(2 * i + 2, 0, i + 1))
        step(Chunk(2 * i + 2, 0, i + 1), Chunk(2 * i + 1, 1, i), Chunk(2 * i + 3, 1, i + 1))
    for n in range(13 if loads_ahead else 15, CHUNKS + 1):
        peeled(n)


def over_heads(ap, width):
    return ap.unsqueeze(2).to_broadcast([ap.shape[0], ap.shape[1], width])


def mamba_stage(nc, x, W_in, b_in, conv_w, conv_b, A_log, dt_bias, D_param, norm_w, W_out, b_out,
                cum_dram, x2_dram):
    with ExitStack() as ctx:
        def sb(name, shape, dt=F32):
            return ctx.enter_context(nc.sbuf_tensor(name, shape, dt))

        def sem(name):
            return ctx.enter_context(nc.semaphore(name))

        bank = [ctx.enter_context(nc.psum_tensor(f"bank{i}", [P, 512], F32)) for i in range(8)]

        win = sb("win", [P, KH, PROJ])
        wout = sb("wout", [P, KI, HID])
        ident = sb("ident", [P, P])
        tri = sb("tri", [P, P])
        ones = sb("ones", [P, P])
        keep = sb("keep", [P, CHUNKS])
        half_exp = sb("half_exp", [P, 1])
        rows = sb("rows", [68, P])
        cols = sb("cols", [P, 68])
        hw = sb("hw", [P, TAPS * CT])
        hb = sb("hb", [P, CT])
        zb = sb("zb", [P, INNER])
        bo = sb("bo", [P, HID])
        bdt = sb("bdt", [P, HEADS])
        bdt2 = sb("bdt2", [P, HEADS])
        neg_a = sb("neg_a", [P, HEADS])
        dpar = sb("dpar", [P, HEADS])
        x_in = sb("x_in", [P, 2, HID])
        xb = sb("xb", [P, 2, HID])
        stat = sb("stat", [P, 6])
        mv = sb("mv", [P, 2])
        carrier = sb("carrier", [P, 1])
        eps = sb("eps", [P, 2])
        vpe = sb("vpe", [P, 1])
        rstd = sb("rstd", [P, 1])
        xn = sb("xn", [P, HID])
        xnT = sb("xnT", [P, KH, P])
        dtm = sb("dtm", [P, HEADS])
        edt = sb("edt", [P, HEADS])
        den = sb("den", [P, HEADS])
        sw = sb("sw", [P, HEADS])
        sw2 = sb("sw2", [P, HEADS])
        poly = sb("poly", [P, HEADS])
        dts = sb("dts", [P, 2, HEADS])
        adt = sb("adt", [P, HEADS])
        cum = sb("cum", [P, 3, HEADS])
        ecum = sb("ecum", [P, 3, HEADS])
        ekeep = sb("ekeep", [P, 2, 2, HEADS])
        cum_s = sb("cum_s", [P, 2, HEADS])
        wdec = sb("wdec", [P, 2, HEADS])
        cumT = sb("cumT", [HEADS, P])
        cin = sb("cin", [P, CT, HALO + P])
        cv = sb("cv", [P, CT, P])
        th = sb("th", [P, CT, P])
        ct = sb("ct", [P, 2, P])
        sz = sb("sz", [P, 2, INNER])
        tz = sb("tz", [P, INNER])
        cbm = sb("cbm", [P, 2, P])
        bs = sb("bs", [P, 2, P])
        xs = sb("xs", [P, 2, INNER])
        xd = sb("xd", [P, 2, INNER])
        xdec = sb("xdec", [P, 2, INNER])
        cumb = sb("cumb", [P, 2, PH, P])
        L = sb("L", [P, PIECES, PH, P])
        S = sb("S", [P, INNER])
        y = sb("y", [P, INNER])
        yT = sb("yT", [P, KI, P])
        ssq = sb("ssq", [P, 1])
        vpe2 = sb("vpe2", [P, 1])
        rstd2 = sb("rstd2", [P, 1])
        x2o = sb("x2o", [P, 2, HID])

        win_in = sem("win_in"); wout_in = sem("wout_in"); vec_in = sem("vec_in")
        x_ld = [sem("x_ld0"), sem("x_ld1")]
        cum_st = sem("cum_st")
        cumb_ld = [sem("cumb_ld0"), sem("cumb_ld1")]
        x2_st = [sem("x2_st0"), sem("x2_st1")]
        pool_set = sem("pool_set"); consts = sem("consts"); cols_ps = sem("cols_ps")
        vset = sem("vset"); aset = sem("aset"); params = sem("params"); s_zero = sem("s_zero")
        xnT_ps = sem("xnT_ps"); dt_ps = sem("dt_ps"); bc_ps = sem("bc_ps"); z_ps = sem("z_ps")
        cum_ps = sem("cum_ps"); diag_ps = sem("diag_ps"); off_ps = sem("off_ps")
        state_ps = sem("state_ps"); cb_ps = sem("cb_ps"); x_ps = sem("x_ps"); yT_ps = sem("yT_ps")
        out_ps = sem("out_ps"); xT_ps = sem("xT_ps")
        v_own = sem("v_own"); v_own2 = sem("v_own2")
        var_rd = sem("var_rd"); xn_rd = sem("xn_rd"); dtm_rd = sem("dtm_rd"); adt_rd = sem("adt_rd")
        bc_ev = sem("bc_ev"); bcc_rd = sem("bcc_rd"); z_ev = sem("z_ev"); cumT_rd = sem("cumT_rd")
        dif_rd = sem("dif_rd"); bct_rd = sem("bct_rd"); wdec_rd = sem("wdec_rd"); m_rd = sem("m_rd")
        off_ev = sem("off_ev"); y_rd = sem("y_rd"); S_rd = sem("S_rd"); cb_rd = sem("cb_rd")
        xc_rd = sem("xc_rd"); xt_rd = sem("xt_rd"); x2_rd = sem("x2_rd")
        xnT_rd = sem("xnT_rd"); edt_rd = sem("edt_rd"); tbc_rd = sem("tbc_rd"); tz_rd = sem("tz_rd")
        ecum_rd = sem("ecum_rd"); l_rd = sem("l_rd"); ssq_rd = sem("ssq_rd"); yT_rd = sem("yT_rd")
        tx_rd = sem("tx_rd"); seg_rd = sem("seg_rd"); xs_rd = sem("xs_rd")
        g_var = sem("g_var"); g_ssq = sem("g_ssq"); g_xdec = sem("g_xdec"); rstd_rd = sem("rstd_rd"); rstd2_rd = sem("rstd2_rd")
        xb_rd = sem("xb_rd"); s_dec = sem("s_dec"); xd_rd = sem("xd_rd")

        block = ctx.enter_context(nc.Block())

        x_rows = x.rearrange("b (c p) h -> (b c) p h", p=P)
        x2_rows = x2_dram.rearrange("(c p) h -> c p h", p=P)

        @block.sync
        def _(sp):
            def load_x(c):
                sp.dma_start(x_in[:, c.p, :], x_rows[c.n, :, :]).then_inc(x_ld[c.p], 16)

            load_x(Chunk(0, 0, 0))
            load_x(Chunk(1, 1, 0))
            for k in range(KH):
                sp.dma_start(win[:, k, :], W_in[k * P:(k + 1) * P, :]).then_inc(win_in, 16)
            sp.dma_start(wout[:, :, :], W_out.rearrange("(k p) h -> p k h", p=P)).then_inc(wout_in, 16)

            def step(cur, prev, nxt):
                if cur:
                    n = cur.n
                    wait(sp, cumT_rd, n + 1)
                    sp.dma_start(cum_dram[cur.p], cumT[:, :]).then_inc(cum_st, 16)
                    wait(sp, cum_st, 16 * n + 16)
                    back = cum_dram[cur.p].rearrange("(q h) l -> q (h l)", q=PIECES)

                    def piece(q):
                        wait(sp, l_rd, 4 * n + q - 1)
                        sp.dma_start(cumb[:, q % 2].rearrange("p h l -> p (h l)"),
                                     back[q:q + 1, :].to_broadcast([P, PH * P])).then_inc(cumb_ld[q % 2], 16)

                    for q in range(PIECES):
                        piece(q)
                    if nxt:
                        wait(sp, xb_rd, n + 1)
                        wait(sp, xn_rd, n + 1)
                        sp.dma_start(x_in[:, cur.p, :], x_rows[n + 2, :, :]).then_inc(x_ld[cur.p], 16)
                if prev:
                    wait(sp, x2_rd, prev.n + 1)
                    sp.dma_start(x2_rows[prev.n, :, :], x2o[:, prev.p, :]).then_inc(x2_st[prev.p], 16)

            run_steps(sp, step, loads_ahead=True)
            for p in range(2):
                wait(sp, x2_st[p], 16 * (CHUNKS // 2))

        @block.gpsimd
        def _(pool):
            nc.gpsimd.memset(ident[:, :], 0.0).then_inc(pool_set, 1)
            nc.gpsimd.memset(tri[:, :], 1.0).then_inc(pool_set, 1)
            nc.gpsimd.memset(ones[:, :], 1.0).then_inc(consts, 1)
            nc.gpsimd.memset(half_exp[:, :], -0.5).then_inc(pool_set, 1)
            nc.gpsimd.memset(eps[:, 0:1], LN_EPS).then_inc(pool_set, 1)
            nc.gpsimd.memset(eps[:, 1:2], RMS_EPS).then_inc(pool_set, 1)
            nc.gpsimd.memset(keep[:, :], 1.0).then_inc(pool_set, 1)
            pool.wait_ge(pool_set, 6)
            nc.gpsimd.affine_select(out=ident[:, :], in_=ident[:, :], compare_op=ALU.not_equal, fill=1.0,
                                    base=0, pattern=[[-1, P]], channel_multiplier=1).then_inc(consts, 1)
            nc.gpsimd.affine_select(out=tri[:, :], in_=tri[:, :], compare_op=ALU.is_ge, fill=0.0,
                                    base=0, pattern=[[1, P]], channel_multiplier=-1).then_inc(consts, 1)
            nc.gpsimd.memset(keep[:, :].rearrange("p (s c) -> p s c", c=PER_SEQ)[:, :, 0:1], 0.0)\
                .then_inc(consts, 1)
            nc.gpsimd.memset(S[:, :], 0.0).then_inc(S_rd, 1)
            nc.gpsimd.memset(cin[:, :, :], 0.0).then_inc(s_zero, 1)

            def root(src, e, tmp, dst, own, done):
                own.then(nc.gpsimd.tensor_tensor(tmp[:, :], src, eps[:, e:e + 1], ALU.add))
                nc.gpsimd.tensor_tensor(dst[:, :], tmp[:, :], half_exp[:, :], ALU.pow).then_inc(done, 1)

            def norm_root(c):
                wait(pool, var_rd, c.n + 1)
                root(mv[:, 1:2], 0, vpe, rstd, Own(pool, g_var, 1, c.n), rstd_rd)

            norm_root(Chunk(0, 0, 0))

            def step(cur, prev, nxt):
                if cur:
                    wait(pool, x_ld[cur.p], 16 * cur.h + 16)
                    wait(pool, x2_rd, cur.n - 1)
                    wait(pool, vec_in, 16 * 12)
                    nc.gpsimd.tensor_tensor(xb[:, cur.p, :], x_in[:, cur.p, :], bo[:, :], ALU.add)\
                        .then_inc(xb_rd, 1)
                if prev:
                    wait(pool, off_ps, prev.n + 1)
                    wait(pool, wdec_rd, prev.n + 1)
                    nc.gpsimd.tensor_tensor(S[:, :].rearrange("p (h d) -> p h d", d=HD),
                                            S[:, :].rearrange("p (h d) -> p h d", d=HD),
                                            over_heads(ekeep[:, prev.p, 1, :], HD), ALU.mult).then_inc(s_dec, 1)
                if nxt:
                    norm_root(nxt)
                if prev:
                    wait(pool, x2_rd, prev.n)
                    wait(pool, ssq_rd, prev.n + 1)
                    root(ssq[:, :], 1, vpe2, rstd2, Own(pool, g_ssq, 1, prev.n), rstd2_rd)
                if cur:
                    wait(pool, xs_rd, cur.n + 1)
                    wait(pool, wdec_rd, cur.n + 1)
                    wait(pool, S_rd, cur.n)
                    xv = xs[:, cur.p, :].rearrange("p (h d) -> p h d", d=HD)
                    nc.gpsimd.tensor_tensor(xd[:, cur.p, :].rearrange("p (h d) -> p h d", d=HD), xv,
                                            over_heads(dts[:, cur.p, :], HD), ALU.mult)
                    Own(pool, g_xdec, 1, cur.n).then(nc.gpsimd.tensor_tensor(
                        xdec[:, cur.p, :].rearrange("p (h d) -> p h d", d=HD), xv,
                        over_heads(wdec[:, cur.p, :], HD), ALU.mult))
                    nc.gpsimd.tensor_tensor(xv, xv, over_heads(dpar[:, :], HD), ALU.mult).then_inc(xd_rd, 1)

            run_steps(pool, step)

        @block.scalar
        def _(act):
            def vec(dst, src):
                act.dma_start(dst, src).then_inc(vec_in, 16)

            def spread(dst, src):
                vec(dst, src.rearrange("(a n) -> a n", a=1).to_broadcast([P, src.shape[0]]))

            vec(rows[0:40, :], conv_w.rearrange("j a (t p) -> (j a t) p", p=P))
            vec(rows[40:50, :], b_in[X0:DT0].rearrange("(t p) -> t p", p=P))
            vec(rows[50:60, :], conv_b.rearrange("(t p) -> t p", p=P))
            vec(rows[60:68, :], norm_w.rearrange("(t p) -> t p", p=P))
            spread(bdt[:, :], b_in[DT0:PROJ])
            spread(bdt2[:, :], dt_bias)
            spread(neg_a[:, :], A_log)
            spread(dpar[:, :], D_param)
            spread(zb[:, 0:512], b_in[0:512])
            spread(zb[:, 512:1024], b_in[512:1024])
            spread(bo[:, 0:256], b_out[0:256])
            spread(bo[:, 256:512], b_out[256:512])
            act.wait_ge(vec_in, 16 * 12)
            nc.scalar.activation(neg_a[:, :], neg_a[:, :], ACT.Exp).then_inc(aset, 1)

            def decays(c, q):
                wait(act, cumb_ld[q % 2], 32 * c.n + 16 * (q // 2) + 16)
                wait(act, cumT_rd, c.n + 1)
                for h in range(PH):
                    row = cumb[:, q % 2, h, :]
                    ins = nc.scalar.activation(row, row, ACT.Relu, scale=-1.0,
                                               bias=cum_s[:, c.p, q * PH + h:q * PH + h + 1])
                ins.then_inc(seg_rd, 1)
                wait(act, seg_rd, 4 * c.n + q + 1)
                wait(act, diag_ps, 4 * c.n + q - 3)
                nc.scalar.activation(L[:, q, :, :], cumb[:, q % 2, :, :], ACT.Exp, scale=-1.0).then_inc(l_rd, 1)

            def step(cur, prev, nxt):
                if cur:
                    wait(act, xnT_ps, cur.n + 1)
                    nc.scalar.activation(xnT[:, :, :].rearrange("p k t -> p (k t)"), bank[0][:, :], ACT.Copy)\
                        .then_inc(xnT_rd, 1)
                    wait(act, dtm_rd, cur.n + 1)
                    nc.scalar.activation(edt[:, :], dtm[:, :], ACT.Exp).then_inc(edt_rd, 1)
                if prev:
                    decays(prev, 3)
                if cur:
                    wait(act, bcc_rd, cur.n + 1)
                    nc.scalar.activation(th[:, KI:CT, :], cv[:, KI:CT, :], ACT.Tanh).then_inc(tbc_rd, 1)
                    wait(act, z_ev, cur.n + 1)
                    nc.scalar.activation(tz[:, :], sz[:, cur.p, :], ACT.Tanh).then_inc(tz_rd, 1)
                    wait(act, dif_rd, cur.n + 1)
                    nc.scalar.activation(ecum[:, :, :], cum[:, :, :], ACT.Exp).then_inc(ecum_rd, 1)
                    decays(cur, 0)
                    decays(cur, 1)
                if prev:
                    wait(act, y_rd, prev.n + 1)
                    wait(act, out_ps, prev.n)
                    wait(act, rstd2_rd, prev.n)
                    nc.scalar.activation(yT[:, :, :].rearrange("p k t -> p (k t)"), y[:, :], ACT.Square,
                                         scale=INNER ** -0.5, accum_out=ssq[:, :]).then_inc(ssq_rd, 1)
                if cur:
                    decays(cur, 2)
                if prev:
                    wait(act, yT_ps, prev.n + 1)
                    wait(act, ssq_rd, prev.n + 1)
                    for j in range(2):
                        ins = nc.scalar.activation(yT[:, 4 * j:4 * j + 4, :].rearrange("p k t -> p (k t)"),
                                                   bank[6 + j][:, :], ACT.Copy)
                    ins.then_inc(yT_rd, 1)
                if cur:
                    for j in range(2):
                        wait(act, xc_rd, 2 * cur.n + j + 1)
                        nc.scalar.activation(th[:, 4 * j:4 * j + 4, :], cv[:, 4 * j:4 * j + 4, :], ACT.Tanh)\
                            .then_inc(tx_rd, 1)
                    wait(act, xT_ps, cur.n + 1)
                    wait(act, y_rd, cur.n - 1)
                    for j in range(2):
                        ins = nc.scalar.activation(xs[:, cur.p, 512 * j:512 * j + 512], bank[2 + j][:, :], ACT.Copy)
                    ins.then_inc(xs_rd, 1)

            run_steps(act, step)

        @block.vector
        def _(dve):
            dve.wait_ge(cols_ps, 1)
            nc.vector.tensor_copy(cols[:, :], bank[0][:, 0:68]).then_inc(vset, 1)
            dve.wait_ge(vset, 1)
            nc.vector.tensor_scalar(hw[:, :], cols[:, 0:40], 0.5, None, ALU.mult).then_inc(vset, 1)
            nc.vector.tensor_scalar(hb[:, :], cols[:, 50:60], 0.5, None, ALU.mult).then_inc(vset, 1)
            dve.wait_ge(vec_in, 16 * 12)
            nc.vector.tensor_tensor(bdt[:, :], bdt[:, :], bdt2[:, :], ALU.add).then_inc(vset, 1)
            nc.vector.tensor_scalar(zb[:, :], zb[:, :], 0.5, None, ALU.mult).then_inc(vset, 1)
            dve.wait_ge(aset, 1)
            nc.vector.tensor_scalar(neg_a[:, :], neg_a[:, :], -1.0, None, ALU.mult).then_inc(vset, 1)
            dve.wait_ge(vset, 6)
            dve.wait_ge(s_zero, 1)
            dve.wait_ge(consts, 4)

            def norm(c):
                wait(dve, x_ld[c.p], 16 * c.h + 16)
                stats = nc.vector.bn_stats(stat[:, :], x_in[:, c.p, :])
                stats.then_inc(n_own, 1)
                wait(dve, n_own, c.n + 1)
                nc.vector.memset(carrier[:, :], 0.0)
                nc.vector.bn_aggr(mv[:, :], stat[:, :]).then_inc(var_rd, 1)
                wait(dve, rstd_rd, c.n + 1)
                wait(dve, var_rd, c.n + 1)
                wait(dve, xnT_ps, c.n)
                nc.vector.tensor_scalar(xn[:, :], x_in[:, c.p, :], mv[:, 0:1], rstd[:, 0:1],
                                        ALU.subtract, ALU.mult).then_inc(xn_rd, 1)

            def masked(c, q):
                wait(dve, l_rd, 4 * c.n + q + 1)
                piece = L[:, q, :, :]
                nc.vector.tensor_tensor(piece, piece, cbm[:, c.p:c.p + 1, :].to_broadcast([P, PH, P]),
                                        ALU.mult).then_inc(m_rd, 1)

            def steplen(c, own):
                wait(dve, dt_ps, c.n + 1)
                own.then(nc.vector.tensor_tensor(dtm[:, :], bank[1][:, 0:HEADS], bdt[:, :], ALU.add))
                nc.vector.tensor_scalar(dtm[:, :], dtm[:, :], 0.0, None, ALU.min).then_inc(dtm_rd, 1)
                wait(dve, edt_rd, c.n + 1)
                own.then(nc.vector.tensor_scalar(den[:, :], edt[:, :], 0.2, 2.0, ALU.min, ALU.add))
                own.then(nc.vector.reciprocal(den[:, :], den[:, :]))
                own.then(nc.vector.scalar_tensor_tensor(out=sw[:, :], in0=edt[:, :], scalar=0.2, in1=den[:, :],
                                                        op0=ALU.min, op1=ALU.mult))
                own.then(nc.vector.tensor_tensor(sw2[:, :], sw[:, :], sw[:, :], ALU.mult))
                own.then(nc.vector.tensor_scalar(poly[:, :], sw2[:, :], 2 / 7, 2 / 5, ALU.mult, ALU.add))
                own.then(nc.vector.tensor_tensor(poly[:, :], poly[:, :], sw2[:, :], ALU.mult))
                own.then(nc.vector.scalar_tensor_tensor(out=poly[:, :], in0=poly[:, :], scalar=2 / 3, in1=sw2[:, :],
                                                        op0=ALU.add, op1=ALU.mult))
                own.then(nc.vector.scalar_tensor_tensor(out=poly[:, :], in0=poly[:, :], scalar=2.0, in1=sw[:, :],
                                                        op0=ALU.add, op1=ALU.mult))
                own.then(nc.vector.tensor_scalar(dts[:, c.p, :], poly[:, :], DT_MAX, DT_MIN, ALU.min, ALU.max))
                nc.vector.tensor_tensor(adt[:, :], dts[:, c.p, :], neg_a[:, :], ALU.mult).then_inc(adt_rd, 1)

            def convolve(t0, tiles, own, done):
                for j in range(TAPS):
                    for t in range(t0, t0 + tiles):
                        w = hw[:, j * CT + t:j * CT + t + 1]
                        if j == 0:
                            ins = nc.vector.tensor_scalar(cv[:, t, :], cin[:, t, 0:P], w, hb[:, t:t + 1],
                                                          ALU.mult, ALU.add)
                        else:
                            ins = nc.vector.scalar_tensor_tensor(out=cv[:, t, :], in0=cin[:, t, j:j + P], scalar=w,
                                                                 in1=cv[:, t, :], op0=ALU.mult, op1=ALU.add)
                    if j < TAPS - 1:
                        own.then(ins)
                ins.then_inc(done, 1)

            def take(c, t0, tiles, src, own, evacuated):
                own.then(nc.vector.tensor_scalar(cin[:, t0:t0 + tiles, 0:HALO], cin[:, t0:t0 + tiles, P:P + HALO],
                                                 keep[:, bass.ds(c.n, 1)], None, ALU.mult))
                bias = over_heads(cols[:, 40 + t0:40 + t0 + tiles], P)
                nc.vector.tensor_tensor(cin[:, t0:t0 + tiles, HALO:HALO + P],
                                        src.rearrange("p (t l) -> p t l", l=P), bias, ALU.add).then_inc(evacuated, 1)

            def step(cur, prev, nxt):
                own = Own(dve, v_own, FRONT, cur.n) if cur else None
                own2 = Own(dve, v_own2, BACK, prev.n) if prev else None
                if prev:
                    masked(prev, 1)
                if cur:
                    steplen(cur, own)
                if prev:
                    masked(prev, 2)
                if cur:
                    wait(dve, bc_ps, cur.n + 1)
                    take(cur, KI, 2, bank[2][:, 0:2 * P], own, bc_ev)
                    wait(dve, bc_ev, cur.n + 1)
                    convolve(KI, 2, own, bcc_rd)
                    wait(dve, z_ps, cur.n + 1)
                    for j in range(2):
                        ins = nc.vector.scalar_tensor_tensor(out=sz[:, cur.p, 512 * j:512 * j + 512],
                                                             in0=bank[3 + j][:, :], scalar=0.5,
                                                             in1=zb[:, 512 * j:512 * j + 512],
                                                             op0=ALU.mult, op1=ALU.add)
                    ins.then_inc(z_ev, 1)
                    wait(dve, tbc_rd, cur.n + 1)
                    nc.vector.scalar_tensor_tensor(out=cv[:, KI, :], in0=th[:, KI, :], scalar=1.0, in1=cv[:, KI, :],
                                                   op0=ALU.add, op1=ALU.mult)
                    nc.vector.scalar_tensor_tensor(out=ct[:, cur.p, :], in0=th[:, KI + 1, :], scalar=1.0,
                                                   in1=cv[:, KI + 1, :], op0=ALU.add, op1=ALU.mult).then_inc(bct_rd, 1)
                    wait(dve, cum_ps, cur.n + 1)
                    own.then(nc.vector.tensor_copy(cum[:, 0:2, :],
                                                   bank[5][:, 0:2 * HEADS].rearrange("p (a h) -> p a h", a=2)))
                    wait(dve, cum_st, 16 * cur.n)
                    wait(dve, l_rd, 4 * cur.n - 4)
                    nc.vector.tensor_copy(cum_s[:, cur.p, :], cum[:, 0, :])
                    nc.vector.tensor_copy(cumT[:, :], bank[5][0:HEADS, 2 * HEADS:2 * HEADS + P]).then_inc(cumT_rd, 1)
                    nc.vector.tensor_tensor(cum[:, 2, :], cum[:, 1, :], cum[:, 0, :], ALU.subtract)\
                        .then_inc(dif_rd, 1)
                if prev:
                    masked(prev, 3)
                if cur:
                    wait(dve, cb_ps, cur.n + 1)
                    nc.vector.tensor_tensor(cbm[:, cur.p, :], bank[1][:, 0:P], tri[:, :], ALU.mult)
                    nc.vector.tensor_copy(bs[:, cur.p, :], bank[1][:, P:2 * P]).then_inc(cb_rd, 1)
                    wait(dve, cb_rd, cur.n + 1)
                    wait(dve, tz_rd, cur.n + 1)
                    own.then(nc.vector.scalar_tensor_tensor(out=sz[:, cur.p, :], in0=tz[:, :], scalar=1.0,
                                                            in1=sz[:, cur.p, :], op0=ALU.add, op1=ALU.mult))
                    wait(dve, ecum_rd, cur.n + 1)
                    nc.vector.tensor_scalar(ekeep[:, cur.p, :, :], ecum[:, 0:2, :], keep[:, bass.ds(cur.n, 1)], None,
                                            ALU.mult)
                    nc.vector.tensor_tensor(wdec[:, cur.p, :], ecum[:, 2, :], dts[:, cur.p, :], ALU.mult)\
                        .then_inc(wdec_rd, 1)
                    wait(dve, wdec_rd, cur.n + 1)
                    masked(cur, 0)
                if prev:
                    m = prev.n
                    wait(dve, yT_ps, m)
                    wait(dve, ssq_rd, m)
                    wait(dve, off_ps, m + 1)
                    for j in range(2):
                        ins = nc.vector.tensor_tensor(
                            y[:, 512 * j:512 * j + 512].rearrange("p (h d) -> p h d", d=HD),
                            bank[j][:, :].rearrange("p (h d) -> p h d", d=HD),
                            over_heads(ekeep[:, prev.p, 0, 32 * j:32 * j + 32], HD), ALU.mult)
                    ins.then_inc(off_ev, 1)
                    wait(dve, off_ev, m + 1)
                    wait(dve, diag_ps, 4 * m + 4)
                    for j in range(2):
                        ins = nc.vector.tensor_tensor(y[:, 512 * j:512 * j + 512], y[:, 512 * j:512 * j + 512],
                                                      bank[6 + j][:, :], ALU.add)
                    own2.then(ins)
                    wait(dve, xd_rd, m + 1)
                    own2.then(nc.vector.tensor_tensor(y[:, :], y[:, :], xs[:, prev.p, :], ALU.add))
                    nc.vector.tensor_tensor(y[:, :], y[:, :], sz[:, prev.p, :], ALU.mult).then_inc(y_rd, 1)
                    wait(dve, state_ps, m + 1)
                    wait(dve, s_dec, m + 1)
                    for j in range(2):
                        ins = nc.vector.tensor_tensor(S[:, 512 * j:512 * j + 512], S[:, 512 * j:512 * j + 512],
                                                      bank[2 + j][:, :], ALU.add)
                    ins.then_inc(S_rd, 1)
                if cur:
                    wait(dve, xT_ps, cur.n)
                    for j in range(2):
                        wait(dve, x_ps, 2 * cur.n + j + 1)
                        take(cur, 4 * j, 4, bank[4 + j][:, :], own, xev)
                        wait(dve, xev, 2 * cur.n + j + 1)
                        convolve(4 * j, 4, own, xc_rd)
                if nxt:
                    norm(nxt)
                if cur:
                    for j in range(2):
                        wait(dve, tx_rd, 2 * cur.n + j + 1)
                        ins = nc.vector.scalar_tensor_tensor(out=cv[:, 4 * j:4 * j + 4, :],
                                                             in0=th[:, 4 * j:4 * j + 4, :], scalar=1.0,
                                                             in1=cv[:, 4 * j:4 * j + 4, :], op0=ALU.add, op1=ALU.mult)
                    ins.then_inc(xt_rd, 1)
                if prev:
                    wait(dve, out_ps, prev.n + 1)
                    wait(dve, rstd2_rd, prev.n + 1)
                    wait(dve, x2_st[prev.p], 16 * prev.h)
                    nc.vector.scalar_tensor_tensor(out=x2o[:, prev.p, :], in0=bank[0][:, :], scalar=rstd2[:, 0:1],
                                                   in1=xb[:, prev.p, :], op0=ALU.mult, op1=ALU.add).then_inc(x2_rd, 1)
                if cur:
                    own.close()
                if prev:
                    own2.close()

            n_own = sem("n_own")
            xev = sem("xev")
            FRONT = 10 + 1 + 3 + 1 + 1 + 2 * (1 + 3)
            BACK = 2
            norm(Chunk(0, 0, 0))
            dve.wait_ge(wout_in, 16)
            for k in range(KI):
                ins = nc.vector.tensor_scalar(wout[:, k, :], wout[:, k, :], cols[:, 60 + k:61 + k], None, ALU.mult)
            ins.then_inc(params, 1)
            run_steps(dve, step)

        @block.tensor
        def _(pe):
            pe.wait_ge(consts, 4)
            pe.wait_ge(vec_in, 16 * 12)
            nc.tensor.transpose(bank[0][:, 0:68], rows[:, :], ident[0:68, 0:68]).then_inc(cols_ps, 1)
            pe.wait_ge(vset, 1)

            def step(cur, prev, nxt):
                if cur:
                    n = cur.n
                    wait(pe, xn_rd, n + 1)
                    wait(pe, x2_rd, n - 1)
                    for k in range(KH):
                        ins = nc.tensor.transpose(bank[0][:, k * P:(k + 1) * P], xn[:, k * P:(k + 1) * P], ident[:, :])
                    ins.then_inc(xnT_ps, 1)
                    wait(pe, xnT_rd, n + 1)
                    if isinstance(n, int) and n == 0:
                        pe.wait_ge(win_in, 16 * KH)
                    wait(pe, off_ev, n - 1)
                    for k in range(KH):
                        ins = nc.tensor.matmul(bank[1][:, 0:HEADS], xnT[:, k, :], win[:, k, DT0:PROJ],
                                               start=(k == 0), stop=(k == KH - 1))
                    ins.then_inc(dt_ps, 1)
                    wait(pe, xs_rd, n)
                    for t in range(2):
                        for k in range(KH):
                            ins = nc.tensor.matmul(bank[2][:, t * P:(t + 1) * P],
                                                   win[:, k, B0 + t * P:B0 + (t + 1) * P], xnT[:, k, :],
                                                   start=(k == 0), stop=(k == KH - 1))
                    ins.then_inc(bc_ps, 1)
                    for j in range(2):
                        for k in range(KH):
                            ins = nc.tensor.matmul(bank[3 + j][:, :], xnT[:, k, :], win[:, k, 512 * j:512 * j + 512],
                                                   start=(k == 0), stop=(k == KH - 1))
                    ins.then_inc(z_ps, 1)
                    wait(pe, adt_rd, n + 1)
                    nc.tensor.matmul(bank[5][:, 0:HEADS], tri[:, :], adt[:, :], start=True, stop=True)
                    nc.tensor.matmul(bank[5][:, HEADS:2 * HEADS], ones[:, :], adt[:, :], start=True, stop=True)
                    nc.tensor.matmul(bank[5][0:HEADS, 2 * HEADS:2 * HEADS + P], adt[:, :], tri[:, :],
                                     start=True, stop=True).then_inc(cum_ps, 1)
                def bc_products():
                    wait(pe, bct_rd, n + 1)
                    wait(pe, dtm_rd, n + 1)
                    nc.tensor.matmul(bank[1][:, 0:P], cv[:, KI, :], ct[:, cur.p, :], start=True, stop=True)
                    nc.tensor.transpose(bank[1][:, P:2 * P], cv[:, KI, :], ident[:, :]).then_inc(cb_ps, 1)

                if cur and not prev:
                    bc_products()
                if prev:
                    m = prev.n
                    wait(pe, xd_rd, m + 1)
                    wait(pe, yT_rd, m)
                    for q in range(PIECES):
                        wait(pe, m_rd, 4 * m + q + 1)
                        for h in range(q * PH, (q + 1) * PH):
                            at = HD * (h % 32)
                            ins = nc.tensor.matmul(bank[6 + h // 32][:, at:at + HD], L[:, q, h % PH, :],
                                                   xd[:, prev.p, h * HD:(h + 1) * HD], start=True, stop=True)
                        ins.then_inc(diag_ps, 1)
                        if cur and q == 0:
                            bc_products()
                    wait(pe, S_rd, m + 1)
                    if cur:
                        wait(pe, cb_rd, n + 1)
                    else:
                        wait(pe, x2_rd, m)
                        wait(pe, off_ev, m)
                    for j in range(2):
                        ins = nc.tensor.matmul(bank[j][:, :], ct[:, prev.p, :], S[:, 512 * j:512 * j + 512],
                                               start=True, stop=True)
                    ins.then_inc(off_ps, 1)
                    if cur:
                        wait(pe, bc_ev, n + 1)
                        wait(pe, z_ev, n + 1)
                    else:
                        wait(pe, xs_rd, m + 1)
                    for j in range(2):
                        ins = nc.tensor.matmul(bank[2 + j][:, :], bs[:, prev.p, :],
                                               xdec[:, prev.p, 512 * j:512 * j + 512], start=True, stop=True)
                    ins.then_inc(state_ps, 1)
                if cur:
                    wait(pe, z_ev, n + 1)
                    wait(pe, dif_rd, n + 1)
                    for j in range(2):
                        for t in range(4):
                            c0 = X0 + (4 * j + t) * P
                            for k in range(KH):
                                ins = nc.tensor.matmul(bank[4 + j][:, t * P:(t + 1) * P], win[:, k, c0:c0 + P],
                                                       xnT[:, k, :], start=(k == 0), stop=(k == KH - 1))
                        ins.then_inc(x_ps, 1)
                if prev:
                    wait(pe, y_rd, m + 1)
                    for k in range(KI):
                        ins = nc.tensor.transpose(bank[6 + k // 4][:, (k % 4) * P:(k % 4 + 1) * P],
                                                  y[:, k * P:(k + 1) * P], ident[:, :])
                    ins.then_inc(yT_ps, 1)
                    wait(pe, yT_rd, m + 1)
                    if isinstance(m, int) and m == 0:
                        pe.wait_ge(params, 1)
                    for k in range(KI):
                        ins = nc.tensor.matmul(bank[0][:, :], yT[:, k, :], wout[:, k, :],
                                               start=(k == 0), stop=(k == KI - 1))
                    ins.then_inc(out_ps, 1)
                if cur:
                    wait(pe, xt_rd, n + 1)
                    if prev:
                        wait(pe, S_rd, m + 2)
                    for k in range(KI):
                        ins = nc.tensor.transpose(bank[2 + k // 4][:, (k % 4) * P:(k % 4 + 1) * P],
                                                  cv[:, k, :], ident[:, :])
                    ins.then_inc(xT_ps, 1)

            pe.wait_ge(params, 1)
            run_steps(pe, step)


def moe_stage(nc, x2_dram, xn2_dram, gate_w, gate_bias, w1, w2, w3, shared_gate, shared_up, shared_down, out):
    with ExitStack() as ctx:
        def sb(name, shape, dt=F32):
            return ctx.enter_context(nc.sbuf_tensor(name, shape, dt))

        def sem(name):
            return ctx.enter_context(nc.semaphore(name))

        bank = [ctx.enter_context(nc.psum_tensor(f"mbank{i}", [P, 512], F32)) for i in range(8)]
        SLOT_BANK = 6
        NBUF = 4

        ident = sb("m_ident", [P, P])
        tri_f = sb("tri_f", [P, P])
        tri = sb("m_tri", [P, P], BF16)
        ones = sb("m_ones", [P, P], BF16)
        half_exp = sb("m_half_exp", [P, 1])
        eps = sb("m_eps", [P, 1])
        carrier = sb("m_carrier", [P, 1])
        low = sb("low", [P, GROUPS, GROUPS])
        row_i = sb("row_i", [P, 1], I32)
        slot_i = sb("slot_i", [P, CAP, EXPERTS], I32)
        slot_b = sb("slot_b", [P, CAP, EXPERTS], BF16)
        tile_i = sb("tile_i", [P, CHUNKS], I32)
        tile_f = sb("tile_f", [P, CHUNKS])
        row_f = sb("row_f", [P, 1])
        dump = sb("dump", [P, 1])
        one32 = sb("one32", [P, EXPERTS])
        zeros = sb("zeros", [P, HID])
        gw = sb("gw", [EXPERTS, HID])
        gwT = sb("gwT", [P, KH, EXPERTS])
        gbias = sb("gbias", [P, EXPERTS])
        sg = sb("sg", [P, KH, FS])
        su = sb("su", [P, KH, FS])
        sd = sb("sd", [P, KS, HID])
        x2i = sb("x2i", [P, 2, HID])
        xk = sb("xk", [P, 2, HID])
        stat = sb("m_stat", [P, 6])
        mv = sb("m_mv", [P, 2])
        vpe = sb("m_vpe", [P, 1])
        rstd = sb("m_rstd", [P, 1])
        xn = sb("m_xn", [P, 2, HID])
        xnT = sb("m_xnT", [P, 2, KH, P])
        tg = sb("tg", [P, KS * P])
        hT = sb("hT", [P, KS, P])
        oo = sb("oo", [P, 2, HID])
        tl = sb("tl", [P, EXPERTS])
        score = sb("score", [P, EXPERTS])
        sc = sb("sc", [P, EXPERTS])
        top8 = sb("top8", [P, GROUPS, 8])
        gsum = sb("gsum", [P, GROUPS])
        above = sb("above", [P, GROUPS, GROUPS])
        ties = sb("ties", [P, GROUPS, GROUPS])
        rank = sb("rank", [P, GROUPS])
        masked = sb("masked", [P, EXPERTS])
        best8 = sb("best8", [P, 8])
        gt = sb("gt", [P, EXPERTS])
        eq = sb("eq", [P, EXPERTS])
        eqc = sb("eqc", [P, EXPERTS])
        need = sb("need", [P, 1])
        sel = sb("sel", [P, 2, EXPERTS])
        selb = sb("selb", [P, 2, EXPERTS], BF16)
        wt = sb("wt", [P, EXPERTS])
        wsum = sb("wsum", [P, 1])
        base = sb("base", [P, EXPERTS])
        incl = sb("incl", [P, EXPERTS])
        posb = sb("posb", [P, 1, EXPERTS], BF16)
        onehot = sb("onehot", [P, CAP, EXPERTS], BF16)
        R = sb("R", [P, 2, EXPERTS, IDC], BF16)
        zb6 = sb("zb6", [P, EXPERTS * IDC], BF16)
        table = sb("table", [P, EXPERTS, IDC])
        tok = sb("tok", [P, EXPERTS])
        wslot = sb("wslot", [P, EXPERTS])
        unused = sb("unused", [P, EXPERTS])
        dest = sb("dest", [P, EXPERTS])
        w1s = sb("w1s", [P, NBUF, KH, F])
        w3s = sb("w3s", [P, NBUF, KH, F])
        w2s = sb("w2s", [P, NBUF, KF, HID])
        src_ix = [sb(f"src_ix{p}", [P, 1], U32) for p in range(2)]
        dst_ix = [sb(f"dst_ix{p}", [P, 1], U32) for p in range(2)]
        wcol = sb("wcol", [P, 2])
        xe = [sb(f"xe{p}", [P, HID]) for p in range(2)]
        xeT = sb("xeT", [P, 2, KH, P])
        te = sb("te", [P, F])
        ae = sb("ae", [P, F])
        hTe = sb("hTe", [P, 2, KF, P])
        gcar = sb("gcar", [P, 4])
        ob = [sb(f"ob{p}", [P, HID]) for p in range(2)]

        par_ld = sem("par_ld"); sh_ld = sem("sh_ld"); zero_st = sem("zero_st")
        x_ld = [sem("mx_ld0"), sem("mx_ld1")]
        xn_st = [sem("xn_st0"), sem("xn_st1")]
        o_st = [sem("o_st0"), sem("o_st1")]
        w_ld = [sem(f"w_ld{j}") for j in range(NBUF)]
        xe_ld = [sem("xe_ld0"), sem("xe_ld1")]
        add_st = sem("add_st")
        g_set = sem("g_set"); g_set2 = sem("g_set2"); gw_ps = sem("gw_ps"); v_set = sem("v_set")
        xnT_ps = sem("m_xnT_ps"); gu_ps = sem("gu_ps"); lg_ps = sem("lg_ps"); cnt_ps = sem("cnt_ps")
        dn_ps = sem("dn_ps"); slot_ps = sem("slot_ps")
        xeT_ps = sem("xeT_ps"); gue_ps = sem("gue_ps"); dne_ps = sem("dne_ps")
        v_own = sem("mv_own"); v_cnt = sem("v_cnt"); n_own = sem("mn_own"); var_rd = sem("m_var_rd")
        xn_rd = sem("m_xn_rd"); h_rd = sem("h_rd"); sel_rd = sem("sel_rd"); oh_rd = sem("oh_rd")
        o_rd = sem("o_rd"); v_h = sem("v_h"); fin = sem("fin"); ix_rd = sem("ix_rd"); he_rd = sem("he_rd")
        v_he = sem("v_he"); wcol_rd = sem("wcol_rd")
        xnT_rd = sem("m_xnT_rd"); tg_rd = sem("tg_rd"); xk_rd = sem("xk_rd"); tl_rd = sem("tl_rd")
        xeT_rd = sem("xeT_rd"); te_rd = sem("te_rd"); ob_rd = sem("ob_rd")
        g_var = sem("mg_var"); rstd_rd = sem("m_rstd_rd"); g_car = sem("g_car"); g_car2 = sem("g_car2")

        block = ctx.enter_context(nc.Block())

        x2_rows = x2_dram.rearrange("(c p) h -> c p h", p=P)
        xn2_rows = xn2_dram.rearrange("(c p) h -> c p h", p=P)
        out_rows = out.rearrange("(c p) h -> c p h", p=P)

        def run_experts(eng, step):
            for e in range(NBUF):
                step(e, e, 0)
            with eng.Fori(1, EXPERTS // NBUF - 1) as i:
                for j in range(NBUF):
                    step(NBUF * i + j, j, i)
            for j in range(NBUF):
                step(EXPERTS - NBUF + j, j, EXPERTS // NBUF - 1)

        def turns(e, j, i):
            return 2 * i + j // 2

        @block.sync
        def _(sp):
            sp.dma_start(x2i[:, 0, :], x2_rows[0, :, :]).then_inc(x_ld[0], 16)
            sp.dma_start(x2i[:, 1, :], x2_rows[1, :, :]).then_inc(x_ld[1], 16)
            sp.dma_start(gw[:, :], gate_w).then_inc(par_ld, 16)
            sp.dma_start(gbias[:, :], gate_bias.rearrange("(a n) -> a n", a=1).to_broadcast([P, EXPERTS]))\
                .then_inc(par_ld, 16)
            for dst, src in ((sg, shared_gate), (su, shared_up), (sd, shared_down)):
                sp.dma_start(dst[:, :, :], src.rearrange("(k p) f -> p k f", p=P)).then_inc(sh_ld, 16)

            def load_expert(e, j, i):
                wait(sp, dne_ps, e - NBUF + 1)
                sp.dma_start(w1s[:, j, :, :], w1[bass.ds(e, 1), :, :].rearrange("a (k p) f -> p (a k) f", p=P))\
                    .then_inc(w_ld[j], 16)
                sp.dma_start(w3s[:, j, :, :], w3[bass.ds(e, 1), :, :].rearrange("a (k p) f -> p (a k) f", p=P))\
                    .then_inc(w_ld[j], 16)
                sp.dma_start(w2s[:, j, :, :], w2[bass.ds(e, 1), :, :].rearrange("a (k p) h -> p (a k) h", p=P))\
                    .then_inc(w_ld[j], 16)

            for e in range(NBUF):
                load_expert(e, e, 0)
            sp.wait_ge(g_set2, 1)
            sp.dma_start(out_rows[CHUNKS, :, :], zeros[:, :]).then_inc(zero_st, 16)

            def step(cur, prev, nxt):
                if cur:
                    n = cur.n
                    wait(sp, xn_rd, n + 1)
                    sp.dma_start(xn2_rows[n, :, :], xn[:, cur.p, :]).then_inc(xn_st[cur.p], 16)
                    wait(sp, xk_rd, n + 1)
                    if nxt:
                        sp.dma_start(x2i[:, cur.p, :], x2_rows[n + 2, :, :]).then_inc(x_ld[cur.p], 16)
                if prev:
                    wait(sp, o_rd, prev.n + 1)
                    sp.dma_start(out_rows[prev.n, :, :], oo[:, prev.p, :]).then_inc(o_st[prev.p], 16)

            run_steps(sp, step, loads_ahead=True)
            for p in range(2):
                sp.wait_ge(xn_st[p], 16 * CHUNKS // 2)
                sp.wait_ge(o_st[p], 16 * CHUNKS // 2)
            sp.wait_ge(zero_st, 16)

            with sp.Fori(1, EXPERTS // NBUF) as i:
                for j in range(NBUF):
                    load_expert(NBUF * i + j, j, i)

        @block.gpsimd
        def _(pool):
            nc.gpsimd.memset(ident[:, :], 0.0).then_inc(g_set, 1)
            nc.gpsimd.memset(tri_f[:, :], 1.0).then_inc(g_set, 1)
            nc.gpsimd.memset(low[:, :, :], 1.0).then_inc(g_set, 1)
            nc.gpsimd.memset(half_exp[:, :], -0.5).then_inc(g_set, 1)
            nc.gpsimd.memset(eps[:, :], LN_EPS).then_inc(g_set, 1)
            nc.gpsimd.memset(zeros[:, :], 0.0).then_inc(g_set2, 1)
            pool.wait_ge(g_set, 5)
            nc.gpsimd.affine_select(out=ident[:, :], in_=ident[:, :], compare_op=ALU.not_equal, fill=1.0,
                                    base=0, pattern=[[-1, P]], channel_multiplier=1).then_inc(g_set2, 1)
            nc.gpsimd.affine_select(out=tri_f[:, :], in_=tri_f[:, :], compare_op=ALU.is_ge, fill=0.0,
                                    base=0, pattern=[[1, P]], channel_multiplier=-1).then_inc(g_set2, 1)
            nc.gpsimd.affine_select(out=low[:, :, :], in_=low[:, :, :], compare_op=ALU.is_gt, fill=0.0,
                                    base=0, pattern=[[1, GROUPS], [-1, GROUPS]], channel_multiplier=0)\
                .then_inc(g_set2, 1)
            nc.gpsimd.iota(row_i[:, :], pattern=[[0, 1]], base=0, channel_multiplier=1).then_inc(g_set2, 1)
            nc.gpsimd.iota(tile_i[:, :], pattern=[[1, CHUNKS]], base=0, channel_multiplier=0).then_inc(g_set2, 1)
            nc.gpsimd.iota(slot_i[:, :, :], pattern=[[1, CAP], [0, EXPERTS]], base=0, channel_multiplier=0)\
                .then_inc(g_set2, 1)

            def norm_root(c):
                wait(pool, var_rd, c.n + 1)
                Own(pool, g_var, 1, c.n).then(nc.gpsimd.tensor_tensor(vpe[:, :], mv[:, 1:2], eps[:, :], ALU.add))
                nc.gpsimd.tensor_tensor(rstd[:, :], vpe[:, :], half_exp[:, :], ALU.pow).then_inc(rstd_rd, 1)

            norm_root(Chunk(0, 0, 0))

            def step(cur, prev, nxt):
                if nxt:
                    norm_root(nxt)

            run_steps(pool, step)
            for p in range(2):
                pool.wait_ge(xn_st[p], 16 * CHUNKS // 2)
                pool.wait_ge(o_st[p], 16 * CHUNKS // 2)
            pool.wait_ge(zero_st, 16)

            def gather(e, j, i):
                p = j % 2
                wait(pool, ix_rd, e + 1)
                wait(pool, xeT_ps, e - 1)
                wait(pool, g_car, e - 1)
                nc.gpsimd.tensor_tensor(gcar[:, p:p + 1], half_exp[:, :], half_exp[:, :], ALU.add).then_inc(g_car, 1)
                nc.gpsimd.indirect_dma_start(
                    out=xe[p][:, :], out_offset=None, in_=xn2_dram,
                    in_offset=bass.IndirectOffsetOnAxis(ap=src_ix[p][:, 0:1], axis=0),
                    bounds_check=TOKENS - 1, oob_is_err=True).then_inc(xe_ld[p], 16)

            def scatter(e, j, i):
                p = j % 2
                wait(pool, ob_rd, e + 1)
                wait(pool, add_st, 16 * e)
                wait(pool, wcol_rd, e + 1)
                wait(pool, g_car2, e - 1)
                nc.gpsimd.tensor_tensor(gcar[:, 2 + p:3 + p], half_exp[:, :], half_exp[:, :], ALU.add)\
                    .then_inc(g_car2, 1)
                nc.gpsimd.indirect_dma_start(
                    out=out, out_offset=bass.IndirectOffsetOnAxis(ap=dst_ix[p][:, 0:1], axis=0),
                    in_=ob[p][:, :], in_offset=None, bounds_check=TOKENS + P - 1, oob_is_err=True,
                    compute_op=ALU.add).then_inc(add_st, 16)

            def expert(e, j, i):
                if not (isinstance(e, int) and e + 2 >= EXPERTS):
                    gather(e + 2, (j + 2) % 4, i)
                if not (isinstance(e, int) and e < 1):
                    scatter(e - 1, (j + 3) % 4, i)

            gather(0, 0, 0)
            gather(1, 1, 0)
            run_experts(pool, expert)
            scatter(EXPERTS - 1, 3, EXPERTS // NBUF - 1)
            pool.wait_ge(add_st, 16 * EXPERTS)

        @block.scalar
        def _(act):
            def step(cur, prev, nxt):
                if cur:
                    wait(act, xnT_ps, cur.n + 1)
                    nc.scalar.activation(xnT[:, cur.p, :, :], bank[0][:, :].rearrange("p (k t) -> p k t", t=P),
                                         ACT.Copy).then_inc(xnT_rd, 1)
                    wait(act, x_ld[cur.p], 16 * cur.h + 16)
                    wait(act, o_rd, cur.n - 1)
                    wait(act, xn_rd, cur.n + 1)
                    nc.scalar.activation(xk[:, cur.p, :], x2i[:, cur.p, :], ACT.Copy).then_inc(xk_rd, 1)
                if prev:
                    wait(act, gu_ps, prev.n + 1)
                    nc.scalar.activation(tg[:, :], bank[1][:, :], ACT.Tanh, scale=0.5).then_inc(tg_rd, 1)
                if cur:
                    wait(act, lg_ps, cur.n + 1)
                    wait(act, sel_rd, cur.n)
                    nc.scalar.activation(tl[:, :], bank[4][:, 0:EXPERTS], ACT.Tanh, scale=0.5).then_inc(tl_rd, 1)

            run_steps(act, step)

            def turn_expert(e, j, i):
                p = j % 2
                wait(act, xeT_ps, e + 1)
                nc.scalar.activation(xeT[:, p, :, :], bank[p][:, :].rearrange("p (k t) -> p k t", t=P), ACT.Copy)\
                    .then_inc(xeT_rd, 1)

            def weigh_expert(e, j, i):
                p = j % 2
                wait(act, dne_ps, e + 1)
                wait(act, wcol_rd, e + 1)
                wait(act, add_st, 16 * (e - 1))
                nc.scalar.activation(ob[p][:, :], bank[4 + p][:, :], ACT.Copy, scale=wcol[:, p:p + 1]).then_inc(ob_rd, 1)

            def expert(e, j, i):
                wait(act, gue_ps, e + 1)
                wait(act, he_rd, e)
                nc.scalar.activation(te[:, :], bank[2 + j % 2][:, 0:F], ACT.Tanh, scale=0.5).then_inc(te_rd, 1)
                if not (isinstance(e, int) and e + 1 >= EXPERTS):
                    turn_expert(e + 1, (j + 1) % 4, i)
                if not (isinstance(e, int) and e < 1):
                    weigh_expert(e - 1, (j + 3) % 4, i)

            turn_expert(0, 0, 0)
            run_experts(act, expert)
            weigh_expert(EXPERTS - 1, 3, EXPERTS // NBUF - 1)

        @block.vector
        def _(dve):
            dve.wait_ge(g_set2, 7)
            nc.vector.tensor_copy(tri[:, :], tri_f[:, :]).then_inc(v_set, 1)
            nc.vector.memset(ones[:, :], 1.0).then_inc(v_set, 1)
            nc.vector.memset(zb6[:, :], 0.0).then_inc(v_set, 1)
            nc.vector.tensor_copy(slot_b[:, :, :], slot_i[:, :, :]).then_inc(v_set, 1)
            nc.vector.tensor_copy(tile_f[:, :], tile_i[:, :]).then_inc(v_set, 1)
            nc.vector.tensor_copy(row_f[:, :], row_i[:, :]).then_inc(v_set, 1)
            nc.vector.memset(one32[:, :], 1.0).then_inc(v_set, 1)
            nc.vector.memset(base[:, :], 0.0).then_inc(v_set, 1)
            dve.wait_ge(v_set, 8)
            nc.vector.tensor_scalar(dump[:, :], row_f[:, :], float(TOKENS), None, ALU.add).then_inc(v_set, 1)
            for p in range(2):
                nc.vector.memset(R[:, p, :, 2:3], 1.0).then_inc(v_set, 1)
                nc.vector.tensor_scalar(R[:, p, :, 1:2].rearrange("p e c -> p (e c)"), one32[:, :], row_f[:, 0:1],
                                        None, ALU.mult).then_inc(v_set, 1)
            dve.wait_ge(gw_ps, 1)
            nc.vector.tensor_copy(gwT[:, :, :], bank[0][:, 0:KH * EXPERTS].rearrange("p (k e) -> p k e", e=EXPERTS))\
                .then_inc(v_set, 1)
            dve.wait_ge(v_set, 14)

            COUNT = 3

            def norm(c):
                wait(dve, x_ld[c.p], 16 * c.h + 16)
                nc.vector.bn_stats(stat[:, :], x2i[:, c.p, :]).then_inc(n_own, 1)
                wait(dve, n_own, c.n + 1)
                nc.vector.memset(carrier[:, :], 0.0)
                nc.vector.bn_aggr(mv[:, :], stat[:, :]).then_inc(var_rd, 1)
                wait(dve, rstd_rd, c.n + 1)
                wait(dve, var_rd, c.n + 1)
                wait(dve, xnT_ps, c.n - 1)
                wait(dve, xn_st[c.p], 16 * c.h)
                nc.vector.tensor_scalar(xn[:, c.p, :], x2i[:, c.p, :], mv[:, 0:1], rstd[:, 0:1],
                                        ALU.subtract, ALU.mult).then_inc(xn_rd, 1)

            def choose(c, own):
                wait(dve, tl_rd, c.n + 1)
                own.then(nc.vector.tensor_scalar(score[:, :], tl[:, :], 0.5, 0.5, ALU.mult, ALU.add))
                own.then(nc.vector.tensor_tensor(sc[:, :], score[:, :], gbias[:, :], ALU.add))
                nc.vector.memset(carrier[:, :], 0.0)
                for g in range(GROUPS):
                    ins = nc.vector.max(top8[:, g, :], sc[:, g * GE:(g + 1) * GE])
                own.then(ins)
                own.then(nc.vector.tensor_tensor(gsum[:, :], top8[:, :, 0], top8[:, :, 1], ALU.add))
                other = gsum[:, :].unsqueeze(1).to_broadcast([P, GROUPS, GROUPS])
                mine = gsum[:, :].unsqueeze(2).to_broadcast([P, GROUPS, GROUPS])
                nc.vector.tensor_tensor(above[:, :, :], other, mine, ALU.is_gt)
                own.then(nc.vector.tensor_tensor(ties[:, :, :], other, mine, ALU.is_equal))
                own.then(nc.vector.tensor_tensor(ties[:, :, :], ties[:, :, :], low[:, :, :], ALU.mult))
                own.then(nc.vector.tensor_tensor(above[:, :, :], above[:, :, :], ties[:, :, :], ALU.add))
                own.then(nc.vector.tensor_reduce(rank[:, :], above[:, :, :], AX.X, ALU.add))
                own.then(nc.vector.tensor_scalar(rank[:, :], rank[:, :], 2.0, None, ALU.is_lt))
                own.then(nc.vector.tensor_tensor(masked[:, :].rearrange("p (g e) -> p g e", e=GE),
                                                 sc[:, :].rearrange("p (g e) -> p g e", e=GE),
                                                 over_heads(rank[:, :], GE), ALU.mult))
                nc.vector.memset(carrier[:, :], 0.0)
                own.then(nc.vector.max(best8[:, :], masked[:, :]))
                fourth = best8[:, TOPK - 1:TOPK]
                nc.vector.tensor_scalar(gt[:, :], masked[:, :], fourth, None, ALU.is_gt)
                own.then(nc.vector.tensor_scalar(eq[:, :], masked[:, :], fourth, None, ALU.is_equal))
                nc.vector.tensor_reduce(need[:, :], gt[:, :], AX.X, ALU.add)
                own.then(nc.vector.tensor_tensor_scan(eqc[:, :], one32[:, :], eq[:, :], 0.0, ALU.mult, ALU.add))
                own.then(nc.vector.tensor_scalar(need[:, :], need[:, :], -1.0, float(TOPK), ALU.mult, ALU.add))
                own.then(nc.vector.scalar_tensor_tensor(out=eq[:, :], in0=eqc[:, :], scalar=need[:, 0:1], in1=eq[:, :],
                                                        op0=ALU.is_le, op1=ALU.mult))
                wait(dve, cnt_ps, c.n - 1)
                nc.vector.tensor_tensor(selb[:, c.p, :], gt[:, :], eq[:, :], ALU.add)
                own.then(nc.vector.tensor_tensor(sel[:, c.p, :], gt[:, :], eq[:, :], ALU.add))
                own.then(nc.vector.tensor_tensor(wt[:, :], score[:, :], sel[:, c.p, :], ALU.mult))
                own.then(nc.vector.tensor_reduce(wsum[:, :], wt[:, :], AX.X, ALU.add))
                own.then(nc.vector.tensor_scalar(wsum[:, :], wsum[:, :], 1e-20, None, ALU.add))
                own.then(nc.vector.reciprocal(wsum[:, :], wsum[:, :]))
                own.then(nc.vector.tensor_scalar(wt[:, :], wt[:, :], wsum[:, 0:1], ROUTED_SCALE, ALU.mult, ALU.mult))
                col = [R[:, c.p, :, a:a + 1].rearrange("p e c -> p (e c)") for a in range(IDC)]
                wait(dve, slot_ps, c.n - 1)
                own.then(nc.vector.tensor_copy(col[3], wt[:, :]))
                own.then(nc.vector.tensor_tensor(wt[:, :], wt[:, :], col[3], ALU.subtract))
                own.then(nc.vector.tensor_copy(col[4], wt[:, :]))
                own.then(nc.vector.tensor_tensor(wt[:, :], wt[:, :], col[4], ALU.subtract))
                nc.vector.tensor_copy(col[5], wt[:, :])
                nc.vector.tensor_scalar(col[0], one32[:, :], tile_f[:, bass.ds(c.n, 1)], None, ALU.mult)\
                    .then_inc(sel_rd, 1)
                wait(dve, sel_rd, c.n + 1)

            def count(c, own):
                wait(dve, cnt_ps, c.n + 1)
                own.then(nc.vector.tensor_tensor(incl[:, :], bank[5][:, 0:EXPERTS], base[:, :], ALU.add))
                nc.vector.tensor_tensor(base[:, :], bank[5][:, EXPERTS:2 * EXPERTS], base[:, :], ALU.add)
                own.then(nc.vector.tensor_tensor(incl[:, :], incl[:, :], sel[:, c.p, :], ALU.mult))
                own.then(nc.vector.tensor_scalar(posb[:, 0, :], incl[:, :], -1.0, None, ALU.add))
                wait(dve, slot_ps, c.n)
                nc.vector.tensor_tensor(onehot[:, :, :], slot_b[:, :, :], posb[:, :, :].to_broadcast([P, CAP, EXPERTS]),
                                        ALU.is_equal).then_inc(oh_rd, 1)
                wait(dve, oh_rd, c.n + 1)

            def step(cur, prev, nxt):
                if prev:
                    count(prev, Own(dve, v_cnt, COUNT, prev.n))
                    wait(dve, tg_rd, prev.n + 1)
                    nc.vector.scalar_tensor_tensor(out=tg[:, :], in0=tg[:, :], scalar=1.0, in1=bank[1][:, :],
                                                   op0=ALU.add, op1=ALU.mult).then_inc(v_h, 1)
                    wait(dve, v_h, prev.n + 1)
                    wait(dve, dn_ps, prev.n)
                    nc.vector.scalar_tensor_tensor(out=hT[:, :, :].rearrange("p k t -> p (k t)"), in0=tg[:, :],
                                                   scalar=0.5, in1=bank[2][:, :], op0=ALU.mult, op1=ALU.mult)\
                        .then_inc(h_rd, 1)
                if cur:
                    own = Own(dve, v_own, CHOICE, cur.n)
                    choose(cur, own)
                    own.close()
                if nxt:
                    norm(nxt)
                if prev:
                    wait(dve, dn_ps, prev.n + 1)
                    wait(dve, xk_rd, prev.n + 1)
                    wait(dve, o_st[prev.p], 16 * prev.h)
                    nc.vector.tensor_tensor(oo[:, prev.p, :], bank[3][:, :], xk[:, prev.p, :], ALU.add)\
                        .then_inc(o_rd, 1)

            CHOICE = 25
            dve.wait_ge(par_ld, 32)
            norm(Chunk(0, 0, 0))
            run_steps(dve, step)

            dve.wait_ge(slot_ps, CHUNKS)
            nc.vector.tensor_copy(table[:, :, :],
                                  bank[SLOT_BANK][:, 0:EXPERTS * IDC].rearrange("p (e c) -> p e c", c=IDC))\
                .then_inc(fin, 1)
            dve.wait_ge(fin, 1)
            cell = [table[:, :, a:a + 1].rearrange("p e c -> p (e c)") for a in range(IDC)]
            nc.vector.scalar_tensor_tensor(out=tok[:, :], in0=cell[0], scalar=float(P), in1=cell[1],
                                           op0=ALU.mult, op1=ALU.add)
            nc.vector.tensor_scalar(unused[:, :], cell[2], -1.0, 1.0, ALU.mult, ALU.add)
            nc.vector.tensor_tensor(wslot[:, :], cell[3], cell[4], ALU.add).then_inc(fin, 1)
            dve.wait_ge(fin, 2)
            nc.vector.tensor_tensor(wslot[:, :], wslot[:, :], cell[5], ALU.add)
            nc.vector.scalar_tensor_tensor(out=dest[:, :], in0=unused[:, :], scalar=dump[:, 0:1], in1=tok[:, :],
                                           op0=ALU.mult, op1=ALU.add).then_inc(fin, 1)
            dve.wait_ge(fin, 3)

            def source(e, j, i):
                p = j % 2
                wait(dve, xe_ld[p], 16 * turns(e, j, i))
                nc.vector.tensor_scalar(src_ix[p][:, :], tok[:, bass.ds(e, 1)], 1.0, None, ALU.mult).then_inc(ix_rd, 1)

            def target(e, j, i):
                p = j % 2
                wait(dve, add_st, 16 * (e - 1))
                nc.vector.tensor_scalar(dst_ix[p][:, :], dest[:, bass.ds(e, 1)], 1.0, None, ALU.mult)
                nc.vector.tensor_scalar(wcol[:, p:p + 1], wslot[:, bass.ds(e, 1)], 1.0, None, ALU.mult)\
                    .then_inc(wcol_rd, 1)

            def expert(e, j, i):
                b = bank[2 + j % 2]
                if not (isinstance(e, int) and e + 2 >= EXPERTS):
                    source(e + 2, (j + 2) % 4, i if j < 2 else i + 1)
                wait(dve, te_rd, e + 1)
                nc.vector.scalar_tensor_tensor(out=ae[:, :], in0=te[:, :], scalar=1.0, in1=b[:, 0:F],
                                               op0=ALU.add, op1=ALU.mult).then_inc(v_he, 1)
                wait(dve, v_he, e + 1)
                wait(dve, dne_ps, e - 1)
                nc.vector.scalar_tensor_tensor(out=hTe[:, j % 2, :, :].rearrange("p k t -> p (k t)"), in0=ae[:, :],
                                               scalar=0.5, in1=b[:, F:2 * F], op0=ALU.mult, op1=ALU.mult)\
                    .then_inc(he_rd, 1)
                target(e, j, i)

            source(0, 0, 0)
            source(1, 1, 0)
            run_experts(dve, expert)

        @block.tensor
        def _(pe):
            pe.wait_ge(g_set2, 2)
            pe.wait_ge(par_ld, 32)
            for k in range(KH):
                ins = nc.tensor.transpose(bank[0][:, k * EXPERTS:(k + 1) * EXPERTS], gw[:, k * P:(k + 1) * P],
                                          ident[0:EXPERTS, 0:EXPERTS])
            ins.then_inc(gw_ps, 1)
            pe.wait_ge(v_set, 14)
            nc.tensor.matmul(bank[SLOT_BANK][:, 0:EXPERTS * IDC], ones[:, :], zb6[:, :], start=True, stop=True,
                             skip_group_check=True)

            def step(cur, prev, nxt):
                if cur:
                    n = cur.n
                    wait(pe, xn_rd, n + 1)
                    wait(pe, xnT_rd, n)
                    for k in range(KH):
                        ins = nc.tensor.transpose(bank[0][:, k * P:(k + 1) * P], xn[:, cur.p, k * P:(k + 1) * P],
                                                  ident[:, :])
                    ins.then_inc(xnT_ps, 1)
                if prev:
                    m = prev.n
                    if isinstance(m, int) and m == 0:
                        pe.wait_ge(sh_ld, 48)
                    wait(pe, h_rd, m)
                    for b, w in ((1, sg), (2, su)):
                        for f in range(KS):
                            for k in range(KH):
                                ins = nc.tensor.matmul(bank[b][:, f * P:(f + 1) * P], w[:, k, f * P:(f + 1) * P],
                                                       xnT[:, prev.p, k, :], start=(k == 0), stop=(k == KH - 1))
                    ins.then_inc(gu_ps, 1)
                if cur:
                    wait(pe, xnT_rd, n + 1)
                    wait(pe, tl_rd, n)
                    for k in range(KH):
                        ins = nc.tensor.matmul(bank[4][:, 0:EXPERTS], xnT[:, cur.p, k, :], gwT[:, k, :],
                                               start=(k == 0), stop=(k == KH - 1))
                    ins.then_inc(lg_ps, 1)
                if prev:
                    wait(pe, sel_rd, m + 1)
                    wait(pe, oh_rd, m)
                    nc.tensor.matmul(bank[5][:, 0:EXPERTS], tri[:, :], selb[:, prev.p, :], start=True, stop=True)
                    nc.tensor.matmul(bank[5][:, EXPERTS:2 * EXPERTS], ones[:, :], selb[:, prev.p, :],
                                     start=True, stop=True).then_inc(cnt_ps, 1)
                    wait(pe, h_rd, m + 1)
                    wait(pe, o_rd, m)
                    for f in range(KS):
                        ins = nc.tensor.matmul(bank[3][:, :], hT[:, f, :], sd[:, f, :],
                                               start=(f == 0), stop=(f == KS - 1))
                    ins.then_inc(dn_ps, 1)
                    wait(pe, oh_rd, m + 1)
                    for e in range(EXPERTS):
                        ins = nc.tensor.matmul(bank[SLOT_BANK][:, e * IDC:(e + 1) * IDC], onehot[:, :, e],
                                               R[:, prev.p, e, :], start=False, stop=True, skip_group_check=True)
                    ins.then_inc(slot_ps, 1)

            run_steps(pe, step)

            def turn(e, j, i):
                p = j % 2
                wait(pe, xe_ld[p], 16 * turns(e, j, i) + 16)
                wait(pe, xeT_rd, e - 1)
                for k in range(KH):
                    ins = nc.tensor.transpose(bank[p][:, k * P:(k + 1) * P], xe[p][:, k * P:(k + 1) * P], ident[:, :])
                ins.then_inc(xeT_ps, 1)

            def down(e, j, i):
                p = j % 2
                wait(pe, he_rd, e + 1)
                wait(pe, ob_rd, e - 1)
                for f in range(KF):
                    ins = nc.tensor.matmul(bank[4 + p][:, :], hTe[:, p, f, :], w2s[:, j, f, :],
                                           start=(f == 0), stop=(f == KF - 1))
                ins.then_inc(dne_ps, 1)

            def expert(e, j, i):
                p = j % 2
                wait(pe, w_ld[j], 48 * i + 48)
                wait(pe, xeT_rd, e + 1)
                wait(pe, he_rd, e - 1)
                for b, w in ((0, w1s), (F, w3s)):
                    for f in range(KF):
                        for k in range(KH):
                            ins = nc.tensor.matmul(bank[2 + p][:, b + f * P:b + (f + 1) * P],
                                                   w[:, j, k, f * P:(f + 1) * P], xeT[:, p, k, :],
                                                   start=(k == 0), stop=(k == KH - 1))
                ins.then_inc(gue_ps, 1)
                if not (isinstance(e, int) and e + 1 >= EXPERTS):
                    turn(e + 1, (j + 1) % 4, i if j < 3 else i + 1)
                if not (isinstance(e, int) and e < 1):
                    down(e - 1, (j + 3) % 4, i)

            pe.wait_ge(o_rd, CHUNKS)
            pe.wait_ge(fin, 1)
            turn(0, 0, 0)
            run_experts(pe, expert)
            down(EXPERTS - 1, 3, EXPERTS // NBUF - 1)


def build(nc, x, W_in, b_in, conv_w, conv_b, A_log, dt_bias, D_param, norm_w, W_out, b_out,
          gate_w, gate_bias, w1, w2, w3, shared_gate, shared_up, shared_down, out):
    cum_dram = nc.dram_tensor("cum_rows", (2, HEADS, P), F32, kind="Internal").ap()
    x2_dram = nc.dram_tensor("x2_rows", (TOKENS, HID), F32, kind="Internal").ap()
    xn2_dram = nc.dram_tensor("xn2_rows", (TOKENS, HID), F32, kind="Internal").ap()
    mamba_stage(nc, x, W_in, b_in, conv_w, conv_b, A_log, dt_bias, D_param, norm_w, W_out, b_out,
                cum_dram, x2_dram)
    moe_stage(nc, x2_dram, xn2_dram, gate_w, gate_bias, w1, w2, w3, shared_gate, shared_up, shared_down, out)


_INS = ["L0_attn_x", "L0_attn_W_in", "L0_attn_b_in", "L0_attn_conv_w", "L0_attn_conv_b", "L0_attn_A_log",
        "L0_attn_dt_bias", "L0_attn_D_param", "L0_attn_norm_w", "L0_attn_W_out", "L0_attn_b_out",
        "L0_ffn_gate_w", "L0_ffn_gate_bias", "L0_ffn_w1", "L0_ffn_w2", "L0_ffn_w3",
        "L0_ffn_shared_gate", "L0_ffn_shared_up", "L0_ffn_shared_down"]


def kernel(**inputs):
    import numpy as np
    import concourse.bacc as bacc
    from concourse.bass_utils import run_bass_kernel_spmd

    nc = bacc.Bacc("TRN2", target_bir_lowering=False, num_devices=1)
    arrays, args = {}, []
    for name in _INS:
        a = np.ascontiguousarray(inputs[name])
        arrays[f"in_{name}"] = a
        args.append(nc.dram_tensor(f"in_{name}", a.shape, mybir.dt.from_np(a.dtype), kind="ExternalInput").ap())
    out = nc.dram_tensor("out_0", (TOKENS + P, HID), F32, kind="ExternalOutput").ap()
    build(nc, *args, out)
    r = run_bass_kernel_spmd(nc, [arrays], core_ids=[0])
    got = r.results[0]["out_0"]
    return got[:TOKENS].reshape(4, 512, 512)
```

```python
from contextlib import ExitStack

import concourse.bass as bass
from concourse import mybir

ALU = mybir.AluOpType
ACT = mybir.ActivationFunctionType
AX = mybir.AxisListType
F32 = mybir.dt.float32
BF16 = mybir.dt.bfloat16
I32 = mybir.dt.int32
U32 = mybir.dt.uint32

P = 128
HID = 512
KH = HID // P
INNER = 1024
HEADS = 64
HD = INNER // HEADS
KI = INNER // P
CT = (INNER + 2 * P) // P
TAPS = 4
HALO = TAPS - 1
Z0, X0, B0, DT0 = 0, INNER, 2 * INNER, 2 * INNER + 2 * P
PROJ = DT0 + HEADS
TOKENS = 2048
CHUNKS = TOKENS // P
PER_SEQ = 4
LN_EPS, RMS_EPS = 1e-5, 1e-6
DT_MIN, DT_MAX = 1e-3, 1e-1
PIECES = 4
PH = HEADS // PIECES
TH = P // HD
PITCH = P + HD

EXPERTS = 32
GROUPS = 4
GE = EXPERTS // GROUPS
TOPK = 4
CAP = 128
F = 256
KF = F // P
FS = 512
KS = FS // P
ROUTED_SCALE = 2.0
IDC = 6


def wait(eng, sem, value):
    if isinstance(value, int) and value <= 0:
        return
    eng.wait_ge(sem, value)


class Own:

    def __init__(self, eng, sem, rate, n):
        self.eng, self.sem, self.rate, self.n, self.k = eng, sem, rate, n, 0

    def then(self, ins):
        self.k += 1
        ins.then_inc(self.sem, 1)
        self.eng.wait_ge(self.sem, self.rate * self.n + self.k)

    def close(self):
        assert self.k == self.rate, (self.k, self.rate)


class Chunk:

    def __init__(self, n, p, h):
        self.n, self.p, self.h = n, p, h


def run_steps(eng, step, loads_ahead=False):
    last = CHUNKS - 1

    def at(n):
        return Chunk(n, n % 2, n // 2) if 0 <= n <= last else None

    def peeled(n):
        step(at(n), at(n - 1), at(n + 2) if loads_ahead else at(n + 1))

    for n in range(3):
        peeled(n)
    with eng.Fori(1, 6 if loads_ahead else 7) as i:
        step(Chunk(2 * i + 1, 1, i), Chunk(2 * i, 0, i), Chunk(2 * i + 2, 0, i + 1))
        step(Chunk(2 * i + 2, 0, i + 1), Chunk(2 * i + 1, 1, i), Chunk(2 * i + 3, 1, i + 1))
    for n in range(13 if loads_ahead else 15, CHUNKS + 1):
        peeled(n)


def over_heads(ap, width):
    return ap.unsqueeze(2).to_broadcast([ap.shape[0], ap.shape[1], width])


ROWS = 76
Z_ROW, D0 = 68, ROWS
VECS = 11


def mamba_stage(nc, x, W_in, b_in, conv_w, conv_b, A_log, dt_bias, D_param, norm_w, W_out, b_out,
                cum_dram, ecum_dram, x2_dram):
    with ExitStack() as ctx:
        def sb(name, shape, dt=F32):
            return ctx.enter_context(nc.sbuf_tensor(name, shape, dt))

        def sem(name):
            return ctx.enter_context(nc.semaphore(name))

        bank = [ctx.enter_context(nc.psum_tensor(f"bank{i}", [P, 512], F32)) for i in range(8)]

        win = sb("win", [P, KH, PROJ])
        wout = sb("wout", [P, KI, HID])
        ident = sb("ident", [P, P])
        tri = sb("tri", [P, P])
        ones = sb("ones", [P, P])
        keep = sb("keep", [P, CHUNKS + 1])
        half_exp = sb("half_exp", [P, 1])
        dhead = sb("dhead", [KI, TH])
        drow = sb("drow", [KI, P])
        rows = sb("rows", [ROWS, P])
        cols = sb("cols", [P, ROWS + KI])
        hw = sb("hw", [P, TAPS * CT])
        hb = sb("hb", [P, CT])
        hzb = sb("hzb", [P, KI])
        bo = sb("bo", [P, HID])
        bdt = sb("bdt", [P, HEADS])
        neg_a = sb("neg_a", [P, HEADS])
        x_in = sb("x_in", [P, 2, HID])
        xb = sb("xb", [P, 2, HID])
        stat = sb("stat", [P, 6])
        mv = sb("mv", [P, 2])
        carrier = sb("carrier", [P, 1])
        eps = sb("eps", [P, 2])
        vpe = sb("vpe", [P, 1])
        rstd = sb("rstd", [P, 1])
        xn = sb("xn", [P, HID])
        xnT = sb("xnT", [P, KH, P])
        dtm = sb("dtm", [P, HEADS])
        edt = sb("edt", [P, HEADS])
        den = sb("den", [P, HEADS])
        sw = sb("sw", [P, HEADS])
        sw2 = sb("sw2", [P, HEADS])
        poly = sb("poly", [P, HEADS])
        dts = sb("dts", [P, 2, HEADS])
        adt = sb("adt", [P, HEADS])
        cum = sb("cum", [P, 3, HEADS])
        ecum = sb("ecum", [P, 2, HEADS])
        ekeep = sb("ekeep", [P, 2, HEADS])
        cum_s = sb("cum_s", [P, 2, HEADS])
        wdec = sb("wdec", [P, 2, HEADS])
        cumT = sb("cumT", [HEADS, P])
        ecumT = sb("ecumT", [HEADS, P])
        ecx = sb("ecx", [P, KI, P])
        cin = sb("cin", [P, CT, HALO + P])
        cv = sb("cv", [P, CT, P])
        th = sb("th", [P, CT, P])
        ct = sb("ct", [P, 2, P])
        sz = sb("sz", [P, 2, INNER])
        tz = sb("tz", [P, INNER])
        cbm = sb("cbm", [P, 2, P])
        bs = sb("bs", [P, 2, P])
        xs = sb("xs", [P, INNER])
        xd = sb("xd", [P, HEADS, PITCH])
        xdec = sb("xdec", [P, INNER])
        xD = sb("xD", [P, KI, P])
        L = sb("L", [P, PIECES, PH, P])
        S = sb("S", [P, INNER])
        y = sb("y", [P, KI, P])
        sq = sb("sq", [P, KI, P])
        sqs = sb("sqs", [P, P])
        vpe2 = sb("vpe2", [P, 1])
        rstd2 = sb("rstd2", [P, 1])
        x2o = sb("x2o", [P, 2, HID])

        win_in = sem("win_in"); wout_in = sem("wout_in"); vec_in = sem("vec_in")
        x_ld = [sem("x_ld0"), sem("x_ld1")]
        cum_st = sem("cum_st"); ec_st = sem("ec_st"); ecx_ld = sem("ecx_ld")
        cum_ld = [sem(f"cum_ld{q}") for q in range(PIECES)]
        x2_st = [sem("x2_st0"), sem("x2_st1")]
        pool_set = sem("pool_set"); consts = sem("consts"); cols_ps = sem("cols_ps")
        vset = sem("vset"); aset = sem("aset"); params = sem("params"); s_zero = sem("s_zero")
        xnT_ps = sem("xnT_ps"); dt_ps = sem("dt_ps"); bc_ps = sem("bc_ps"); z_ps = sem("z_ps")
        cum_ps = sem("cum_ps"); diag_ps = sem("diag_ps"); off_ps = sem("off_ps")
        state_ps = sem("state_ps"); cb_ps = sem("cb_ps"); x_ps = sem("x_ps"); sq_ps = sem("sq_ps")
        out_ps = sem("out_ps"); xT_ps = sem("xT_ps")
        v_own = sem("v_own"); v_own2 = sem("v_own2")
        var_rd = sem("var_rd"); xn_rd = sem("xn_rd"); dtm_rd = sem("dtm_rd"); adt_rd = sem("adt_rd")
        bc_ev = sem("bc_ev"); bcc_rd = sem("bcc_rd"); z_ev = sem("z_ev"); cumT_rd = sem("cumT_rd")
        dif_rd = sem("dif_rd"); bct_rd = sem("bct_rd"); wdec_rd = sem("wdec_rd"); m_rd = sem("m_rd")
        off_ev = sem("off_ev"); sqs_rd = sem("sqs_rd"); vpe2_rd = sem("vpe2_rd"); xd_zero = sem("xd_zero"); drow_rd = sem("drow_rd"); y_rd = sem("y_rd"); S_rd = sem("S_rd"); cb_rd = sem("cb_rd")
        xc_rd = sem("xc_rd"); xt_rd = sem("xt_rd"); x2_rd = sem("x2_rd")
        xnT_rd = sem("xnT_rd"); edt_rd = sem("edt_rd"); tbc_rd = sem("tbc_rd"); tz_rd = sem("tz_rd")
        ecum_rd = sem("ecum_rd"); l_rd = sem("l_rd"); sq_rd = sem("sq_rd"); ecumT_rd = sem("ecumT_rd")
        tx_rd = sem("tx_rd"); seg_rd = sem("seg_rd"); xs_rd = sem("xs_rd")
        g_var = sem("g_var"); g_xdec = sem("g_xdec"); xD_rd = sem("xD_rd"); rstd_rd = sem("rstd_rd"); rstd2_rd = sem("rstd2_rd")
        xb_rd = sem("xb_rd"); s_dec = sem("s_dec"); xd_rd = sem("xd_rd")

        block = ctx.enter_context(nc.Block())

        x_rows = x.rearrange("b (c p) h -> (b c) p h", p=P)
        x2_rows = x2_dram.rearrange("(c p) h -> c p h", p=P)

        @block.sync
        def _(sp):
            def load_x(c):
                sp.dma_start(x_in[:, c.p, :], x_rows[c.n, :, :]).then_inc(x_ld[c.p], 16)

            load_x(Chunk(0, 0, 0))
            load_x(Chunk(1, 1, 0))
            for k in range(KH):
                sp.dma_start(win[:, k, :], W_in[k * P:(k + 1) * P, :]).then_inc(win_in, 16)
            sp.dma_start(wout[:, :, :], W_out.rearrange("(k p) h -> p k h", p=P)).then_inc(wout_in, 16)

            def step(cur, prev, nxt):
                if cur:
                    n = cur.n
                    wait(sp, cumT_rd, n + 1)
                    sp.dma_start(cum_dram[cur.p], cumT[:, :]).then_inc(cum_st, 16)
                    wait(sp, cum_st, 16 * n + 16)
                    back = cum_dram[cur.p].rearrange("(q h) l -> q (h l)", q=PIECES)

                    def piece(q):
                        wait(sp, diag_ps, 4 * n + q - 3)
                        sp.dma_start(L[:, q].rearrange("p h l -> p (h l)"),
                                     back[q:q + 1, :].to_broadcast([P, PH * P])).then_inc(cum_ld[q], 16)

                    piece(0)
                    piece(1)
                    wait(sp, ecumT_rd, n + 1)
                    sp.dma_start(ecum_dram[cur.p], ecumT[:, :]).then_inc(ec_st, 16)
                    piece(2)
                    piece(3)
                    wait(sp, ec_st, 16 * n + 16)
                    wait(sp, y_rd, n)
                    per_tile = ecum_dram[cur.p].rearrange("(t j) l -> j t l", j=TH)
                    for j in range(TH):
                        sp.dma_start(ecx[j * HD:(j + 1) * HD, :, :],
                                     per_tile[j:j + 1, :, :].to_broadcast([HD, KI, P])).then_inc(ecx_ld, 16)
                    if nxt:
                        wait(sp, xb_rd, n + 1)
                        wait(sp, xn_rd, n + 1)
                        sp.dma_start(x_in[:, cur.p, :], x_rows[n + 2, :, :]).then_inc(x_ld[cur.p], 16)
                if prev:
                    wait(sp, x2_rd, prev.n + 1)
                    sp.dma_start(x2_rows[prev.n, :, :], x2o[:, prev.p, :]).then_inc(x2_st[prev.p], 16)

            run_steps(sp, step, loads_ahead=True)
            for p in range(2):
                wait(sp, x2_st[p], 16 * (CHUNKS // 2))

        @block.gpsimd
        def _(pool):
            nc.gpsimd.memset(ident[:, :], 0.0).then_inc(pool_set, 1)
            nc.gpsimd.memset(tri[:, :], 1.0).then_inc(pool_set, 1)
            nc.gpsimd.memset(ones[:, :], 1.0).then_inc(consts, 1)
            nc.gpsimd.memset(half_exp[:, :], -0.5).then_inc(pool_set, 1)
            nc.gpsimd.memset(eps[:, 0:1], LN_EPS).then_inc(pool_set, 1)
            nc.gpsimd.memset(eps[:, 1:2], RMS_EPS).then_inc(pool_set, 1)
            nc.gpsimd.memset(keep[:, :], 1.0).then_inc(pool_set, 1)
            pool.wait_ge(pool_set, 6)
            nc.gpsimd.affine_select(out=ident[:, :], in_=ident[:, :], compare_op=ALU.not_equal, fill=1.0,
                                    base=0, pattern=[[-1, P]], channel_multiplier=1).then_inc(consts, 1)
            nc.gpsimd.affine_select(out=tri[:, :], in_=tri[:, :], compare_op=ALU.is_ge, fill=0.0,
                                    base=0, pattern=[[1, P]], channel_multiplier=-1).then_inc(consts, 1)
            nc.gpsimd.memset(keep[:, 0:CHUNKS].rearrange("p (s c) -> p s c", c=PER_SEQ)[:, :, 0:1], 0.0)\
                .then_inc(consts, 1)
            nc.gpsimd.memset(S[:, :], 0.0).then_inc(S_rd, 1)
            nc.gpsimd.memset(cin[:, :, :], 0.0).then_inc(s_zero, 1)

            def norm_root(c):
                wait(pool, var_rd, c.n + 1)
                Own(pool, g_var, 1, c.n).then(nc.gpsimd.tensor_tensor(vpe[:, :], mv[:, 1:2], eps[:, 0:1], ALU.add))
                nc.gpsimd.tensor_tensor(rstd[:, :], vpe[:, :], half_exp[:, :], ALU.pow).then_inc(rstd_rd, 1)

            norm_root(Chunk(0, 0, 0))

            def step(cur, prev, nxt):
                if cur:
                    wait(pool, x_ld[cur.p], 16 * cur.h + 16)
                    wait(pool, x2_rd, cur.n - 1)
                    wait(pool, vec_in, 16 * VECS)
                    nc.gpsimd.tensor_tensor(xb[:, cur.p, :], x_in[:, cur.p, :], bo[:, :], ALU.add)\
                        .then_inc(xb_rd, 1)
                if prev:
                    wait(pool, off_ps, prev.n + 1)
                    wait(pool, wdec_rd, prev.n + 1)
                    nc.gpsimd.tensor_tensor(S[:, :].rearrange("p (h d) -> p h d", d=HD),
                                            S[:, :].rearrange("p (h d) -> p h d", d=HD),
                                            over_heads(ekeep[:, prev.p, :], HD), ALU.mult).then_inc(s_dec, 1)
                if nxt:
                    norm_root(nxt)
                if prev:
                    wait(pool, x2_rd, prev.n)
                    wait(pool, vpe2_rd, prev.n + 1)
                    nc.gpsimd.tensor_tensor(rstd2[:, :], vpe2[:, :], half_exp[:, :], ALU.pow).then_inc(rstd2_rd, 1)
                if cur:
                    wait(pool, xt_rd, cur.n + 1)
                    wait(pool, y_rd, cur.n)
                    nc.gpsimd.tensor_tensor(xD[:, :, :], cv[:, 0:KI, :], over_heads(cols[:, D0:D0 + KI], P), ALU.mult)\
                        .then_inc(xD_rd, 1)
                    wait(pool, xs_rd, cur.n + 1)
                    wait(pool, wdec_rd, cur.n + 1)
                    wait(pool, S_rd, cur.n)
                    xv = xs[:, :].rearrange("p (h d) -> p h d", d=HD)
                    nc.gpsimd.tensor_tensor(xd[:, :, 0:HD], xv, over_heads(dts[:, cur.p, :], HD), ALU.mult)
                    nc.gpsimd.tensor_tensor(xdec[:, :].rearrange("p (h d) -> p h d", d=HD), xv,
                                            over_heads(wdec[:, cur.p, :], HD), ALU.mult).then_inc(xd_rd, 1)

            pool.wait_ge(vset, 1)
            pool.wait_ge(xd_zero, 1)
            run_steps(pool, step)

        @block.scalar
        def _(act):
            def vec(dst, src):
                act.dma_start(dst, src).then_inc(vec_in, 16)

            def spread(dst, src):
                vec(dst, src.rearrange("(a n) -> a n", a=1).to_broadcast([P, src.shape[0]]))

            vec(rows[0:40, :], conv_w.rearrange("j a (t p) -> (j a t) p", p=P))
            vec(rows[40:50, :], b_in[X0:DT0].rearrange("(t p) -> t p", p=P))
            vec(rows[50:60, :], conv_b.rearrange("(t p) -> t p", p=P))
            vec(rows[60:68, :], norm_w.rearrange("(t p) -> t p", p=P))
            vec(rows[Z_ROW:Z_ROW + KI, :], b_in[Z0:X0].rearrange("(t p) -> t p", p=P))
            vec(dhead[:, :], D_param.rearrange("(t j) -> t j", j=TH))
            spread(bdt[:, :], b_in[DT0:PROJ])
            spread(poly[:, :], dt_bias)
            spread(neg_a[:, :], A_log)
            spread(bo[:, 0:256], b_out[0:256])
            spread(bo[:, 256:512], b_out[256:512])
            act.wait_ge(vec_in, 16 * VECS)
            nc.scalar.activation(neg_a[:, :], neg_a[:, :], ACT.Exp).then_inc(aset, 1)

            def decays(c, q):
                wait(act, cum_ld[q], 16 * c.n + 16)
                wait(act, cumT_rd, c.n + 1)
                for h in range(PH):
                    row = L[:, q, h, :]
                    ins = nc.scalar.activation(row, row, ACT.Relu, scale=-1.0,
                                               bias=cum_s[:, c.p, q * PH + h:q * PH + h + 1])
                ins.then_inc(seg_rd, 1)
                wait(act, seg_rd, 4 * c.n + q + 1)
                nc.scalar.activation(L[:, q, :, :], L[:, q, :, :], ACT.Exp, scale=-1.0).then_inc(l_rd, 1)

            def step(cur, prev, nxt):
                if cur:
                    wait(act, xnT_ps, cur.n + 1)
                    nc.scalar.activation(xnT[:, :, :].rearrange("p k t -> p (k t)"), bank[0][:, :], ACT.Copy)\
                        .then_inc(xnT_rd, 1)
                    wait(act, dtm_rd, cur.n + 1)
                    nc.scalar.activation(edt[:, :], dtm[:, :], ACT.Exp).then_inc(edt_rd, 1)
                if prev:
                    decays(prev, 3)
                if cur:
                    wait(act, bcc_rd, cur.n + 1)
                    nc.scalar.activation(th[:, KI:CT, :], cv[:, KI:CT, :], ACT.Tanh).then_inc(tbc_rd, 1)
                    wait(act, dif_rd, cur.n + 1)
                    nc.scalar.activation(ecum[:, :, :], cum[:, 1:3, :], ACT.Exp).then_inc(ecum_rd, 1)
                    wait(act, ec_st, 16 * cur.n)
                    nc.scalar.activation(ecumT[:, :], cumT[:, :], ACT.Exp).then_inc(ecumT_rd, 1)
                    wait(act, z_ev, cur.n + 1)
                    nc.scalar.activation(tz[:, :], sz[:, cur.p, :], ACT.Tanh).then_inc(tz_rd, 1)
                    decays(cur, 0)
                    decays(cur, 1)
                if prev:
                    wait(act, y_rd, prev.n + 1)
                    wait(act, sqs_rd, prev.n)
                    nc.scalar.activation(sq[:, :, :], y[:, :, :], ACT.Square, scale=INNER ** -0.5).then_inc(sq_rd, 1)
                if cur:
                    decays(cur, 2)
                if cur:
                    for j in range(2):
                        wait(act, xc_rd, 2 * cur.n + j + 1)
                        nc.scalar.activation(th[:, 4 * j:4 * j + 4, :], cv[:, 4 * j:4 * j + 4, :], ACT.Tanh)\
                            .then_inc(tx_rd, 1)
                    wait(act, xT_ps, cur.n + 1)
                    wait(act, xd_rd, cur.n)
                    for j in range(2):
                        ins = nc.scalar.activation(xs[:, 512 * j:512 * j + 512], bank[2 + j][:, :], ACT.Copy)
                    ins.then_inc(xs_rd, 1)

            run_steps(act, step)

        @block.vector
        def _(dve):
            nc.vector.memset(xd[:, :, :], 0.0).then_inc(xd_zero, 1)
            dve.wait_ge(vec_in, 16 * VECS)
            nc.vector.tensor_copy(drow[:, :].rearrange("t (j d) -> t j d", d=HD), over_heads(dhead[:, :], HD))\
                .then_inc(drow_rd, 1)
            dve.wait_ge(cols_ps, 1)
            nc.vector.tensor_copy(cols[:, :], bank[0][:, 0:ROWS + KI]).then_inc(vset, 1)
            dve.wait_ge(vset, 1)
            nc.vector.tensor_scalar(hw[:, :], cols[:, 0:40], 0.5, None, ALU.mult).then_inc(vset, 1)
            nc.vector.tensor_scalar(hb[:, :], cols[:, 50:60], 0.5, None, ALU.mult).then_inc(vset, 1)
            dve.wait_ge(vec_in, 16 * VECS)
            nc.vector.tensor_tensor(bdt[:, :], bdt[:, :], poly[:, :], ALU.add).then_inc(vset, 1)
            nc.vector.tensor_scalar(hzb[:, :], cols[:, Z_ROW:Z_ROW + KI], 0.5, None, ALU.mult).then_inc(vset, 1)
            dve.wait_ge(aset, 1)
            nc.vector.tensor_scalar(neg_a[:, :], neg_a[:, :], -1.0, None, ALU.mult).then_inc(vset, 1)
            dve.wait_ge(vset, 6)
            dve.wait_ge(s_zero, 1)
            dve.wait_ge(consts, 4)

            def norm(c):
                wait(dve, x_ld[c.p], 16 * c.h + 16)
                stats = nc.vector.bn_stats(stat[:, :], x_in[:, c.p, :])
                stats.then_inc(n_own, 1)
                wait(dve, n_own, c.n + 1)
                nc.vector.memset(carrier[:, :], 0.0)
                nc.vector.bn_aggr(mv[:, :], stat[:, :]).then_inc(var_rd, 1)
                wait(dve, rstd_rd, c.n + 1)
                wait(dve, var_rd, c.n + 1)
                wait(dve, xnT_ps, c.n)
                nc.vector.tensor_scalar(xn[:, :], x_in[:, c.p, :], mv[:, 0:1], rstd[:, 0:1],
                                        ALU.subtract, ALU.mult).then_inc(xn_rd, 1)

            def masked(c, q):
                wait(dve, l_rd, 4 * c.n + q + 1)
                piece = L[:, q, :, :]
                nc.vector.tensor_tensor(piece, piece, cbm[:, c.p:c.p + 1, :].to_broadcast([P, PH, P]),
                                        ALU.mult).then_inc(m_rd, 1)

            def steplen(c, own):
                wait(dve, dt_ps, c.n + 1)
                own.then(nc.vector.tensor_tensor(dtm[:, :], bank[1][:, 0:HEADS], bdt[:, :], ALU.add))
                nc.vector.tensor_scalar(dtm[:, :], dtm[:, :], 0.0, None, ALU.min).then_inc(dtm_rd, 1)
                wait(dve, edt_rd, c.n + 1)
                own.then(nc.vector.tensor_scalar(den[:, :], edt[:, :], 0.2, 2.0, ALU.min, ALU.add))
                own.then(nc.vector.reciprocal(den[:, :], den[:, :]))
                own.then(nc.vector.scalar_tensor_tensor(out=sw[:, :], in0=edt[:, :], scalar=0.2, in1=den[:, :],
                                                        op0=ALU.min, op1=ALU.mult))
                own.then(nc.vector.tensor_tensor(sw2[:, :], sw[:, :], sw[:, :], ALU.mult))
                own.then(nc.vector.tensor_scalar(poly[:, :], sw2[:, :], 2 / 7, 2 / 5, ALU.mult, ALU.add))
                own.then(nc.vector.tensor_tensor(poly[:, :], poly[:, :], sw2[:, :], ALU.mult))
                own.then(nc.vector.scalar_tensor_tensor(out=poly[:, :], in0=poly[:, :], scalar=2 / 3, in1=sw2[:, :],
                                                        op0=ALU.add, op1=ALU.mult))
                own.then(nc.vector.scalar_tensor_tensor(out=poly[:, :], in0=poly[:, :], scalar=2.0, in1=sw[:, :],
                                                        op0=ALU.add, op1=ALU.mult))
                own.then(nc.vector.tensor_scalar(dts[:, c.p, :], poly[:, :], DT_MAX, DT_MIN, ALU.min, ALU.max))
                nc.vector.tensor_tensor(adt[:, :], dts[:, c.p, :], neg_a[:, :], ALU.mult).then_inc(adt_rd, 1)

            def convolve(t0, tiles, own, done):
                for j in range(TAPS):
                    for t in range(t0, t0 + tiles):
                        w = hw[:, j * CT + t:j * CT + t + 1]
                        if j == 0:
                            ins = nc.vector.tensor_scalar(cv[:, t, :], cin[:, t, 0:P], w, hb[:, t:t + 1],
                                                          ALU.mult, ALU.add)
                        else:
                            ins = nc.vector.scalar_tensor_tensor(out=cv[:, t, :], in0=cin[:, t, j:j + P], scalar=w,
                                                                 in1=cv[:, t, :], op0=ALU.mult, op1=ALU.add)
                    if j < TAPS - 1:
                        own.then(ins)
                ins.then_inc(done, 1)

            def take(c, t0, tiles, src, own, evacuated):
                own.then(nc.vector.tensor_scalar(cin[:, t0:t0 + tiles, 0:HALO], cin[:, t0:t0 + tiles, P:P + HALO],
                                                 keep[:, bass.ds(c.n, 1)], None, ALU.mult))
                bias = over_heads(cols[:, 40 + t0:40 + t0 + tiles], P)
                nc.vector.tensor_tensor(cin[:, t0:t0 + tiles, HALO:HALO + P],
                                        src.rearrange("p (t l) -> p t l", l=P), bias, ALU.add).then_inc(evacuated, 1)

            def step(cur, prev, nxt):
                own = Own(dve, v_own, FRONT, cur.n) if cur else None
                own2 = Own(dve, v_own2, BACK, prev.n) if prev else None
                if prev:
                    masked(prev, 1)
                if cur:
                    steplen(cur, own)
                if prev:
                    masked(prev, 2)
                if cur:
                    wait(dve, bc_ps, cur.n + 1)
                    take(cur, KI, 2, bank[2][:, 0:2 * P], own, bc_ev)
                    wait(dve, bc_ev, cur.n + 1)
                    convolve(KI, 2, own, bcc_rd)
                    wait(dve, tbc_rd, cur.n + 1)
                    nc.vector.scalar_tensor_tensor(out=cv[:, KI, :], in0=th[:, KI, :], scalar=1.0, in1=cv[:, KI, :],
                                                   op0=ALU.add, op1=ALU.mult)
                    nc.vector.scalar_tensor_tensor(out=ct[:, cur.p, :], in0=th[:, KI + 1, :], scalar=1.0,
                                                   in1=cv[:, KI + 1, :], op0=ALU.add, op1=ALU.mult).then_inc(bct_rd, 1)
                    wait(dve, cum_ps, cur.n + 1)
                    own.then(nc.vector.tensor_copy(cum[:, 0:2, :],
                                                   bank[5][:, 0:2 * HEADS].rearrange("p (a h) -> p a h", a=2)))
                    wait(dve, cum_st, 16 * cur.n)
                    wait(dve, l_rd, 4 * cur.n - 4)
                    nc.vector.tensor_copy(cum_s[:, cur.p, :], cum[:, 0, :])
                    nc.vector.tensor_copy(cumT[:, :], bank[5][0:HEADS, 2 * HEADS:2 * HEADS + P]).then_inc(cumT_rd, 1)
                    nc.vector.tensor_tensor(cum[:, 2, :], cum[:, 1, :], cum[:, 0, :], ALU.subtract)\
                        .then_inc(dif_rd, 1)
                    wait(dve, z_ps, cur.n + 1)
                    for j in range(2):
                        ins = nc.vector.scalar_tensor_tensor(
                            out=sz[:, cur.p, 512 * j:512 * j + 512].rearrange("p (t l) -> p t l", l=P),
                            in0=bank[3 + j][:, :].rearrange("p (t l) -> p t l", l=P), scalar=0.5,
                            in1=over_heads(hzb[:, 4 * j:4 * j + 4], P), op0=ALU.mult, op1=ALU.add)
                    ins.then_inc(z_ev, 1)
                if prev:
                    masked(prev, 3)
                if cur:
                    wait(dve, cb_ps, cur.n + 1)
                    nc.vector.tensor_tensor(cbm[:, cur.p, :], bank[1][:, 0:P], tri[:, :], ALU.mult)
                    nc.vector.tensor_copy(bs[:, cur.p, :], bank[1][:, P:2 * P]).then_inc(cb_rd, 1)
                    wait(dve, cb_rd, cur.n + 1)
                    wait(dve, tz_rd, cur.n + 1)
                    own.then(nc.vector.scalar_tensor_tensor(out=sz[:, cur.p, :], in0=tz[:, :], scalar=1.0,
                                                            in1=sz[:, cur.p, :], op0=ALU.add, op1=ALU.mult))
                    wait(dve, ecum_rd, cur.n + 1)
                    nc.vector.tensor_scalar(ekeep[:, cur.p, :], ecum[:, 0, :], keep[:, bass.ds(cur.n + 1, 1)], None,
                                            ALU.mult)
                    nc.vector.scalar_tensor_tensor(out=wdec[:, cur.p, :], in0=ecum[:, 1, :],
                                                   scalar=keep[:, bass.ds(cur.n + 1, 1)], in1=dts[:, cur.p, :],
                                                   op0=ALU.mult, op1=ALU.mult).then_inc(wdec_rd, 1)
                    wait(dve, wdec_rd, cur.n + 1)
                    masked(cur, 0)
                if prev:
                    m = prev.n
                    wait(dve, out_ps, m)
                    wait(dve, sq_rd, m)
                    wait(dve, ecx_ld, 16 * TH * (m + 1))
                    wait(dve, off_ps, m + 1)
                    half = [y[:, 4 * j:4 * j + 4, :].rearrange("p t l -> p (t l)") for j in range(2)]
                    for j in range(2):
                        ins = nc.vector.tensor_tensor(
                            half[j], bank[j][:, :], ecx[:, 4 * j:4 * j + 4, :].rearrange("p t l -> p (t l)"), ALU.mult)
                    ins.then_inc(off_ev, 1)
                    wait(dve, off_ev, m + 1)
                    for j in range(2):
                        ins = nc.vector.tensor_tensor(half[j], half[j], bank[6 + j][:, :], ALU.add)
                    own2.then(ins)
                    wait(dve, xD_rd, m + 1)
                    own2.then(nc.vector.tensor_tensor(y[:, :, :], y[:, :, :], xD[:, :, :], ALU.add))
                    nc.vector.tensor_tensor(y[:, :, :], y[:, :, :],
                                            sz[:, prev.p, :].rearrange("p (t l) -> p t l", l=P), ALU.mult)\
                        .then_inc(y_rd, 1)
                    wait(dve, state_ps, m + 1)
                    wait(dve, s_dec, m + 1)
                    for j in range(2):
                        ins = nc.vector.tensor_tensor(S[:, 512 * j:512 * j + 512], S[:, 512 * j:512 * j + 512],
                                                      bank[2 + j][:, :], ALU.add)
                    ins.then_inc(S_rd, 1)
                if cur:
                    wait(dve, xT_ps, cur.n)
                    wait(dve, xD_rd, cur.n)
                    for j in range(2):
                        if prev and j == 1:
                            wait(dve, sq_rd, m + 1)
                            wait(dve, sq_ps, m)
                            nc.vector.tensor_reduce(sqs[:, :], sq[:, :, :].rearrange("p t l -> p l t"), AX.X, ALU.add)\
                                .then_inc(sqs_rd, 1)
                        wait(dve, x_ps, 2 * cur.n + j + 1)
                        take(cur, 4 * j, 4, bank[4 + j][:, :], own, xev)
                        wait(dve, xev, 2 * cur.n + j + 1)
                        convolve(4 * j, 4, own, xc_rd)
                elif prev:
                    wait(dve, sq_rd, m + 1)
                    wait(dve, sq_ps, m)
                    nc.vector.tensor_reduce(sqs[:, :], sq[:, :, :].rearrange("p t l -> p l t"), AX.X, ALU.add)\
                        .then_inc(sqs_rd, 1)
                if nxt:
                    norm(nxt)
                if prev:
                    wait(dve, sq_ps, m + 1)
                    wait(dve, rstd2_rd, m)
                    nc.vector.tensor_tensor(vpe2[:, :], bank[6][:, 0:1], eps[:, 1:2], ALU.add).then_inc(vpe2_rd, 1)
                if cur:
                    for j in range(2):
                        wait(dve, tx_rd, 2 * cur.n + j + 1)
                        ins = nc.vector.scalar_tensor_tensor(out=cv[:, 4 * j:4 * j + 4, :],
                                                             in0=th[:, 4 * j:4 * j + 4, :], scalar=1.0,
                                                             in1=cv[:, 4 * j:4 * j + 4, :], op0=ALU.add, op1=ALU.mult)
                    ins.then_inc(xt_rd, 1)
                if prev:
                    wait(dve, out_ps, prev.n + 1)
                    wait(dve, rstd2_rd, prev.n + 1)
                    wait(dve, x2_st[prev.p], 16 * prev.h)
                    nc.vector.scalar_tensor_tensor(out=x2o[:, prev.p, :], in0=bank[0][:, :], scalar=rstd2[:, 0:1],
                                                   in1=xb[:, prev.p, :], op0=ALU.mult, op1=ALU.add).then_inc(x2_rd, 1)
                if cur:
                    own.close()
                if prev:
                    own2.close()

            n_own = sem("n_own")
            xev = sem("xev")
            FRONT = 10 + 1 + 3 + 1 + 1 + 2 * (1 + 3)
            BACK = 2
            norm(Chunk(0, 0, 0))
            dve.wait_ge(wout_in, 16)
            for k in range(KI):
                ins = nc.vector.tensor_scalar(wout[:, k, :], wout[:, k, :], cols[:, 60 + k:61 + k], None, ALU.mult)
            ins.then_inc(params, 1)
            run_steps(dve, step)

        @block.tensor
        def _(pe):
            pe.wait_ge(consts, 4)
            pe.wait_ge(vec_in, 16 * VECS)
            nc.tensor.transpose(bank[0][:, 0:ROWS], rows[:, :], ident[0:ROWS, 0:ROWS])
            pe.wait_ge(drow_rd, 1)
            nc.tensor.transpose(bank[0][:, D0:D0 + KI], drow[:, :], ident[0:KI, 0:KI]).then_inc(cols_ps, 1)
            pe.wait_ge(vset, 1)
            xd_flat = xd[:, :, :].rearrange("p h c -> p (h c)")

            def project(b, c0):
                for t in range(4):
                    for k in range(KH):
                        ins = nc.tensor.matmul(bank[b][:, t * P:(t + 1) * P], win[:, k, c0 + t * P:c0 + (t + 1) * P],
                                               xnT[:, k, :], start=(k == 0), stop=(k == KH - 1))
                return ins

            def step(cur, prev, nxt):
                if cur:
                    n = cur.n
                    wait(pe, xn_rd, n + 1)
                    wait(pe, x2_rd, n - 1)
                    for k in range(KH):
                        ins = nc.tensor.transpose(bank[0][:, k * P:(k + 1) * P], xn[:, k * P:(k + 1) * P], ident[:, :])
                    ins.then_inc(xnT_ps, 1)
                    wait(pe, xnT_rd, n + 1)
                    if isinstance(n, int) and n == 0:
                        pe.wait_ge(win_in, 16 * KH)
                    wait(pe, off_ev, n - 1)
                    for k in range(KH):
                        ins = nc.tensor.matmul(bank[1][:, 0:HEADS], xnT[:, k, :], win[:, k, DT0:PROJ],
                                               start=(k == 0), stop=(k == KH - 1))
                    ins.then_inc(dt_ps, 1)
                    wait(pe, xs_rd, n)
                    for t in range(2):
                        for k in range(KH):
                            ins = nc.tensor.matmul(bank[2][:, t * P:(t + 1) * P],
                                                   win[:, k, B0 + t * P:B0 + (t + 1) * P], xnT[:, k, :],
                                                   start=(k == 0), stop=(k == KH - 1))
                    ins.then_inc(bc_ps, 1)
                    project(3, Z0)
                    wait(pe, adt_rd, n + 1)
                    nc.tensor.matmul(bank[5][:, 0:HEADS], tri[:, :], adt[:, :], start=True, stop=True)
                    nc.tensor.matmul(bank[5][:, HEADS:2 * HEADS], ones[:, :], adt[:, :], start=True, stop=True)
                    nc.tensor.matmul(bank[5][0:HEADS, 2 * HEADS:2 * HEADS + P], adt[:, :], tri[:, :],
                                     start=True, stop=True).then_inc(cum_ps, 1)
                    project(4, Z0 + 4 * P).then_inc(z_ps, 1)
                def bc_products():
                    wait(pe, bct_rd, n + 1)
                    wait(pe, dtm_rd, n + 1)
                    nc.tensor.matmul(bank[1][:, 0:P], cv[:, KI, :], ct[:, cur.p, :], start=True, stop=True)
                    nc.tensor.transpose(bank[1][:, P:2 * P], cv[:, KI, :], ident[:, :]).then_inc(cb_ps, 1)

                if cur and not prev:
                    bc_products()
                if prev:
                    m = prev.n
                    wait(pe, xd_rd, m + 1)
                    wait(pe, vpe2_rd, m)
                    for q in range(PIECES):
                        wait(pe, m_rd, 4 * m + q + 1)
                        for h in range(q * PH, (q + 1) * PH):
                            t, j = h // TH, h % TH
                            at = t * TH * PITCH + j * P
                            ins = nc.tensor.matmul(bank[6 + t // 4][:, (t % 4) * P:(t % 4 + 1) * P],
                                                   xd_flat[:, at:at + P], L[:, q, h % PH, :],
                                                   start=(j == 0), stop=(j == TH - 1))
                        ins.then_inc(diag_ps, 1)
                        if cur and q == 0:
                            bc_products()
                    wait(pe, S_rd, m + 1)
                    if cur:
                        wait(pe, cb_rd, n + 1)
                    else:
                        wait(pe, x2_rd, m)
                        wait(pe, off_ev, m)
                    for t in range(KI):
                        ins = nc.tensor.matmul(bank[t // 4][:, (t % 4) * P:(t % 4 + 1) * P], S[:, t * P:(t + 1) * P],
                                               ct[:, prev.p, :], start=True, stop=True)
                    ins.then_inc(off_ps, 1)
                    if cur:
                        wait(pe, bc_ev, n + 1)
                        wait(pe, z_ev, n + 1)
                    else:
                        wait(pe, xs_rd, m + 1)
                    for j in range(2):
                        ins = nc.tensor.matmul(bank[2 + j][:, :], bs[:, prev.p, :],
                                               xdec[:, 512 * j:512 * j + 512], start=True, stop=True)
                    ins.then_inc(state_ps, 1)
                if cur:
                    wait(pe, z_ev, n + 1)
                    wait(pe, dif_rd, n + 1)
                    for j in range(2):
                        project(4 + j, X0 + 4 * j * P).then_inc(x_ps, 1)
                if prev:
                    wait(pe, y_rd, m + 1)
                    if isinstance(m, int) and m == 0:
                        pe.wait_ge(params, 1)
                    for k in range(KI):
                        ins = nc.tensor.matmul(bank[0][:, :], y[:, k, :], wout[:, k, :],
                                               start=(k == 0), stop=(k == KI - 1))
                    ins.then_inc(out_ps, 1)
                    wait(pe, sqs_rd, m + 1)
                    nc.tensor.matmul(bank[6][:, 0:1], sqs[:, :], ones[:, 0:1], start=True, stop=True)\
                        .then_inc(sq_ps, 1)
                if cur:
                    wait(pe, xt_rd, n + 1)
                    if prev:
                        wait(pe, S_rd, m + 2)
                    for k in range(KI):
                        ins = nc.tensor.transpose(bank[2 + k // 4][:, (k % 4) * P:(k % 4 + 1) * P],
                                                  cv[:, k, :], ident[:, :])
                    ins.then_inc(xT_ps, 1)

            pe.wait_ge(params, 1)
            run_steps(pe, step)


def moe_stage(nc, x2_dram, xn2_dram, gate_w, gate_bias, w1, w2, w3, shared_gate, shared_up, shared_down, out):
    with ExitStack() as ctx:
        def sb(name, shape, dt=F32):
            return ctx.enter_context(nc.sbuf_tensor(name, shape, dt))

        def sem(name):
            return ctx.enter_context(nc.semaphore(name))

        bank = [ctx.enter_context(nc.psum_tensor(f"mbank{i}", [P, 512], F32)) for i in range(8)]
        SLOT_BANK = 6
        NBUF = 4

        ident = sb("m_ident", [P, P])
        tri_f = sb("tri_f", [P, P])
        tri = sb("m_tri", [P, P], BF16)
        ones = sb("m_ones", [P, P], BF16)
        half_exp = sb("m_half_exp", [P, 1])
        eps = sb("m_eps", [P, 1])
        carrier = sb("m_carrier", [P, 1])
        low = sb("low", [P, GROUPS, GROUPS])
        row_i = sb("row_i", [P, 1], I32)
        slot_i = sb("slot_i", [P, CAP, EXPERTS], I32)
        slot_b = sb("slot_b", [P, CAP, EXPERTS], BF16)
        tile_i = sb("tile_i", [P, CHUNKS], I32)
        tile_f = sb("tile_f", [P, CHUNKS])
        row_f = sb("row_f", [P, 1])
        dump = sb("dump", [P, 1])
        one32 = sb("one32", [P, EXPERTS])
        zeros = sb("zeros", [P, HID])
        gw = sb("gw", [EXPERTS, HID])
        gwT = sb("gwT", [P, KH, EXPERTS])
        gbias = sb("gbias", [P, EXPERTS])
        sg = sb("sg", [P, KH, FS])
        su = sb("su", [P, KH, FS])
        sd = sb("sd", [P, KS, HID])
        x2i = sb("x2i", [P, 2, HID])
        xk = sb("xk", [P, 2, HID])
        stat = sb("m_stat", [P, 6])
        mv = sb("m_mv", [P, 2])
        vpe = sb("m_vpe", [P, 1])
        rstd = sb("m_rstd", [P, 1])
        xn = sb("m_xn", [P, 2, HID])
        xnT = sb("m_xnT", [P, 2, KH, P])
        tg = sb("tg", [P, KS * P])
        hT = sb("hT", [P, KS, P])
        oo = sb("oo", [P, 2, HID])
        tl = sb("tl", [P, EXPERTS])
        score = sb("score", [P, EXPERTS])
        sc = sb("sc", [P, EXPERTS])
        top8 = sb("top8", [P, GROUPS, 8])
        gsum = sb("gsum", [P, GROUPS])
        above = sb("above", [P, GROUPS, GROUPS])
        ties = sb("ties", [P, GROUPS, GROUPS])
        rank = sb("rank", [P, GROUPS])
        masked = sb("masked", [P, EXPERTS])
        best8 = sb("best8", [P, 8])
        gt = sb("gt", [P, EXPERTS])
        eq = sb("eq", [P, EXPERTS])
        eqc = sb("eqc", [P, EXPERTS])
        need = sb("need", [P, 1])
        sel = sb("sel", [P, 2, EXPERTS])
        selb = sb("selb", [P, 2, EXPERTS], BF16)
        wt = sb("wt", [P, EXPERTS])
        wsum = sb("wsum", [P, 1])
        base = sb("base", [P, EXPERTS])
        incl = sb("incl", [P, EXPERTS])
        posb = sb("posb", [P, 1, EXPERTS], BF16)
        onehot = sb("onehot", [P, CAP, EXPERTS], BF16)
        R = sb("R", [P, 2, EXPERTS, IDC], BF16)
        zb6 = sb("zb6", [P, EXPERTS * IDC], BF16)
        table = sb("table", [P, EXPERTS, IDC])
        tok = sb("tok", [P, EXPERTS])
        wslot = sb("wslot", [P, EXPERTS])
        unused = sb("unused", [P, EXPERTS])
        dest = sb("dest", [P, EXPERTS])
        w1s = sb("w1s", [P, NBUF, KH, F])
        w3s = sb("w3s", [P, NBUF, KH, F])
        w2s = sb("w2s", [P, NBUF, KF, HID])
        src_ix = [sb(f"src_ix{p}", [P, 1], U32) for p in range(2)]
        dst_ix = [sb(f"dst_ix{p}", [P, 1], U32) for p in range(2)]
        wcol = sb("wcol", [P, 2])
        xe = [sb(f"xe{p}", [P, HID]) for p in range(2)]
        xeT = sb("xeT", [P, 2, KH, P])
        te = sb("te", [P, F])
        ae = sb("ae", [P, F])
        hTe = sb("hTe", [P, 2, KF, P])
        gcar = sb("gcar", [P, 4])
        ob = [sb(f"ob{p}", [P, HID]) for p in range(2)]

        par_ld = sem("par_ld"); sh_ld = sem("sh_ld"); zero_st = sem("zero_st")
        x_ld = [sem("mx_ld0"), sem("mx_ld1")]
        xn_st = [sem("xn_st0"), sem("xn_st1")]
        o_st = [sem("o_st0"), sem("o_st1")]
        w_ld = [sem(f"w_ld{j}") for j in range(NBUF)]
        xe_ld = [sem("xe_ld0"), sem("xe_ld1")]
        add_st = sem("add_st")
        g_set = sem("g_set"); g_set2 = sem("g_set2"); gw_ps = sem("gw_ps"); v_set = sem("v_set")
        xnT_ps = sem("m_xnT_ps"); gu_ps = sem("gu_ps"); lg_ps = sem("lg_ps"); cnt_ps = sem("cnt_ps")
        dn_ps = sem("dn_ps"); slot_ps = sem("slot_ps")
        xeT_ps = sem("xeT_ps"); gue_ps = sem("gue_ps"); dne_ps = sem("dne_ps")
        v_own = sem("mv_own"); v_cnt = sem("v_cnt"); n_own = sem("mn_own"); var_rd = sem("m_var_rd")
        xn_rd = sem("m_xn_rd"); h_rd = sem("h_rd"); sel_rd = sem("sel_rd"); oh_rd = sem("oh_rd")
        o_rd = sem("o_rd"); v_h = sem("v_h"); fin = sem("fin"); ix_rd = sem("ix_rd"); he_rd = sem("he_rd")
        v_he = sem("v_he"); wcol_rd = sem("wcol_rd")
        xnT_rd = sem("m_xnT_rd"); tg_rd = sem("tg_rd"); xk_rd = sem("xk_rd"); tl_rd = sem("tl_rd")
        xeT_rd = sem("xeT_rd"); te_rd = sem("te_rd"); ob_rd = sem("ob_rd")
        g_var = sem("mg_var"); rstd_rd = sem("m_rstd_rd"); g_car = sem("g_car"); g_car2 = sem("g_car2")

        block = ctx.enter_context(nc.Block())

        x2_rows = x2_dram.rearrange("(c p) h -> c p h", p=P)
        xn2_rows = xn2_dram.rearrange("(c p) h -> c p h", p=P)
        out_rows = out.rearrange("(c p) h -> c p h", p=P)

        def run_experts(eng, step):
            for e in range(NBUF):
                step(e, e, 0)
            with eng.Fori(1, EXPERTS // NBUF - 1) as i:
                for j in range(NBUF):
                    step(NBUF * i + j, j, i)
            for j in range(NBUF):
                step(EXPERTS - NBUF + j, j, EXPERTS // NBUF - 1)

        def turns(e, j, i):
            return 2 * i + j // 2

        @block.sync
        def _(sp):
            sp.dma_start(x2i[:, 0, :], x2_rows[0, :, :]).then_inc(x_ld[0], 16)
            sp.dma_start(x2i[:, 1, :], x2_rows[1, :, :]).then_inc(x_ld[1], 16)
            sp.dma_start(gw[:, :], gate_w).then_inc(par_ld, 16)
            sp.dma_start(gbias[:, :], gate_bias.rearrange("(a n) -> a n", a=1).to_broadcast([P, EXPERTS]))\
                .then_inc(par_ld, 16)
            for dst, src in ((sg, shared_gate), (su, shared_up), (sd, shared_down)):
                sp.dma_start(dst[:, :, :], src.rearrange("(k p) f -> p k f", p=P)).then_inc(sh_ld, 16)

            def load_expert(e, j, i):
                wait(sp, dne_ps, e - NBUF + 1)
                sp.dma_start(w1s[:, j, :, :], w1[bass.ds(e, 1), :, :].rearrange("a (k p) f -> p (a k) f", p=P))\
                    .then_inc(w_ld[j], 16)
                sp.dma_start(w3s[:, j, :, :], w3[bass.ds(e, 1), :, :].rearrange("a (k p) f -> p (a k) f", p=P))\
                    .then_inc(w_ld[j], 16)
                sp.dma_start(w2s[:, j, :, :], w2[bass.ds(e, 1), :, :].rearrange("a (k p) h -> p (a k) h", p=P))\
                    .then_inc(w_ld[j], 16)

            for e in range(NBUF):
                load_expert(e, e, 0)
            sp.wait_ge(g_set2, 1)
            sp.dma_start(out_rows[CHUNKS, :, :], zeros[:, :]).then_inc(zero_st, 16)

            def step(cur, prev, nxt):
                if cur:
                    n = cur.n
                    wait(sp, xn_rd, n + 1)
                    sp.dma_start(xn2_rows[n, :, :], xn[:, cur.p, :]).then_inc(xn_st[cur.p], 16)
                    wait(sp, xk_rd, n + 1)
                    if nxt:
                        sp.dma_start(x2i[:, cur.p, :], x2_rows[n + 2, :, :]).then_inc(x_ld[cur.p], 16)
                if prev:
                    wait(sp, o_rd, prev.n + 1)
                    sp.dma_start(out_rows[prev.n, :, :], oo[:, prev.p, :]).then_inc(o_st[prev.p], 16)

            run_steps(sp, step, loads_ahead=True)
            for p in range(2):
                sp.wait_ge(xn_st[p], 16 * CHUNKS // 2)
                sp.wait_ge(o_st[p], 16 * CHUNKS // 2)
            sp.wait_ge(zero_st, 16)

            with sp.Fori(1, EXPERTS // NBUF) as i:
                for j in range(NBUF):
                    load_expert(NBUF * i + j, j, i)

        @block.gpsimd
        def _(pool):
            nc.gpsimd.memset(ident[:, :], 0.0).then_inc(g_set, 1)
            nc.gpsimd.memset(tri_f[:, :], 1.0).then_inc(g_set, 1)
            nc.gpsimd.memset(low[:, :, :], 1.0).then_inc(g_set, 1)
            nc.gpsimd.memset(half_exp[:, :], -0.5).then_inc(g_set, 1)
            nc.gpsimd.memset(eps[:, :], LN_EPS).then_inc(g_set, 1)
            nc.gpsimd.memset(zeros[:, :], 0.0).then_inc(g_set2, 1)
            pool.wait_ge(g_set, 5)
            nc.gpsimd.affine_select(out=ident[:, :], in_=ident[:, :], compare_op=ALU.not_equal, fill=1.0,
                                    base=0, pattern=[[-1, P]], channel_multiplier=1).then_inc(g_set2, 1)
            nc.gpsimd.affine_select(out=tri_f[:, :], in_=tri_f[:, :], compare_op=ALU.is_ge, fill=0.0,
                                    base=0, pattern=[[1, P]], channel_multiplier=-1).then_inc(g_set2, 1)
            nc.gpsimd.affine_select(out=low[:, :, :], in_=low[:, :, :], compare_op=ALU.is_gt, fill=0.0,
                                    base=0, pattern=[[1, GROUPS], [-1, GROUPS]], channel_multiplier=0)\
                .then_inc(g_set2, 1)
            nc.gpsimd.iota(row_i[:, :], pattern=[[0, 1]], base=0, channel_multiplier=1).then_inc(g_set2, 1)
            nc.gpsimd.iota(tile_i[:, :], pattern=[[1, CHUNKS]], base=0, channel_multiplier=0).then_inc(g_set2, 1)
            nc.gpsimd.iota(slot_i[:, :, :], pattern=[[1, CAP], [0, EXPERTS]], base=0, channel_multiplier=0)\
                .then_inc(g_set2, 1)

            def norm_root(c):
                wait(pool, var_rd, c.n + 1)
                Own(pool, g_var, 1, c.n).then(nc.gpsimd.tensor_tensor(vpe[:, :], mv[:, 1:2], eps[:, :], ALU.add))
                nc.gpsimd.tensor_tensor(rstd[:, :], vpe[:, :], half_exp[:, :], ALU.pow).then_inc(rstd_rd, 1)

            norm_root(Chunk(0, 0, 0))

            def step(cur, prev, nxt):
                if nxt:
                    norm_root(nxt)

            run_steps(pool, step)
            for p in range(2):
                pool.wait_ge(xn_st[p], 16 * CHUNKS // 2)
                pool.wait_ge(o_st[p], 16 * CHUNKS // 2)
            pool.wait_ge(zero_st, 16)

            def gather(e, j, i):
                p = j % 2
                wait(pool, ix_rd, e + 1)
                wait(pool, xeT_ps, e - 1)
                wait(pool, g_car, e - 1)
                nc.gpsimd.tensor_tensor(gcar[:, p:p + 1], half_exp[:, :], half_exp[:, :], ALU.add).then_inc(g_car, 1)
                nc.gpsimd.indirect_dma_start(
                    out=xe[p][:, :], out_offset=None, in_=xn2_dram,
                    in_offset=bass.IndirectOffsetOnAxis(ap=src_ix[p][:, 0:1], axis=0),
                    bounds_check=TOKENS - 1, oob_is_err=True).then_inc(xe_ld[p], 16)

            def scatter(e, j, i):
                p = j % 2
                wait(pool, ob_rd, e + 1)
                wait(pool, add_st, 16 * e)
                wait(pool, wcol_rd, e + 1)
                wait(pool, g_car2, e - 1)
                nc.gpsimd.tensor_tensor(gcar[:, 2 + p:3 + p], half_exp[:, :], half_exp[:, :], ALU.add)\
                    .then_inc(g_car2, 1)
                nc.gpsimd.indirect_dma_start(
                    out=out, out_offset=bass.IndirectOffsetOnAxis(ap=dst_ix[p][:, 0:1], axis=0),
                    in_=ob[p][:, :], in_offset=None, bounds_check=TOKENS + P - 1, oob_is_err=True,
                    compute_op=ALU.add).then_inc(add_st, 16)

            def expert(e, j, i):
                if not (isinstance(e, int) and e + 2 >= EXPERTS):
                    gather(e + 2, (j + 2) % 4, i)
                if not (isinstance(e, int) and e < 1):
                    scatter(e - 1, (j + 3) % 4, i)

            gather(0, 0, 0)
            gather(1, 1, 0)
            run_experts(pool, expert)
            scatter(EXPERTS - 1, 3, EXPERTS // NBUF - 1)
            pool.wait_ge(add_st, 16 * EXPERTS)

        @block.scalar
        def _(act):
            def step(cur, prev, nxt):
                if cur:
                    wait(act, xnT_ps, cur.n + 1)
                    nc.scalar.activation(xnT[:, cur.p, :, :], bank[0][:, :].rearrange("p (k t) -> p k t", t=P),
                                         ACT.Copy).then_inc(xnT_rd, 1)
                    wait(act, x_ld[cur.p], 16 * cur.h + 16)
                    wait(act, o_rd, cur.n - 1)
                    wait(act, xn_rd, cur.n + 1)
                    nc.scalar.activation(xk[:, cur.p, :], x2i[:, cur.p, :], ACT.Copy).then_inc(xk_rd, 1)
                if prev:
                    wait(act, gu_ps, prev.n + 1)
                    nc.scalar.activation(tg[:, :], bank[1][:, :], ACT.Tanh, scale=0.5).then_inc(tg_rd, 1)
                if cur:
                    wait(act, lg_ps, cur.n + 1)
                    wait(act, sel_rd, cur.n)
                    nc.scalar.activation(tl[:, :], bank[4][:, 0:EXPERTS], ACT.Tanh, scale=0.5).then_inc(tl_rd, 1)

            run_steps(act, step)

            def turn_expert(e, j, i):
                p = j % 2
                wait(act, xeT_ps, e + 1)
                nc.scalar.activation(xeT[:, p, :, :], bank[p][:, :].rearrange("p (k t) -> p k t", t=P), ACT.Copy)\
                    .then_inc(xeT_rd, 1)

            def weigh_expert(e, j, i):
                p = j % 2
                wait(act, dne_ps, e + 1)
                wait(act, wcol_rd, e + 1)
                wait(act, add_st, 16 * (e - 1))
                nc.scalar.activation(ob[p][:, :], bank[4 + p][:, :], ACT.Copy, scale=wcol[:, p:p + 1]).then_inc(ob_rd, 1)

            def expert(e, j, i):
                wait(act, gue_ps, e + 1)
                wait(act, he_rd, e)
                nc.scalar.activation(te[:, :], bank[2 + j % 2][:, 0:F], ACT.Tanh, scale=0.5).then_inc(te_rd, 1)
                if not (isinstance(e, int) and e + 1 >= EXPERTS):
                    turn_expert(e + 1, (j + 1) % 4, i)
                if not (isinstance(e, int) and e < 1):
                    weigh_expert(e - 1, (j + 3) % 4, i)

            turn_expert(0, 0, 0)
            run_experts(act, expert)
            weigh_expert(EXPERTS - 1, 3, EXPERTS // NBUF - 1)

        @block.vector
        def _(dve):
            dve.wait_ge(g_set2, 7)
            nc.vector.tensor_copy(tri[:, :], tri_f[:, :]).then_inc(v_set, 1)
            nc.vector.memset(ones[:, :], 1.0).then_inc(v_set, 1)
            nc.vector.memset(zb6[:, :], 0.0).then_inc(v_set, 1)
            nc.vector.tensor_copy(slot_b[:, :, :], slot_i[:, :, :]).then_inc(v_set, 1)
            nc.vector.tensor_copy(tile_f[:, :], tile_i[:, :]).then_inc(v_set, 1)
            nc.vector.tensor_copy(row_f[:, :], row_i[:, :]).then_inc(v_set, 1)
            nc.vector.memset(one32[:, :], 1.0).then_inc(v_set, 1)
            nc.vector.memset(base[:, :], 0.0).then_inc(v_set, 1)
            dve.wait_ge(v_set, 8)
            nc.vector.tensor_scalar(dump[:, :], row_f[:, :], float(TOKENS), None, ALU.add).then_inc(v_set, 1)
            for p in range(2):
                nc.vector.memset(R[:, p, :, 2:3], 1.0).then_inc(v_set, 1)
                nc.vector.tensor_scalar(R[:, p, :, 1:2].rearrange("p e c -> p (e c)"), one32[:, :], row_f[:, 0:1],
                                        None, ALU.mult).then_inc(v_set, 1)
            dve.wait_ge(gw_ps, 1)
            nc.vector.tensor_copy(gwT[:, :, :], bank[0][:, 0:KH * EXPERTS].rearrange("p (k e) -> p k e", e=EXPERTS))\
                .then_inc(v_set, 1)
            dve.wait_ge(v_set, 14)

            COUNT = 3

            def norm(c):
                wait(dve, x_ld[c.p], 16 * c.h + 16)
                nc.vector.bn_stats(stat[:, :], x2i[:, c.p, :]).then_inc(n_own, 1)
                wait(dve, n_own, c.n + 1)
                nc.vector.memset(carrier[:, :], 0.0)
                nc.vector.bn_aggr(mv[:, :], stat[:, :]).then_inc(var_rd, 1)
                wait(dve, rstd_rd, c.n + 1)
                wait(dve, var_rd, c.n + 1)
                wait(dve, xnT_ps, c.n - 1)
                wait(dve, xn_st[c.p], 16 * c.h)
                nc.vector.tensor_scalar(xn[:, c.p, :], x2i[:, c.p, :], mv[:, 0:1], rstd[:, 0:1],
                                        ALU.subtract, ALU.mult).then_inc(xn_rd, 1)

            def choose(c, own):
                wait(dve, tl_rd, c.n + 1)
                own.then(nc.vector.tensor_scalar(score[:, :], tl[:, :], 0.5, 0.5, ALU.mult, ALU.add))
                own.then(nc.vector.tensor_tensor(sc[:, :], score[:, :], gbias[:, :], ALU.add))
                nc.vector.memset(carrier[:, :], 0.0)
                for g in range(GROUPS):
                    ins = nc.vector.max(top8[:, g, :], sc[:, g * GE:(g + 1) * GE])
                own.then(ins)
                own.then(nc.vector.tensor_tensor(gsum[:, :], top8[:, :, 0], top8[:, :, 1], ALU.add))
                other = gsum[:, :].unsqueeze(1).to_broadcast([P, GROUPS, GROUPS])
                mine = gsum[:, :].unsqueeze(2).to_broadcast([P, GROUPS, GROUPS])
                nc.vector.tensor_tensor(above[:, :, :], other, mine, ALU.is_gt)
                own.then(nc.vector.tensor_tensor(ties[:, :, :], other, mine, ALU.is_equal))
                own.then(nc.vector.tensor_tensor(ties[:, :, :], ties[:, :, :], low[:, :, :], ALU.mult))
                own.then(nc.vector.tensor_tensor(above[:, :, :], above[:, :, :], ties[:, :, :], ALU.add))
                own.then(nc.vector.tensor_reduce(rank[:, :], above[:, :, :], AX.X, ALU.add))
                own.then(nc.vector.tensor_scalar(rank[:, :], rank[:, :], 2.0, None, ALU.is_lt))
                own.then(nc.vector.tensor_tensor(masked[:, :].rearrange("p (g e) -> p g e", e=GE),
                                                 sc[:, :].rearrange("p (g e) -> p g e", e=GE),
                                                 over_heads(rank[:, :], GE), ALU.mult))
                nc.vector.memset(carrier[:, :], 0.0)
                own.then(nc.vector.max(best8[:, :], masked[:, :]))
                fourth = best8[:, TOPK - 1:TOPK]
                nc.vector.tensor_scalar(gt[:, :], masked[:, :], fourth, None, ALU.is_gt)
                own.then(nc.vector.tensor_scalar(eq[:, :], masked[:, :], fourth, None, ALU.is_equal))
                nc.vector.tensor_reduce(need[:, :], gt[:, :], AX.X, ALU.add)
                own.then(nc.vector.tensor_tensor_scan(eqc[:, :], one32[:, :], eq[:, :], 0.0, ALU.mult, ALU.add))
                own.then(nc.vector.tensor_scalar(need[:, :], need[:, :], -1.0, float(TOPK), ALU.mult, ALU.add))
                own.then(nc.vector.scalar_tensor_tensor(out=eq[:, :], in0=eqc[:, :], scalar=need[:, 0:1], in1=eq[:, :],
                                                        op0=ALU.is_le, op1=ALU.mult))
                wait(dve, cnt_ps, c.n - 1)
                nc.vector.tensor_tensor(selb[:, c.p, :], gt[:, :], eq[:, :], ALU.add)
                own.then(nc.vector.tensor_tensor(sel[:, c.p, :], gt[:, :], eq[:, :], ALU.add))
                own.then(nc.vector.tensor_tensor(wt[:, :], score[:, :], sel[:, c.p, :], ALU.mult))
                own.then(nc.vector.tensor_reduce(wsum[:, :], wt[:, :], AX.X, ALU.add))
                own.then(nc.vector.tensor_scalar(wsum[:, :], wsum[:, :], 1e-20, None, ALU.add))
                own.then(nc.vector.reciprocal(wsum[:, :], wsum[:, :]))
                own.then(nc.vector.tensor_scalar(wt[:, :], wt[:, :], wsum[:, 0:1], ROUTED_SCALE, ALU.mult, ALU.mult))
                col = [R[:, c.p, :, a:a + 1].rearrange("p e c -> p (e c)") for a in range(IDC)]
                wait(dve, slot_ps, c.n - 1)
                own.then(nc.vector.tensor_copy(col[3], wt[:, :]))
                own.then(nc.vector.tensor_tensor(wt[:, :], wt[:, :], col[3], ALU.subtract))
                own.then(nc.vector.tensor_copy(col[4], wt[:, :]))
                own.then(nc.vector.tensor_tensor(wt[:, :], wt[:, :], col[4], ALU.subtract))
                nc.vector.tensor_copy(col[5], wt[:, :])
                nc.vector.tensor_scalar(col[0], one32[:, :], tile_f[:, bass.ds(c.n, 1)], None, ALU.mult)\
                    .then_inc(sel_rd, 1)
                wait(dve, sel_rd, c.n + 1)

            def count(c, own):
                wait(dve, cnt_ps, c.n + 1)
                own.then(nc.vector.tensor_tensor(incl[:, :], bank[5][:, 0:EXPERTS], base[:, :], ALU.add))
                nc.vector.tensor_tensor(base[:, :], bank[5][:, EXPERTS:2 * EXPERTS], base[:, :], ALU.add)
                own.then(nc.vector.tensor_tensor(incl[:, :], incl[:, :], sel[:, c.p, :], ALU.mult))
                own.then(nc.vector.tensor_scalar(posb[:, 0, :], incl[:, :], -1.0, None, ALU.add))
                wait(dve, slot_ps, c.n)
                nc.vector.tensor_tensor(onehot[:, :, :], slot_b[:, :, :], posb[:, :, :].to_broadcast([P, CAP, EXPERTS]),
                                        ALU.is_equal).then_inc(oh_rd, 1)
                wait(dve, oh_rd, c.n + 1)

            def step(cur, prev, nxt):
                if prev:
                    count(prev, Own(dve, v_cnt, COUNT, prev.n))
                    wait(dve, tg_rd, prev.n + 1)
                    nc.vector.scalar_tensor_tensor(out=tg[:, :], in0=tg[:, :], scalar=1.0, in1=bank[1][:, :],
                                                   op0=ALU.add, op1=ALU.mult).then_inc(v_h, 1)
                    wait(dve, v_h, prev.n + 1)
                    wait(dve, dn_ps, prev.n)
                    nc.vector.scalar_tensor_tensor(out=hT[:, :, :].rearrange("p k t -> p (k t)"), in0=tg[:, :],
                                                   scalar=0.5, in1=bank[2][:, :], op0=ALU.mult, op1=ALU.mult)\
                        .then_inc(h_rd, 1)
                if cur:
                    own = Own(dve, v_own, CHOICE, cur.n)
                    choose(cur, own)
                    own.close()
                if nxt:
                    norm(nxt)
                if prev:
                    wait(dve, dn_ps, prev.n + 1)
                    wait(dve, xk_rd, prev.n + 1)
                    wait(dve, o_st[prev.p], 16 * prev.h)
                    nc.vector.tensor_tensor(oo[:, prev.p, :], bank[3][:, :], xk[:, prev.p, :], ALU.add)\
                        .then_inc(o_rd, 1)

            CHOICE = 25
            dve.wait_ge(par_ld, 32)
            norm(Chunk(0, 0, 0))
            run_steps(dve, step)

            dve.wait_ge(slot_ps, CHUNKS)
            nc.vector.tensor_copy(table[:, :, :],
                                  bank[SLOT_BANK][:, 0:EXPERTS * IDC].rearrange("p (e c) -> p e c", c=IDC))\
                .then_inc(fin, 1)
            dve.wait_ge(fin, 1)
            cell = [table[:, :, a:a + 1].rearrange("p e c -> p (e c)") for a in range(IDC)]
            nc.vector.scalar_tensor_tensor(out=tok[:, :], in0=cell[0], scalar=float(P), in1=cell[1],
                                           op0=ALU.mult, op1=ALU.add)
            nc.vector.tensor_scalar(unused[:, :], cell[2], -1.0, 1.0, ALU.mult, ALU.add)
            nc.vector.tensor_tensor(wslot[:, :], cell[3], cell[4], ALU.add).then_inc(fin, 1)
            dve.wait_ge(fin, 2)
            nc.vector.tensor_tensor(wslot[:, :], wslot[:, :], cell[5], ALU.add)
            nc.vector.scalar_tensor_tensor(out=dest[:, :], in0=unused[:, :], scalar=dump[:, 0:1], in1=tok[:, :],
                                           op0=ALU.mult, op1=ALU.add).then_inc(fin, 1)
            dve.wait_ge(fin, 3)

            def source(e, j, i):
                p = j % 2
                wait(dve, xe_ld[p], 16 * turns(e, j, i))
                nc.vector.tensor_scalar(src_ix[p][:, :], tok[:, bass.ds(e, 1)], 1.0, None, ALU.mult).then_inc(ix_rd, 1)

            def target(e, j, i):
                p = j % 2
                wait(dve, add_st, 16 * (e - 1))
                nc.vector.tensor_scalar(dst_ix[p][:, :], dest[:, bass.ds(e, 1)], 1.0, None, ALU.mult)
                nc.vector.tensor_scalar(wcol[:, p:p + 1], wslot[:, bass.ds(e, 1)], 1.0, None, ALU.mult)\
                    .then_inc(wcol_rd, 1)

            def expert(e, j, i):
                b = bank[2 + j % 2]
                if not (isinstance(e, int) and e + 2 >= EXPERTS):
                    source(e + 2, (j + 2) % 4, i if j < 2 else i + 1)
                wait(dve, te_rd, e + 1)
                nc.vector.scalar_tensor_tensor(out=ae[:, :], in0=te[:, :], scalar=1.0, in1=b[:, 0:F],
                                               op0=ALU.add, op1=ALU.mult).then_inc(v_he, 1)
                wait(dve, v_he, e + 1)
                wait(dve, dne_ps, e - 1)
                nc.vector.scalar_tensor_tensor(out=hTe[:, j % 2, :, :].rearrange("p k t -> p (k t)"), in0=ae[:, :],
                                               scalar=0.5, in1=b[:, F:2 * F], op0=ALU.mult, op1=ALU.mult)\
                    .then_inc(he_rd, 1)
                target(e, j, i)

            source(0, 0, 0)
            source(1, 1, 0)
            run_experts(dve, expert)

        @block.tensor
        def _(pe):
            pe.wait_ge(g_set2, 2)
            pe.wait_ge(par_ld, 32)
            for k in range(KH):
                ins = nc.tensor.transpose(bank[0][:, k * EXPERTS:(k + 1) * EXPERTS], gw[:, k * P:(k + 1) * P],
                                          ident[0:EXPERTS, 0:EXPERTS])
            ins.then_inc(gw_ps, 1)
            pe.wait_ge(v_set, 14)
            nc.tensor.matmul(bank[SLOT_BANK][:, 0:EXPERTS * IDC], ones[:, :], zb6[:, :], start=True, stop=True,
                             skip_group_check=True)

            def step(cur, prev, nxt):
                if cur:
                    n = cur.n
                    wait(pe, xn_rd, n + 1)
                    wait(pe, xnT_rd, n)
                    for k in range(KH):
                        ins = nc.tensor.transpose(bank[0][:, k * P:(k + 1) * P], xn[:, cur.p, k * P:(k + 1) * P],
                                                  ident[:, :])
                    ins.then_inc(xnT_ps, 1)
                if prev:
                    m = prev.n
                    if isinstance(m, int) and m == 0:
                        pe.wait_ge(sh_ld, 48)
                    wait(pe, h_rd, m)
                    for b, w in ((1, sg), (2, su)):
                        for f in range(KS):
                            for k in range(KH):
                                ins = nc.tensor.matmul(bank[b][:, f * P:(f + 1) * P], w[:, k, f * P:(f + 1) * P],
                                                       xnT[:, prev.p, k, :], start=(k == 0), stop=(k == KH - 1))
                    ins.then_inc(gu_ps, 1)
                if cur:
                    wait(pe, xnT_rd, n + 1)
                    wait(pe, tl_rd, n)
                    for k in range(KH):
                        ins = nc.tensor.matmul(bank[4][:, 0:EXPERTS], xnT[:, cur.p, k, :], gwT[:, k, :],
                                               start=(k == 0), stop=(k == KH - 1))
                    ins.then_inc(lg_ps, 1)
                if prev:
                    wait(pe, sel_rd, m + 1)
                    wait(pe, oh_rd, m)
                    nc.tensor.matmul(bank[5][:, 0:EXPERTS], tri[:, :], selb[:, prev.p, :], start=True, stop=True)
                    nc.tensor.matmul(bank[5][:, EXPERTS:2 * EXPERTS], ones[:, :], selb[:, prev.p, :],
                                     start=True, stop=True).then_inc(cnt_ps, 1)
                    wait(pe, h_rd, m + 1)
                    wait(pe, o_rd, m)
                    for f in range(KS):
                        ins = nc.tensor.matmul(bank[3][:, :], hT[:, f, :], sd[:, f, :],
                                               start=(f == 0), stop=(f == KS - 1))
                    ins.then_inc(dn_ps, 1)
                    wait(pe, oh_rd, m + 1)
                    for e in range(EXPERTS):
                        ins = nc.tensor.matmul(bank[SLOT_BANK][:, e * IDC:(e + 1) * IDC], onehot[:, :, e],
                                               R[:, prev.p, e, :], start=False, stop=True, skip_group_check=True)
                    ins.then_inc(slot_ps, 1)

            run_steps(pe, step)

            def turn(e, j, i):
                p = j % 2
                wait(pe, xe_ld[p], 16 * turns(e, j, i) + 16)
                wait(pe, xeT_rd, e - 1)
                for k in range(KH):
                    ins = nc.tensor.transpose(bank[p][:, k * P:(k + 1) * P], xe[p][:, k * P:(k + 1) * P], ident[:, :])
                ins.then_inc(xeT_ps, 1)

            def down(e, j, i):
                p = j % 2
                wait(pe, he_rd, e + 1)
                wait(pe, ob_rd, e - 1)
                for f in range(KF):
                    ins = nc.tensor.matmul(bank[4 + p][:, :], hTe[:, p, f, :], w2s[:, j, f, :],
                                           start=(f == 0), stop=(f == KF - 1))
                ins.then_inc(dne_ps, 1)

            def expert(e, j, i):
                p = j % 2
                wait(pe, w_ld[j], 48 * i + 48)
                wait(pe, xeT_rd, e + 1)
                wait(pe, he_rd, e - 1)
                for b, w in ((0, w1s), (F, w3s)):
                    for f in range(KF):
                        for k in range(KH):
                            ins = nc.tensor.matmul(bank[2 + p][:, b + f * P:b + (f + 1) * P],
                                                   w[:, j, k, f * P:(f + 1) * P], xeT[:, p, k, :],
                                                   start=(k == 0), stop=(k == KH - 1))
                ins.then_inc(gue_ps, 1)
                if not (isinstance(e, int) and e + 1 >= EXPERTS):
                    turn(e + 1, (j + 1) % 4, i if j < 3 else i + 1)
                if not (isinstance(e, int) and e < 1):
                    down(e - 1, (j + 3) % 4, i)

            pe.wait_ge(o_rd, CHUNKS)
            pe.wait_ge(fin, 1)
            turn(0, 0, 0)
            run_experts(pe, expert)
            down(EXPERTS - 1, 3, EXPERTS // NBUF - 1)


def build(nc, x, W_in, b_in, conv_w, conv_b, A_log, dt_bias, D_param, norm_w, W_out, b_out,
          gate_w, gate_bias, w1, w2, w3, shared_gate, shared_up, shared_down, out):
    cum_dram = nc.dram_tensor("cum_rows", (2, HEADS, P), F32, kind="Internal").ap()
    ecum_dram = nc.dram_tensor("ecum_rows", (2, HEADS, P), F32, kind="Internal").ap()
    x2_dram = nc.dram_tensor("x2_rows", (TOKENS, HID), F32, kind="Internal").ap()
    xn2_dram = nc.dram_tensor("xn2_rows", (TOKENS, HID), F32, kind="Internal").ap()
    mamba_stage(nc, x, W_in, b_in, conv_w, conv_b, A_log, dt_bias, D_param, norm_w, W_out, b_out,
                cum_dram, ecum_dram, x2_dram)
    moe_stage(nc, x2_dram, xn2_dram, gate_w, gate_bias, w1, w2, w3, shared_gate, shared_up, shared_down, out)


_INS = ["L0_attn_x", "L0_attn_W_in", "L0_attn_b_in", "L0_attn_conv_w", "L0_attn_conv_b", "L0_attn_A_log",
        "L0_attn_dt_bias", "L0_attn_D_param", "L0_attn_norm_w", "L0_attn_W_out", "L0_attn_b_out",
        "L0_ffn_gate_w", "L0_ffn_gate_bias", "L0_ffn_w1", "L0_ffn_w2", "L0_ffn_w3",
        "L0_ffn_shared_gate", "L0_ffn_shared_up", "L0_ffn_shared_down"]


def kernel(**inputs):
    import numpy as np
    import concourse.bacc as bacc
    from concourse.bass_utils import run_bass_kernel_spmd

    nc = bacc.Bacc("TRN2", target_bir_lowering=False, num_devices=1)
    arrays, args = {}, []
    for name in _INS:
        a = np.ascontiguousarray(inputs[name])
        arrays[f"in_{name}"] = a
        args.append(nc.dram_tensor(f"in_{name}", a.shape, mybir.dt.from_np(a.dtype), kind="ExternalInput").ap())
    out = nc.dram_tensor("out_0", (TOKENS + P, HID), F32, kind="ExternalOutput").ap()
    build(nc, *args, out)
    r = run_bass_kernel_spmd(nc, [arrays], core_ids=[0])
    got = r.results[0]["out_0"]
    return got[:TOKENS].reshape(4, 512, 512)
```

```python
from contextlib import ExitStack

import concourse.bass as bass
from concourse import mybir

ALU = mybir.AluOpType
ACT = mybir.ActivationFunctionType
AX = mybir.AxisListType
F32 = mybir.dt.float32
BF16 = mybir.dt.bfloat16
I32 = mybir.dt.int32
U32 = mybir.dt.uint32

P = 128
HID = 512
KH = HID // P
INNER = 1024
HEADS = 64
HD = INNER // HEADS
KI = INNER // P
CT = (INNER + 2 * P) // P
TAPS = 4
HALO = TAPS - 1
Z0, X0, B0, DT0 = 0, INNER, 2 * INNER, 2 * INNER + 2 * P
PROJ = DT0 + HEADS
TOKENS = 2048
CHUNKS = TOKENS // P
PER_SEQ = 4
LN_EPS, RMS_EPS = 1e-5, 1e-6
DT_MIN, DT_MAX = 1e-3, 1e-1
PIECES = 4
PH = HEADS // PIECES
TH = P // HD
PITCH = P + HD

EXPERTS = 32
GROUPS = 4
GE = EXPERTS // GROUPS
TOPK = 4
CAP = 128
F = 256
KF = F // P
FS = 512
KS = FS // P
ROUTED_SCALE = 2.0
IDC = 6


def wait(eng, sem, value):
    if isinstance(value, int) and value <= 0:
        return
    eng.wait_ge(sem, value)


class Own:

    def __init__(self, eng, sem, rate, n):
        self.eng, self.sem, self.rate, self.n, self.k = eng, sem, rate, n, 0

    def then(self, ins):
        self.k += 1
        ins.then_inc(self.sem, 1)
        self.eng.wait_ge(self.sem, self.rate * self.n + self.k)

    def close(self):
        assert self.k == self.rate, (self.k, self.rate)


class Chunk:

    def __init__(self, n, p, h):
        self.n, self.p, self.h = n, p, h


def run_steps(eng, step, loads_ahead=False):
    last = CHUNKS - 1

    def at(n):
        return Chunk(n, n % 2, n // 2) if 0 <= n <= last else None

    def peeled(n):
        step(at(n), at(n - 1), at(n + 2) if loads_ahead else at(n + 1))

    for n in range(3):
        peeled(n)
    with eng.Fori(1, 6 if loads_ahead else 7) as i:
        step(Chunk(2 * i + 1, 1, i), Chunk(2 * i, 0, i), Chunk(2 * i + 2, 0, i + 1))
        step(Chunk(2 * i + 2, 0, i + 1), Chunk(2 * i + 1, 1, i), Chunk(2 * i + 3, 1, i + 1))
    for n in range(13 if loads_ahead else 15, CHUNKS + 1):
        peeled(n)


def over_heads(ap, width):
    return ap.unsqueeze(2).to_broadcast([ap.shape[0], ap.shape[1], width])


ROWS = 76
Z_ROW, D0 = 68, ROWS
VECS = 11


def mamba_stage(nc, x, W_in, b_in, conv_w, conv_b, A_log, dt_bias, D_param, norm_w, W_out, b_out,
                cum_dram, ecum_dram, x2_dram):
    with ExitStack() as ctx:
        def sb(name, shape, dt=F32):
            return ctx.enter_context(nc.sbuf_tensor(name, shape, dt))

        def sem(name):
            return ctx.enter_context(nc.semaphore(name))

        bank = [ctx.enter_context(nc.psum_tensor(f"bank{i}", [P, 512], F32)) for i in range(8)]

        win = sb("win", [P, KH, PROJ])
        wout = sb("wout", [P, KI, HID])
        ident = sb("ident", [P, P])
        tri = sb("tri", [P, P])
        ones = sb("ones", [P, P])
        keep = sb("keep", [P, CHUNKS + 1])
        half_exp = sb("half_exp", [P, 1])
        dhead = sb("dhead", [KI, TH])
        drow = sb("drow", [KI, P])
        rows = sb("rows", [ROWS, P])
        cols = sb("cols", [P, ROWS + KI])
        hw = sb("hw", [P, TAPS * CT])
        hb = sb("hb", [P, CT])
        hzb = sb("hzb", [P, KI])
        bo = sb("bo", [P, HID])
        bdt = sb("bdt", [P, HEADS])
        neg_a = sb("neg_a", [P, HEADS])
        x_in = sb("x_in", [P, 2, HID])
        xb = sb("xb", [P, 2, HID])
        stat = sb("stat", [P, 6])
        mv = sb("mv", [P, 2])
        carrier = sb("carrier", [P, 1])
        eps = sb("eps", [P, 2])
        vpe = sb("vpe", [P, 1])
        rstd = sb("rstd", [P, 1])
        xn = sb("xn", [P, HID])
        xnT = sb("xnT", [P, KH, P])
        dtm = sb("dtm", [P, HEADS])
        edt = sb("edt", [P, HEADS])
        den = sb("den", [P, HEADS])
        sw = sb("sw", [P, HEADS])
        sw2 = sb("sw2", [P, HEADS])
        poly = sb("poly", [P, HEADS])
        dts = sb("dts", [P, 2, HEADS])
        adt = sb("adt", [P, HEADS])
        cum = sb("cum", [P, 3, HEADS])
        ecum = sb("ecum", [P, 2, HEADS])
        ekeep = sb("ekeep", [P, 2, HEADS])
        cum_s = sb("cum_s", [P, 2, HEADS])
        wdec = sb("wdec", [P, 2, HEADS])
        cumT = sb("cumT", [HEADS, P])
        ecumT = sb("ecumT", [HEADS, P])
        ecx = sb("ecx", [P, KI, P])
        cin = sb("cin", [P, CT, HALO + P])
        cv = sb("cv", [P, CT, P])
        th = sb("th", [P, CT, P])
        ct = sb("ct", [P, 2, P])
        sz = sb("sz", [P, 2, INNER])
        tz = sb("tz", [P, INNER])
        cbm = sb("cbm", [P, 2, P])
        bs = sb("bs", [P, 2, P])
        xs = sb("xs", [P, INNER])
        xd = sb("xd", [P, HEADS, PITCH])
        xdec = sb("xdec", [P, INNER])
        xD = sb("xD", [P, KI, P])
        L = sb("L", [P, PIECES, PH, P])
        S = sb("S", [P, INNER])
        y = sb("y", [P, KI, P])
        sq = sb("sq", [P, KI, P])
        sqs = sb("sqs", [P, P])
        vpe2 = sb("vpe2", [P, 1])
        rstd2 = sb("rstd2", [P, 1])
        x2o = sb("x2o", [P, 2, HID])

        bcdt_in = sem("bcdt_in"); wz_in = sem("wz_in"); wx_in = sem("wx_in")
        wout_in = sem("wout_in"); vec_in = sem("vec_in")
        x_ld = [sem("x_ld0"), sem("x_ld1")]
        cum_st = sem("cum_st"); ec_st = sem("ec_st"); ecx_ld = sem("ecx_ld")
        cum_ld = [sem(f"cum_ld{q}") for q in range(PIECES)]
        x2_st = [sem("x2_st0"), sem("x2_st1")]
        pool_set = sem("pool_set"); consts = sem("consts"); cols_ps = sem("cols_ps")
        vset = sem("vset"); aset = sem("aset"); params = sem("params"); s_zero = sem("s_zero")
        xnT_ps = sem("xnT_ps"); dt_ps = sem("dt_ps"); bc_ps = sem("bc_ps"); z_ps = sem("z_ps")
        cum_ps = sem("cum_ps"); diag_ps = sem("diag_ps"); off_ps = sem("off_ps")
        state_ps = sem("state_ps"); cb_ps = sem("cb_ps"); x_ps = sem("x_ps"); sq_ps = sem("sq_ps")
        out_ps = sem("out_ps"); xT_ps = sem("xT_ps")
        n_own = sem("n_own"); xev = sem("xev"); v_own = sem("v_own"); v_own2 = sem("v_own2")
        var_rd = sem("var_rd"); xn_rd = sem("xn_rd"); dtm_rd = sem("dtm_rd"); adt_rd = sem("adt_rd")
        bc_ev = sem("bc_ev"); bcc_rd = sem("bcc_rd"); z_ev = sem("z_ev"); cumT_rd = sem("cumT_rd")
        dif_rd = sem("dif_rd"); bct_rd = sem("bct_rd"); wdec_rd = sem("wdec_rd"); m_rd = sem("m_rd")
        off_ev = sem("off_ev"); sqs_rd = sem("sqs_rd"); vpe2_rd = sem("vpe2_rd")
        drow_rd = sem("drow_rd"); y_rd = sem("y_rd"); S_rd = sem("S_rd"); cb_rd = sem("cb_rd")
        xc_rd = sem("xc_rd"); xt_rd = sem("xt_rd"); x2_rd = sem("x2_rd")
        xnT_rd = sem("xnT_rd"); edt_rd = sem("edt_rd"); tbc_rd = sem("tbc_rd"); tz_rd = sem("tz_rd")
        ecum_rd = sem("ecum_rd"); l_rd = sem("l_rd"); sq_rd = sem("sq_rd"); ecumT_rd = sem("ecumT_rd")
        tx_rd = sem("tx_rd"); seg_rd = sem("seg_rd"); xs_rd = sem("xs_rd")
        g_var = sem("g_var"); xdec_rd = sem("xdec_rd"); xD_rd = sem("xD_rd"); m0_rd = sem("m0_rd")
        xd_zero = sem("xd_zero"); rstd_rd = sem("rstd_rd"); rstd2_rd = sem("rstd2_rd")
        xb_rd = sem("xb_rd"); s_dec = sem("s_dec"); xd_rd = sem("xd_rd")

        block = ctx.enter_context(nc.Block())

        x_rows = x.rearrange("b (c p) h -> (b c) p h", p=P)
        x2_rows = x2_dram.rearrange("(c p) h -> c p h", p=P)

        @block.sync
        def _(sp):
            def load_x(c):
                sp.dma_start(x_in[:, c.p, :], x_rows[c.n, :, :]).then_inc(x_ld[c.p], 16)

            load_x(Chunk(0, 0, 0))
            load_x(Chunk(1, 1, 0))
            sp.wait_ge(vec_in, 16 * VECS)
            for (first, last), done in (((B0, PROJ), bcdt_in), ((Z0, X0), wz_in), ((X0, B0), wx_in)):
                sp.dma_start(win[:, :, first:last], W_in[:, first:last].rearrange("(k p) c -> p k c", p=P))\
                    .then_inc(done, 16)
            sp.dma_start(wout[:, :, :], W_out.rearrange("(k p) h -> p k h", p=P)).then_inc(wout_in, 16)

            def step(cur, prev, nxt):
                if cur:
                    n = cur.n
                    wait(sp, cumT_rd, n + 1)
                    sp.dma_start(cum_dram[cur.p], cumT[:, :]).then_inc(cum_st, 16)
                    wait(sp, cum_st, 16 * n + 16)
                    back = cum_dram[cur.p].rearrange("(q h) l -> q (h l)", q=PIECES)

                    def piece(q):
                        wait(sp, diag_ps, 4 * n + q - 3)
                        sp.dma_start(L[:, q].rearrange("p h l -> p (h l)"),
                                     back[q:q + 1, :].to_broadcast([P, PH * P])).then_inc(cum_ld[q], 16)

                    piece(0)
                    piece(1)
                    wait(sp, ecumT_rd, n + 1)
                    sp.dma_start(ecum_dram[cur.p], ecumT[:, :]).then_inc(ec_st, 16)
                    piece(2)
                    piece(3)
                    wait(sp, ec_st, 16 * n + 16)
                    wait(sp, y_rd, n)
                    per_tile = ecum_dram[cur.p].rearrange("(t j) l -> j t l", j=TH)
                    for j in range(TH):
                        sp.dma_start(ecx[j * HD:(j + 1) * HD, :, :],
                                     per_tile[j:j + 1, :, :].to_broadcast([HD, KI, P])).then_inc(ecx_ld, 16)
                    if nxt:
                        wait(sp, xb_rd, n + 1)
                        wait(sp, xn_rd, n + 1)
                        sp.dma_start(x_in[:, cur.p, :], x_rows[n + 2, :, :]).then_inc(x_ld[cur.p], 16)
                if prev:
                    wait(sp, x2_rd, prev.n + 1)
                    sp.dma_start(x2_rows[prev.n, :, :], x2o[:, prev.p, :]).then_inc(x2_st[prev.p], 16)

            run_steps(sp, step, loads_ahead=True)
            for p in range(2):
                wait(sp, x2_st[p], 16 * (CHUNKS // 2))

        @block.gpsimd
        def _(pool):
            nc.gpsimd.memset(ident[:, :], 0.0).then_inc(pool_set, 1)
            nc.gpsimd.memset(tri[:, :], 1.0).then_inc(pool_set, 1)
            nc.gpsimd.memset(ones[:, :], 1.0).then_inc(consts, 1)
            nc.gpsimd.memset(half_exp[:, :], -0.5).then_inc(pool_set, 1)
            nc.gpsimd.memset(eps[:, 0:1], LN_EPS).then_inc(pool_set, 1)
            nc.gpsimd.memset(eps[:, 1:2], RMS_EPS).then_inc(pool_set, 1)
            nc.gpsimd.memset(keep[:, :], 1.0).then_inc(pool_set, 1)
            pool.wait_ge(pool_set, 6)
            nc.gpsimd.affine_select(out=ident[:, :], in_=ident[:, :], compare_op=ALU.not_equal, fill=1.0,
                                    base=0, pattern=[[-1, P]], channel_multiplier=1).then_inc(consts, 1)
            nc.gpsimd.affine_select(out=tri[:, :], in_=tri[:, :], compare_op=ALU.is_ge, fill=0.0,
                                    base=0, pattern=[[1, P]], channel_multiplier=-1).then_inc(consts, 1)
            nc.gpsimd.memset(keep[:, 0:CHUNKS].rearrange("p (s c) -> p s c", c=PER_SEQ)[:, :, 0:1], 0.0)\
                .then_inc(consts, 1)
            nc.gpsimd.memset(S[:, :], 0.0).then_inc(S_rd, 1)
            nc.gpsimd.memset(cin[:, :, :], 0.0).then_inc(s_zero, 1)

            def norm_root(c):
                wait(pool, var_rd, c.n + 1)
                Own(pool, g_var, 1, c.n).then(nc.gpsimd.tensor_tensor(vpe[:, :], mv[:, 1:2], eps[:, 0:1], ALU.add))
                nc.gpsimd.tensor_tensor(rstd[:, :], vpe[:, :], half_exp[:, :], ALU.pow).then_inc(rstd_rd, 1)

            norm_root(Chunk(0, 0, 0))
            nc.gpsimd.memset(xd[:, :, :], 0.0).then_inc(xd_zero, 1)

            def step(cur, prev, nxt):
                if cur:
                    wait(pool, x_ld[cur.p], 16 * cur.h + 16)
                    wait(pool, x2_rd, cur.n - 1)
                    wait(pool, vec_in, 16 * VECS)
                    nc.gpsimd.tensor_tensor(xb[:, cur.p, :], x_in[:, cur.p, :], bo[:, :], ALU.add)\
                        .then_inc(xb_rd, 1)
                if nxt:
                    norm_root(nxt)
                if prev:
                    wait(pool, off_ps, prev.n + 1)
                    wait(pool, wdec_rd, prev.n + 1)
                    nc.gpsimd.tensor_tensor(S[:, :].rearrange("p (h d) -> p h d", d=HD),
                                            S[:, :].rearrange("p (h d) -> p h d", d=HD),
                                            over_heads(ekeep[:, prev.p, :], HD), ALU.mult).then_inc(s_dec, 1)
                if cur:
                    wait(pool, l_rd, 4 * cur.n + 1)
                    nc.gpsimd.tensor_tensor(L[:, 0, :, :], L[:, 0, :, :],
                                            cbm[:, cur.p:cur.p + 1, :].to_broadcast([P, PH, P]), ALU.mult)\
                        .then_inc(m0_rd, 1)
                if cur:
                    wait(pool, xt_rd, cur.n + 1)
                    wait(pool, y_rd, cur.n)
                    nc.gpsimd.tensor_tensor(xD[:, :, :], cv[:, 0:KI, :], over_heads(cols[:, D0:D0 + KI], P), ALU.mult)\
                        .then_inc(xD_rd, 1)
                if prev:
                    wait(pool, x2_rd, prev.n)
                    wait(pool, vpe2_rd, prev.n + 1)
                    nc.gpsimd.tensor_tensor(rstd2[:, :], vpe2[:, :], half_exp[:, :], ALU.pow).then_inc(rstd2_rd, 1)
                if cur:
                    wait(pool, xs_rd, cur.n + 1)
                    wait(pool, wdec_rd, cur.n + 1)
                    wait(pool, S_rd, cur.n)
                    xv = xs[:, :].rearrange("p (h d) -> p h d", d=HD)
                    nc.gpsimd.tensor_tensor(xd[:, :, 0:HD], xv, over_heads(dts[:, cur.p, :], HD), ALU.mult)\
                        .then_inc(xd_rd, 1)
                    nc.gpsimd.tensor_tensor(xdec[:, :].rearrange("p (h d) -> p h d", d=HD), xv,
                                            over_heads(wdec[:, cur.p, :], HD), ALU.mult).then_inc(xdec_rd, 1)

            pool.wait_ge(vset, 1)
            pool.wait_ge(xd_zero, 1)
            run_steps(pool, step)

        @block.scalar
        def _(act):
            def vec(dst, src):
                act.dma_start(dst, src).then_inc(vec_in, 16)

            def spread(dst, src):
                vec(dst, src.rearrange("(a n) -> a n", a=1).to_broadcast([P, src.shape[0]]))

            vec(rows[0:40, :], conv_w.rearrange("j a (t p) -> (j a t) p", p=P))
            vec(rows[40:50, :], b_in[X0:DT0].rearrange("(t p) -> t p", p=P))
            vec(rows[50:60, :], conv_b.rearrange("(t p) -> t p", p=P))
            vec(rows[60:68, :], norm_w.rearrange("(t p) -> t p", p=P))
            vec(rows[Z_ROW:Z_ROW + KI, :], b_in[Z0:X0].rearrange("(t p) -> t p", p=P))
            vec(dhead[:, :], D_param.rearrange("(t j) -> t j", j=TH))
            spread(bdt[:, :], b_in[DT0:PROJ])
            spread(poly[:, :], dt_bias)
            spread(neg_a[:, :], A_log)
            spread(bo[:, 0:256], b_out[0:256])
            spread(bo[:, 256:512], b_out[256:512])
            act.wait_ge(vec_in, 16 * VECS)
            nc.scalar.activation(neg_a[:, :], neg_a[:, :], ACT.Exp).then_inc(aset, 1)

            def differences(c, q):
                wait(act, cum_ld[q], 16 * c.n + 16)
                wait(act, cumT_rd, c.n + 1)
                for h in range(PH):
                    row = L[:, q, h, :]
                    ins = nc.scalar.activation(row, row, ACT.Relu, scale=-1.0,
                                               bias=cum_s[:, c.p, q * PH + h:q * PH + h + 1])
                ins.then_inc(seg_rd, 1)

            def decays(c, q):
                wait(act, seg_rd, 4 * c.n + q + 1)
                nc.scalar.activation(L[:, q, :, :], L[:, q, :, :], ACT.Exp, scale=-1.0).then_inc(l_rd, 1)

            def tanh_x(c, j):
                wait(act, xc_rd, 2 * c.n + j + 1)
                nc.scalar.activation(th[:, 4 * j:4 * j + 4, :], cv[:, 4 * j:4 * j + 4, :], ACT.Tanh)\
                    .then_inc(tx_rd, 1)

            def take_xnT(c):
                wait(act, xnT_ps, c.n + 1)
                nc.scalar.activation(xnT[:, :, :].rearrange("p k t -> p (k t)"), bank[5][:, :], ACT.Copy)\
                    .then_inc(xnT_rd, 1)

            take_xnT(Chunk(0, 0, 0))

            def step(cur, prev, nxt):
                if cur:
                    wait(act, dtm_rd, cur.n + 1)
                    nc.scalar.activation(edt[:, :], dtm[:, :], ACT.Exp).then_inc(edt_rd, 1)
                if prev:
                    if isinstance(prev.n, int) and prev.n == 0:
                        differences(prev, 2)
                        decays(prev, 2)
                    differences(prev, 3)
                    decays(prev, 3)
                if cur:
                    wait(act, bcc_rd, cur.n + 1)
                    nc.scalar.activation(th[:, KI:CT, :], cv[:, KI:CT, :], ACT.Tanh).then_inc(tbc_rd, 1)
                    wait(act, dif_rd, cur.n + 1)
                    nc.scalar.activation(ecum[:, :, :], cum[:, 1:3, :], ACT.Exp).then_inc(ecum_rd, 1)
                    wait(act, ec_st, 16 * cur.n)
                    nc.scalar.activation(ecumT[:, :], cumT[:, :], ACT.Exp).then_inc(ecumT_rd, 1)
                    wait(act, z_ev, cur.n + 1)
                    nc.scalar.activation(tz[:, :], sz[:, cur.p, :], ACT.Tanh).then_inc(tz_rd, 1)
                    differences(cur, 0)
                    decays(cur, 0)
                    tanh_x(cur, 0)
                    differences(cur, 1)
                    decays(cur, 1)
                if prev:
                    wait(act, y_rd, prev.n + 1)
                    wait(act, sqs_rd, prev.n)
                    nc.scalar.activation(sq[:, :, :], y[:, :, :], ACT.Square, scale=INNER ** -0.5).then_inc(sq_rd, 1)
                if cur and prev:
                    differences(cur, 2)
                if cur:
                    tanh_x(cur, 1)
                if nxt:
                    take_xnT(nxt)
                if cur and prev:
                    decays(cur, 2)
                if cur:
                    wait(act, xT_ps, cur.n + 1)
                    wait(act, xdec_rd, cur.n)
                    for j in range(2):
                        ins = nc.scalar.activation(xs[:, 512 * j:512 * j + 512], bank[6 + j][:, :], ACT.Copy)
                    ins.then_inc(xs_rd, 1)

            run_steps(act, step)

        @block.vector
        def _(dve):
            def norm(c):
                wait(dve, x_ld[c.p], 16 * c.h + 16)
                stats = nc.vector.bn_stats(stat[:, :], x_in[:, c.p, :])
                stats.then_inc(n_own, 1)
                wait(dve, n_own, c.n + 1)
                nc.vector.memset(carrier[:, :], 0.0)
                nc.vector.bn_aggr(mv[:, :], stat[:, :]).then_inc(var_rd, 1)
                wait(dve, rstd_rd, c.n + 1)
                wait(dve, var_rd, c.n + 1)
                wait(dve, xnT_ps, c.n)
                nc.vector.tensor_scalar(xn[:, :], x_in[:, c.p, :], mv[:, 0:1], rstd[:, 0:1],
                                        ALU.subtract, ALU.mult).then_inc(xn_rd, 1)

            def masked(c, q):
                wait(dve, l_rd, 4 * c.n + q + 1)
                piece = L[:, q, :, :]
                nc.vector.tensor_tensor(piece, piece, cbm[:, c.p:c.p + 1, :].to_broadcast([P, PH, P]),
                                        ALU.mult).then_inc(m_rd, 1)

            def steplen(c, own):
                wait(dve, dt_ps, c.n + 1)
                own.then(nc.vector.tensor_tensor(dtm[:, :], bank[1][:, 0:HEADS], bdt[:, :], ALU.add))
                nc.vector.tensor_scalar(dtm[:, :], dtm[:, :], 0.0, None, ALU.min).then_inc(dtm_rd, 1)
                wait(dve, edt_rd, c.n + 1)
                own.then(nc.vector.tensor_scalar(den[:, :], edt[:, :], 0.2, 2.0, ALU.min, ALU.add))
                own.then(nc.vector.reciprocal(den[:, :], den[:, :]))
                own.then(nc.vector.scalar_tensor_tensor(out=sw[:, :], in0=edt[:, :], scalar=0.2, in1=den[:, :],
                                                        op0=ALU.min, op1=ALU.mult))
                own.then(nc.vector.tensor_tensor(sw2[:, :], sw[:, :], sw[:, :], ALU.mult))
                own.then(nc.vector.tensor_scalar(poly[:, :], sw2[:, :], 2 / 7, 2 / 5, ALU.mult, ALU.add))
                own.then(nc.vector.tensor_tensor(poly[:, :], poly[:, :], sw2[:, :], ALU.mult))
                own.then(nc.vector.scalar_tensor_tensor(out=poly[:, :], in0=poly[:, :], scalar=2 / 3, in1=sw2[:, :],
                                                        op0=ALU.add, op1=ALU.mult))
                own.then(nc.vector.scalar_tensor_tensor(out=poly[:, :], in0=poly[:, :], scalar=2.0, in1=sw[:, :],
                                                        op0=ALU.add, op1=ALU.mult))
                own.then(nc.vector.tensor_scalar(dts[:, c.p, :], poly[:, :], DT_MAX, DT_MIN, ALU.min, ALU.max))
                nc.vector.tensor_tensor(adt[:, :], dts[:, c.p, :], neg_a[:, :], ALU.mult).then_inc(adt_rd, 1)

            def convolve(t0, tiles, own, done):
                for j in range(TAPS):
                    for t in range(t0, t0 + tiles):
                        w = hw[:, j * CT + t:j * CT + t + 1]
                        if j == 0:
                            ins = nc.vector.tensor_scalar(cv[:, t, :], cin[:, t, 0:P], w, hb[:, t:t + 1],
                                                          ALU.mult, ALU.add)
                        else:
                            ins = nc.vector.scalar_tensor_tensor(out=cv[:, t, :], in0=cin[:, t, j:j + P], scalar=w,
                                                                 in1=cv[:, t, :], op0=ALU.mult, op1=ALU.add)
                    if j < TAPS - 1:
                        own.then(ins)
                ins.then_inc(done, 1)

            def take(c, t0, tiles, src, own, evacuated):
                own.then(nc.vector.tensor_scalar(cin[:, t0:t0 + tiles, 0:HALO], cin[:, t0:t0 + tiles, P:P + HALO],
                                                 keep[:, bass.ds(c.n, 1)], None, ALU.mult))
                bias = over_heads(cols[:, 40 + t0:40 + t0 + tiles], P)
                nc.vector.tensor_tensor(cin[:, t0:t0 + tiles, HALO:HALO + P],
                                        src.rearrange("p (t l) -> p t l", l=P), bias, ALU.add).then_inc(evacuated, 1)

            def convolve_x(c, j, own):
                wait(dve, xT_ps, c.n)
                wait(dve, xD_rd, c.n)
                wait(dve, x_ps, 2 * c.n + j + 1)
                take(c, 4 * j, 4, bank[4 + j][:, :], own, xev)
                wait(dve, xev, 2 * c.n + j + 1)
                convolve(4 * j, 4, own, xc_rd)

            def silu_x(c, j):
                wait(dve, tx_rd, 2 * c.n + j + 1)
                return nc.vector.scalar_tensor_tensor(out=cv[:, 4 * j:4 * j + 4, :], in0=th[:, 4 * j:4 * j + 4, :],
                                                      scalar=1.0, in1=cv[:, 4 * j:4 * j + 4, :],
                                                      op0=ALU.add, op1=ALU.mult)

            def step(cur, prev, nxt):
                own = Own(dve, v_own, FRONT, cur.n) if cur else None
                own2 = Own(dve, v_own2, BACK, prev.n) if prev else None
                if cur:
                    steplen(cur, own)
                if prev:
                    masked(prev, 1)
                    masked(prev, 2)
                if cur:
                    wait(dve, bc_ps, cur.n + 1)
                    take(cur, KI, 2, bank[2][:, 0:2 * P], own, bc_ev)
                    wait(dve, bc_ev, cur.n + 1)
                    convolve(KI, 2, own, bcc_rd)
                    wait(dve, tbc_rd, cur.n + 1)
                    nc.vector.scalar_tensor_tensor(out=cv[:, KI, :], in0=th[:, KI, :], scalar=1.0, in1=cv[:, KI, :],
                                                   op0=ALU.add, op1=ALU.mult)
                    nc.vector.scalar_tensor_tensor(out=ct[:, cur.p, :], in0=th[:, KI + 1, :], scalar=1.0,
                                                   in1=cv[:, KI + 1, :], op0=ALU.add, op1=ALU.mult).then_inc(bct_rd, 1)
                    wait(dve, cum_ps, cur.n + 1)
                    own.then(nc.vector.tensor_copy(cum[:, 0:2, :],
                                                   bank[5][:, 0:2 * HEADS].rearrange("p (a h) -> p a h", a=2)))
                    wait(dve, cum_st, 16 * cur.n)
                    wait(dve, l_rd, 4 * cur.n - 4)
                    nc.vector.tensor_copy(cum_s[:, cur.p, :], cum[:, 0, :])
                    nc.vector.tensor_copy(cumT[:, :], bank[5][0:HEADS, 2 * HEADS:2 * HEADS + P]).then_inc(cumT_rd, 1)
                    nc.vector.tensor_tensor(cum[:, 2, :], cum[:, 1, :], cum[:, 0, :], ALU.subtract)\
                        .then_inc(dif_rd, 1)
                    wait(dve, z_ps, cur.n + 1)
                    for j in range(2):
                        ins = nc.vector.scalar_tensor_tensor(
                            out=sz[:, cur.p, 512 * j:512 * j + 512].rearrange("p (t l) -> p t l", l=P),
                            in0=bank[3 + j][:, :].rearrange("p (t l) -> p t l", l=P), scalar=0.5,
                            in1=over_heads(hzb[:, 4 * j:4 * j + 4], P), op0=ALU.mult, op1=ALU.add)
                    ins.then_inc(z_ev, 1)
                if prev:
                    masked(prev, 3)
                if cur:
                    wait(dve, cb_ps, cur.n + 1)
                    nc.vector.tensor_tensor(cbm[:, cur.p, :], bank[1][:, 0:P], tri[:, :], ALU.mult)
                    nc.vector.tensor_copy(bs[:, cur.p, :], bank[1][:, P:2 * P]).then_inc(cb_rd, 1)
                    wait(dve, cb_rd, cur.n + 1)
                    wait(dve, tz_rd, cur.n + 1)
                    own.then(nc.vector.scalar_tensor_tensor(out=sz[:, cur.p, :], in0=tz[:, :], scalar=1.0,
                                                            in1=sz[:, cur.p, :], op0=ALU.add, op1=ALU.mult))
                    wait(dve, ecum_rd, cur.n + 1)
                    nc.vector.tensor_scalar(ekeep[:, cur.p, :], ecum[:, 0, :], keep[:, bass.ds(cur.n + 1, 1)], None,
                                            ALU.mult)
                    nc.vector.scalar_tensor_tensor(out=wdec[:, cur.p, :], in0=ecum[:, 1, :],
                                                   scalar=keep[:, bass.ds(cur.n + 1, 1)], in1=dts[:, cur.p, :],
                                                   op0=ALU.mult, op1=ALU.mult).then_inc(wdec_rd, 1)
                    wait(dve, wdec_rd, cur.n + 1)
                if nxt:
                    norm(nxt)
                if cur:
                    convolve_x(cur, 0, own)
                    silu_x(cur, 0)
                if prev:
                    m = prev.n
                    wait(dve, out_ps, m)
                    wait(dve, sq_rd, m)
                    wait(dve, ecx_ld, 16 * TH * (m + 1))
                    wait(dve, off_ps, m + 1)
                    half = [y[:, 4 * j:4 * j + 4, :].rearrange("p t l -> p (t l)") for j in range(2)]
                    for j in range(2):
                        ins = nc.vector.tensor_tensor(
                            half[j], bank[j][:, :], ecx[:, 4 * j:4 * j + 4, :].rearrange("p t l -> p (t l)"), ALU.mult)
                    ins.then_inc(off_ev, 1)
                    wait(dve, off_ev, m + 1)
                    for j in range(2):
                        ins = nc.vector.tensor_tensor(half[j], half[j], bank[6 + j][:, :], ALU.add)
                    own2.then(ins)
                    wait(dve, xD_rd, m + 1)
                    own2.then(nc.vector.tensor_tensor(y[:, :, :], y[:, :, :], xD[:, :, :], ALU.add))
                    nc.vector.tensor_tensor(y[:, :, :], y[:, :, :],
                                            sz[:, prev.p, :].rearrange("p (t l) -> p t l", l=P), ALU.mult)\
                        .then_inc(y_rd, 1)
                if cur:
                    convolve_x(cur, 1, own)
                if cur:
                    silu_x(cur, 1).then_inc(xt_rd, 1)
                if not prev:
                    dve.wait_ge(wout_in, 16)
                    for k in range(KI):
                        ins = nc.vector.tensor_scalar(wout[:, k, :], wout[:, k, :], cols[:, 60 + k:61 + k], None,
                                                      ALU.mult)
                    ins.then_inc(params, 1)
                if prev:
                    wait(dve, sq_rd, m + 1)
                    wait(dve, sq_ps, m)
                    nc.vector.tensor_reduce(sqs[:, :], sq[:, :, :].rearrange("p t l -> p l t"), AX.X, ALU.add)\
                        .then_inc(sqs_rd, 1)
                    wait(dve, state_ps, m + 1)
                    wait(dve, s_dec, m + 1)
                    for j in range(2):
                        ins = nc.vector.tensor_tensor(S[:, 512 * j:512 * j + 512], S[:, 512 * j:512 * j + 512],
                                                      bank[2 + j][:, :], ALU.add)
                    ins.then_inc(S_rd, 1)
                    wait(dve, sq_ps, m + 1)
                    wait(dve, rstd2_rd, m)
                    nc.vector.tensor_tensor(vpe2[:, :], bank[4][:, 0:1], eps[:, 1:2], ALU.add).then_inc(vpe2_rd, 1)
                if prev:
                    wait(dve, out_ps, prev.n + 1)
                    wait(dve, rstd2_rd, prev.n + 1)
                    wait(dve, x2_st[prev.p], 16 * prev.h)
                    nc.vector.scalar_tensor_tensor(out=x2o[:, prev.p, :], in0=bank[0][:, :], scalar=rstd2[:, 0:1],
                                                   in1=xb[:, prev.p, :], op0=ALU.mult, op1=ALU.add).then_inc(x2_rd, 1)
                if cur:
                    own.close()
                if prev:
                    own2.close()

            FRONT = 10 + 1 + 3 + 1 + 1 + 2 * (1 + 3)
            BACK = 2
            norm(Chunk(0, 0, 0))
            dve.wait_ge(vec_in, 16 * VECS)
            nc.vector.tensor_copy(drow[:, :].rearrange("t (j d) -> t j d", d=HD), over_heads(dhead[:, :], HD))\
                .then_inc(drow_rd, 1)
            dve.wait_ge(cols_ps, 1)
            nc.vector.tensor_copy(cols[:, :], bank[0][:, 0:ROWS + KI]).then_inc(vset, 1)
            dve.wait_ge(vset, 1)
            nc.vector.tensor_scalar(hw[:, :], cols[:, 0:40], 0.5, None, ALU.mult).then_inc(vset, 1)
            nc.vector.tensor_scalar(hb[:, :], cols[:, 50:60], 0.5, None, ALU.mult).then_inc(vset, 1)
            dve.wait_ge(vec_in, 16 * VECS)
            nc.vector.tensor_tensor(bdt[:, :], bdt[:, :], poly[:, :], ALU.add).then_inc(vset, 1)
            nc.vector.tensor_scalar(hzb[:, :], cols[:, Z_ROW:Z_ROW + KI], 0.5, None, ALU.mult).then_inc(vset, 1)
            dve.wait_ge(aset, 1)
            nc.vector.tensor_scalar(neg_a[:, :], neg_a[:, :], -1.0, None, ALU.mult).then_inc(vset, 1)
            dve.wait_ge(vset, 6)
            dve.wait_ge(s_zero, 1)
            dve.wait_ge(consts, 4)
            run_steps(dve, step)

        @block.tensor
        def _(pe):
            pe.wait_ge(consts, 4)
            pe.wait_ge(vec_in, 16 * VECS)
            nc.tensor.transpose(bank[0][:, 0:ROWS], rows[:, :], ident[0:ROWS, 0:ROWS])
            pe.wait_ge(drow_rd, 1)
            nc.tensor.transpose(bank[0][:, D0:D0 + KI], drow[:, :], ident[0:KI, 0:KI]).then_inc(cols_ps, 1)
            pe.wait_ge(vset, 1)
            xd_flat = xd[:, :, :].rearrange("p h c -> p (h c)")

            def project(b, c0):
                for t in range(4):
                    for k in range(KH):
                        ins = nc.tensor.matmul(bank[b][:, t * P:(t + 1) * P], win[:, k, c0 + t * P:c0 + (t + 1) * P],
                                               xnT[:, k, :], start=(k == 0), stop=(k == KH - 1))
                return ins

            def turn_xn(c):
                wait(pe, xn_rd, c.n + 1)
                wait(pe, xev, 2 * c.n)
                for k in range(KH):
                    ins = nc.tensor.transpose(bank[5][:, k * P:(k + 1) * P], xn[:, k * P:(k + 1) * P], ident[:, :])
                ins.then_inc(xnT_ps, 1)

            def step(cur, prev, nxt):
                if cur:
                    n = cur.n
                    wait(pe, xnT_rd, n + 1)
                    if isinstance(n, int) and n == 0:
                        pe.wait_ge(bcdt_in, 16)
                    wait(pe, off_ev, n - 1)
                    for k in range(KH):
                        ins = nc.tensor.matmul(bank[1][:, 0:HEADS], xnT[:, k, :], win[:, k, DT0:PROJ],
                                               start=(k == 0), stop=(k == KH - 1))
                    ins.then_inc(dt_ps, 1)
                    wait(pe, S_rd, n)
                    for t in range(2):
                        for k in range(KH):
                            ins = nc.tensor.matmul(bank[2][:, t * P:(t + 1) * P],
                                                   win[:, k, B0 + t * P:B0 + (t + 1) * P], xnT[:, k, :],
                                                   start=(k == 0), stop=(k == KH - 1))
                    ins.then_inc(bc_ps, 1)
                    if isinstance(n, int) and n == 0:
                        pe.wait_ge(wz_in, 16)
                    project(3, Z0)
                    wait(pe, adt_rd, n + 1)
                    nc.tensor.matmul(bank[5][:, 0:HEADS], tri[:, :], adt[:, :], start=True, stop=True)
                    nc.tensor.matmul(bank[5][:, HEADS:2 * HEADS], ones[:, :], adt[:, :], start=True, stop=True)
                    nc.tensor.matmul(bank[5][0:HEADS, 2 * HEADS:2 * HEADS + P], adt[:, :], tri[:, :],
                                     start=True, stop=True).then_inc(cum_ps, 1)
                    wait(pe, vpe2_rd, n - 1)
                    project(4, Z0 + 4 * P).then_inc(z_ps, 1)

                def bc_products():
                    wait(pe, bct_rd, n + 1)
                    wait(pe, dtm_rd, n + 1)
                    nc.tensor.matmul(bank[1][:, 0:P], cv[:, KI, :], ct[:, cur.p, :], start=True, stop=True)
                    nc.tensor.transpose(bank[1][:, P:2 * P], cv[:, KI, :], ident[:, :]).then_inc(cb_ps, 1)

                def project_x(j):
                    wait(pe, z_ev, n + 1)
                    wait(pe, dif_rd, n + 1)
                    project(4 + j, X0 + 4 * j * P).then_inc(x_ps, 1)

                if cur and not prev:
                    bc_products()
                    pe.wait_ge(wx_in, 16)
                    project_x(0)
                if prev:
                    m = prev.n
                    wait(pe, xd_rd, m + 1)
                    wait(pe, xs_rd, m + 1)
                    for q in range(PIECES):
                        if q == 0:
                            wait(pe, m0_rd, m + 1)
                        else:
                            wait(pe, m_rd, (PIECES - 1) * m + q)
                        for h in range(q * PH, (q + 1) * PH):
                            t, j = h // TH, h % TH
                            at = t * TH * PITCH + j * P
                            ins = nc.tensor.matmul(bank[6 + t // 4][:, (t % 4) * P:(t % 4 + 1) * P],
                                                   xd_flat[:, at:at + P], L[:, q, h % PH, :],
                                                   start=(j == 0), stop=(j == TH - 1))
                        ins.then_inc(diag_ps, 1)
                        if cur and q == 0:
                            bc_products()
                        if cur and q == 1:
                            project_x(0)
                    wait(pe, S_rd, m + 1)
                    wait(pe, x2_rd, m)
                    if cur:
                        wait(pe, cb_rd, n + 1)
                    else:
                        wait(pe, off_ev, m)
                    for t in range(KI):
                        ins = nc.tensor.matmul(bank[t // 4][:, (t % 4) * P:(t % 4 + 1) * P], S[:, t * P:(t + 1) * P],
                                               ct[:, prev.p, :], start=True, stop=True)
                    ins.then_inc(off_ps, 1)
                    if cur:
                        wait(pe, bc_ev, n + 1)
                        wait(pe, z_ev, n + 1)
                    wait(pe, xdec_rd, m + 1)
                    for j in range(2):
                        ins = nc.tensor.matmul(bank[2 + j][:, :], bs[:, prev.p, :],
                                               xdec[:, 512 * j:512 * j + 512], start=True, stop=True)
                    ins.then_inc(state_ps, 1)
                if cur:
                    project_x(1)
                if prev:
                    wait(pe, y_rd, m + 1)
                    if isinstance(m, int) and m == 0:
                        pe.wait_ge(params, 1)
                    for k in range(KI):
                        ins = nc.tensor.matmul(bank[0][:, :], y[:, k, :], wout[:, k, :],
                                               start=(k == 0), stop=(k == KI - 1))
                    ins.then_inc(out_ps, 1)
                if nxt:
                    turn_xn(nxt)
                if cur:
                    wait(pe, xt_rd, n + 1)
                    for k in range(KI):
                        ins = nc.tensor.transpose(bank[6 + k // 4][:, (k % 4) * P:(k % 4 + 1) * P],
                                                  cv[:, k, :], ident[:, :])
                    ins.then_inc(xT_ps, 1)
                if prev:
                    wait(pe, sqs_rd, m + 1)
                    nc.tensor.matmul(bank[4][:, 0:1], sqs[:, :], ones[:, 0:1], start=True, stop=True)\
                        .then_inc(sq_ps, 1)

            turn_xn(Chunk(0, 0, 0))
            run_steps(pe, step)


def moe_stage(nc, x2_dram, xn2_dram, gate_w, gate_bias, w1, w2, w3, shared_gate, shared_up, shared_down, out):
    with ExitStack() as ctx:
        def sb(name, shape, dt=F32):
            return ctx.enter_context(nc.sbuf_tensor(name, shape, dt))

        def sem(name):
            return ctx.enter_context(nc.semaphore(name))

        bank = [ctx.enter_context(nc.psum_tensor(f"mbank{i}", [P, 512], F32)) for i in range(8)]
        SLOT_BANK = 6
        NBUF = 8

        ident = sb("m_ident", [P, P])
        tri_f = sb("tri_f", [P, P])
        tri = sb("m_tri", [P, P], BF16)
        ones = sb("m_ones", [P, P], BF16)
        half_exp = sb("m_half_exp", [P, 1])
        eps = sb("m_eps", [P, 1])
        carrier = sb("m_carrier", [P, 1])
        low = sb("low", [P, GROUPS, GROUPS])
        row_i = sb("row_i", [P, 1], I32)
        slot_i = sb("slot_i", [P, CAP], I32)
        slot_b = sb("slot_b", [P, CAP, EXPERTS], BF16)
        tile_i = sb("tile_i", [P, CHUNKS], I32)
        tile_f = sb("tile_f", [P, CHUNKS])
        row_f = sb("row_f", [P, 1])
        dump = sb("dump", [P, 1])
        one32 = sb("one32", [P, EXPERTS])
        zeros = sb("zeros", [P, HID])
        gw = sb("gw", [EXPERTS, HID])
        gwT = sb("gwT", [P, KH, EXPERTS])
        gbias = sb("gbias", [P, EXPERTS])
        sg = sb("sg", [P, KH, FS])
        su = sb("su", [P, KH, FS])
        sd = sb("sd", [P, KS, HID])
        x2i = sb("x2i", [P, 2, HID])
        xk = sb("xk", [P, 2, HID])
        stat = sb("m_stat", [P, 6])
        mv = sb("m_mv", [P, 2])
        vpe = sb("m_vpe", [P, 1])
        rstd = sb("m_rstd", [P, 1])
        xn = sb("m_xn", [P, 2, HID])
        xnT = sb("m_xnT", [P, 2, KH, P])
        tg = sb("tg", [P, KS * P])
        hT = sb("hT", [P, KS, P])
        oo = sb("oo", [P, 2, HID])
        tl = sb("tl", [P, EXPERTS])
        score = sb("score", [P, EXPERTS])
        sc = sb("sc", [P, EXPERTS])
        top8 = sb("top8", [P, GROUPS, 8])
        gsum = sb("gsum", [P, GROUPS])
        above = sb("above", [P, GROUPS, GROUPS])
        ties = sb("ties", [P, GROUPS, GROUPS])
        rank = sb("rank", [P, GROUPS])
        masked = sb("masked", [P, EXPERTS])
        best8 = sb("best8", [P, 8])
        gt = sb("gt", [P, EXPERTS])
        eq = sb("eq", [P, EXPERTS])
        eqc = sb("eqc", [P, EXPERTS])
        need = sb("need", [P, 1])
        sel = sb("sel", [P, 2, EXPERTS])
        selb = sb("selb", [P, 2, EXPERTS], BF16)
        wt = sb("wt", [P, EXPERTS])
        wsum = sb("wsum", [P, 1])
        base = sb("base", [P, EXPERTS])
        incl = sb("incl", [P, EXPERTS])
        posb = sb("posb", [P, 1, EXPERTS], BF16)
        onehot = sb("onehot", [P, CAP, EXPERTS], BF16)
        R = sb("R", [P, 2, EXPERTS, IDC], BF16)
        zb6 = sb("zb6", [P, EXPERTS * IDC], BF16)
        table = sb("table", [P, EXPERTS, IDC])
        tok = sb("tok", [P, EXPERTS])
        wslot = sb("wslot", [P, EXPERTS])
        unused = sb("unused", [P, EXPERTS])
        dest = sb("dest", [P, EXPERTS])
        w1s = sb("w1s", [P, NBUF, KH, F])
        w3s = sb("w3s", [P, NBUF, KH, F])
        w2s = sb("w2s", [P, NBUF, KF, HID])
        src_ix = [sb(f"src_ix{p}", [P, 1], U32) for p in range(2)]
        dst_ix = [sb(f"dst_ix{p}", [P, 1], U32) for p in range(2)]
        wcol = sb("wcol", [P, 2])
        xe = [sb(f"xe{p}", [P, HID]) for p in range(2)]
        xeT = sb("xeT", [P, 2, KH, P])
        te = sb("te", [P, F])
        ae = sb("ae", [P, F])
        hTe = sb("hTe", [P, 2, KF, P])
        gcar = sb("gcar", [P, 4])
        ob = [sb(f"ob{p}", [P, HID]) for p in range(2)]

        par_ld = sem("par_ld"); sh_ld = sem("sh_ld"); zero_st = sem("zero_st")
        x_ld = [sem("mx_ld0"), sem("mx_ld1")]
        xn_st = [sem("xn_st0"), sem("xn_st1")]
        o_st = [sem("o_st0"), sem("o_st1")]
        w_ld = [sem(f"w_ld{j}") for j in range(NBUF)]
        first_ld = sem("first_ld")
        xe_ld = [sem("xe_ld0"), sem("xe_ld1")]
        add_st = sem("add_st")
        g_set = sem("g_set"); g_set2 = sem("g_set2"); gw_ps = sem("gw_ps"); gwT_rd = sem("gwT_rd"); v_set = sem("v_set")
        xnT_ps = sem("m_xnT_ps"); gu_ps = sem("gu_ps"); lg_ps = sem("lg_ps"); cnt_ps = sem("cnt_ps")
        dn_ps = sem("dn_ps"); slot_ps = sem("slot_ps")
        xeT_ps = sem("xeT_ps"); gue_ps = sem("gue_ps"); dne_ps = sem("dne_ps")
        v_own = sem("mv_own"); v_cnt = sem("v_cnt"); n_own = sem("mn_own"); var_rd = sem("m_var_rd")
        xn_rd = sem("m_xn_rd"); h_rd = sem("h_rd"); sel_rd = sem("sel_rd"); wt_rd = sem("wt_rd"); oh_rd = sem("oh_rd")
        o_rd = sem("o_rd"); v_h = sem("v_h"); fin = sem("fin"); ix_rd = sem("ix_rd"); he_rd = sem("he_rd")
        v_he = sem("v_he"); wcol_rd = sem("wcol_rd")
        xnT_rd = sem("m_xnT_rd"); tg_rd = sem("tg_rd"); xk_rd = sem("xk_rd"); tl_rd = sem("tl_rd"); dn_rd = sem("dn_rd")
        xeT_rd = sem("xeT_rd"); te_rd = sem("te_rd"); ob_rd = sem("ob_rd")
        g_var = sem("mg_var"); rstd_rd = sem("m_rstd_rd"); g_car = sem("g_car"); g_car2 = sem("g_car2")
        g_wt = sem("g_wt")

        block = ctx.enter_context(nc.Block())

        x2_rows = x2_dram.rearrange("(c p) h -> c p h", p=P)
        xn2_rows = xn2_dram.rearrange("(c p) h -> c p h", p=P)
        out_rows = out.rearrange("(c p) h -> c p h", p=P)

        def column(c, a):
            return R[:, c.p, :, a:a + 1].rearrange("p e c -> p (e c)")

        def run_experts(eng, step):
            for e in range(NBUF):
                step(e, e, 0)
            with eng.Fori(1, EXPERTS // NBUF - 1) as i:
                for j in range(NBUF):
                    step(NBUF * i + j, j, i)
            for j in range(NBUF):
                step(EXPERTS - NBUF + j, j, EXPERTS // NBUF - 1)

        def turns(e, j, i):
            return NBUF // 2 * i + j // 2

        @block.sync
        def _(sp):
            sp.dma_start(x2i[:, 0, :], x2_rows[0, :, :]).then_inc(x_ld[0], 16)
            sp.dma_start(x2i[:, 1, :], x2_rows[1, :, :]).then_inc(x_ld[1], 16)
            sp.dma_start(gw[:, :], gate_w).then_inc(par_ld, 16)
            sp.dma_start(gbias[:, :], gate_bias.rearrange("(a n) -> a n", a=1).to_broadcast([P, EXPERTS]))\
                .then_inc(par_ld, 16)
            for dst, src in ((sg, shared_gate), (su, shared_up), (sd, shared_down)):
                sp.dma_start(dst[:, :, :], src.rearrange("(k p) f -> p k f", p=P)).then_inc(sh_ld, 16)

            def load_expert(e, j, done):
                for dst, src in ((w1s, w1), (w3s, w3), (w2s, w2)):
                    sp.dma_start(dst[:, bass.ds(j, 1), :, :].rearrange("p a k f -> p (a k) f"),
                                 src[bass.ds(e, 1), :, :].rearrange("a (k p) f -> p (a k) f", p=P)).then_inc(done, 16)

            def load_first(e):
                load_expert(e, e, first_ld)

            sp.wait_ge(g_set2, 1)
            sp.dma_start(out_rows[CHUNKS, :, :], zeros[:, :]).then_inc(zero_st, 16)

            def step(cur, prev, nxt):
                if cur:
                    n = cur.n
                    wait(sp, xn_rd, n + 1)
                    sp.dma_start(xn2_rows[n, :, :], xn[:, cur.p, :]).then_inc(xn_st[cur.p], 16)
                    wait(sp, xk_rd, n + 1)
                    if nxt:
                        sp.dma_start(x2i[:, cur.p, :], x2_rows[n + 2, :, :]).then_inc(x_ld[cur.p], 16)
                if cur and not isinstance(cur.n, int):
                    if cur.p == 1:
                        load_first(cur.h - 1)
                elif cur and cur.n >= CHUNKS - 3:
                    load_first(cur.n - (CHUNKS - NBUF))
                if prev:
                    wait(sp, o_rd, prev.n + 1)
                    sp.dma_start(out_rows[prev.n, :, :], oo[:, prev.p, :]).then_inc(o_st[prev.p], 16)

            run_steps(sp, step, loads_ahead=True)
            for p in range(2):
                sp.wait_ge(xn_st[p], 16 * CHUNKS // 2)
                sp.wait_ge(o_st[p], 16 * CHUNKS // 2)
            sp.wait_ge(zero_st, 16)

            with sp.Fori(1, EXPERTS // NBUF) as i:
                for j in range(NBUF):
                    wait(sp, dne_ps, NBUF * (i - 1) + j + 1)
                    load_expert(NBUF * i + j, j, w_ld[j])

        @block.gpsimd
        def _(pool):
            nc.gpsimd.memset(ident[:, :], 0.0).then_inc(g_set, 1)
            nc.gpsimd.memset(tri_f[:, :], 1.0).then_inc(g_set, 1)
            nc.gpsimd.memset(low[:, :, :], 1.0).then_inc(g_set, 1)
            nc.gpsimd.memset(half_exp[:, :], -0.5).then_inc(g_set, 1)
            nc.gpsimd.memset(eps[:, :], LN_EPS).then_inc(g_set, 1)
            nc.gpsimd.memset(zeros[:, :], 0.0).then_inc(g_set2, 1)
            pool.wait_ge(g_set, 5)
            nc.gpsimd.affine_select(out=ident[:, :], in_=ident[:, :], compare_op=ALU.not_equal, fill=1.0,
                                    base=0, pattern=[[-1, P]], channel_multiplier=1).then_inc(g_set2, 1)
            nc.gpsimd.affine_select(out=tri_f[:, :], in_=tri_f[:, :], compare_op=ALU.is_ge, fill=0.0,
                                    base=0, pattern=[[1, P]], channel_multiplier=-1).then_inc(g_set2, 1)
            nc.gpsimd.affine_select(out=low[:, :, :], in_=low[:, :, :], compare_op=ALU.is_gt, fill=0.0,
                                    base=0, pattern=[[1, GROUPS], [-1, GROUPS]], channel_multiplier=0)\
                .then_inc(g_set2, 1)
            nc.gpsimd.iota(row_i[:, :], pattern=[[0, 1]], base=0, channel_multiplier=1).then_inc(g_set2, 1)
            nc.gpsimd.iota(tile_i[:, :], pattern=[[1, CHUNKS]], base=0, channel_multiplier=0).then_inc(g_set2, 1)
            nc.gpsimd.iota(slot_i[:, :], pattern=[[1, CAP]], base=0, channel_multiplier=0)\
                .then_inc(g_set2, 1)

            def norm_root(c):
                wait(pool, var_rd, c.n + 1)
                Own(pool, g_var, 1, c.n).then(nc.gpsimd.tensor_tensor(vpe[:, :], mv[:, 1:2], eps[:, :], ALU.add))
                nc.gpsimd.tensor_tensor(rstd[:, :], vpe[:, :], half_exp[:, :], ALU.pow).then_inc(rstd_rd, 1)

            norm_root(Chunk(0, 0, 0))

            def split_weights(c, own):
                none = zeros[:, 0:EXPERTS]
                wait(pool, wt_rd, c.n + 1)
                wait(pool, slot_ps, c.n - 1)
                own.then(nc.gpsimd.tensor_tensor(column(c, 3), wt[:, :], none, ALU.add))
                own.then(nc.gpsimd.tensor_tensor(wt[:, :], wt[:, :], column(c, 3), ALU.subtract))
                own.then(nc.gpsimd.tensor_tensor(column(c, 4), wt[:, :], none, ALU.add))
                own.then(nc.gpsimd.tensor_tensor(wt[:, :], wt[:, :], column(c, 4), ALU.subtract))
                nc.gpsimd.tensor_tensor(column(c, 5), wt[:, :], none, ALU.add).then_inc(sel_rd, 1)

            def step(cur, prev, nxt):
                if nxt:
                    norm_root(nxt)
                if prev:
                    wait(pool, dn_rd, prev.n + 1)
                    wait(pool, xk_rd, prev.n + 1)
                    nc.gpsimd.tensor_tensor(oo[:, prev.p, :], oo[:, prev.p, :], xk[:, prev.p, :], ALU.add)\
                        .then_inc(o_rd, 1)
                if cur:
                    split_weights(cur, Own(pool, g_wt, 4, cur.n))

            run_steps(pool, step)
            for p in range(2):
                pool.wait_ge(xn_st[p], 16 * CHUNKS // 2)
                pool.wait_ge(o_st[p], 16 * CHUNKS // 2)
            pool.wait_ge(zero_st, 16)

            def gather(e, j, i):
                p = j % 2
                wait(pool, ix_rd, e + 1)
                wait(pool, xeT_ps, e - 1)
                wait(pool, g_car, e - 1)
                nc.gpsimd.tensor_tensor(gcar[:, p:p + 1], half_exp[:, :], half_exp[:, :], ALU.add).then_inc(g_car, 1)
                nc.gpsimd.indirect_dma_start(
                    out=xe[p][:, :], out_offset=None, in_=xn2_dram,
                    in_offset=bass.IndirectOffsetOnAxis(ap=src_ix[p][:, 0:1], axis=0),
                    bounds_check=TOKENS - 1, oob_is_err=True).then_inc(xe_ld[p], 16)

            def scatter(e, j, i):
                p = j % 2
                wait(pool, ob_rd, e + 1)
                wait(pool, add_st, 16 * e)
                wait(pool, wcol_rd, e + 1)
                wait(pool, g_car2, e - 1)
                nc.gpsimd.tensor_tensor(gcar[:, 2 + p:3 + p], half_exp[:, :], half_exp[:, :], ALU.add)\
                    .then_inc(g_car2, 1)
                nc.gpsimd.indirect_dma_start(
                    out=out, out_offset=bass.IndirectOffsetOnAxis(ap=dst_ix[p][:, 0:1], axis=0),
                    in_=ob[p][:, :], in_offset=None, bounds_check=TOKENS + P - 1, oob_is_err=True,
                    compute_op=ALU.add).then_inc(add_st, 16)

            def expert(e, j, i):
                if not (isinstance(e, int) and e + 2 >= EXPERTS):
                    gather(e + 2, (j + 2) % NBUF, i)
                if not (isinstance(e, int) and e < 1):
                    scatter(e - 1, (j - 1) % NBUF, i)

            gather(0, 0, 0)
            gather(1, 1, 0)
            run_experts(pool, expert)
            scatter(EXPERTS - 1, NBUF - 1, EXPERTS // NBUF - 1)
            pool.wait_ge(add_st, 16 * EXPERTS)

        @block.scalar
        def _(act):
            def take_xnT(c):
                wait(act, xnT_ps, c.n + 1)
                nc.scalar.activation(xnT[:, c.p, :, :], bank[0][:, :].rearrange("p (k t) -> p k t", t=P),
                                     ACT.Copy).then_inc(xnT_rd, 1)

            take_xnT(Chunk(0, 0, 0))

            def step(cur, prev, nxt):
                if cur:
                    wait(act, lg_ps, cur.n + 1)
                    wait(act, sel_rd, cur.n)
                    nc.scalar.activation(tl[:, :], bank[4][:, 0:EXPERTS], ACT.Tanh, scale=0.5).then_inc(tl_rd, 1)
                    wait(act, x_ld[cur.p], 16 * cur.h + 16)
                    wait(act, o_rd, cur.n - 1)
                    wait(act, xn_rd, cur.n + 1)
                    nc.scalar.activation(xk[:, cur.p, :], x2i[:, cur.p, :], ACT.Copy).then_inc(xk_rd, 1)
                if prev:
                    wait(act, dn_ps, prev.n + 1)
                    wait(act, o_st[prev.p], 16 * prev.h)
                    nc.scalar.activation(oo[:, prev.p, :], bank[3][:, :], ACT.Copy).then_inc(dn_rd, 1)
                if cur:
                    wait(act, gu_ps, cur.n + 1)
                    nc.scalar.activation(tg[:, :], bank[1][:, :], ACT.Tanh, scale=0.5).then_inc(tg_rd, 1)
                if nxt:
                    take_xnT(nxt)

            run_steps(act, step)

            def turn_expert(e, j, i):
                p = j % 2
                wait(act, xeT_ps, e + 1)
                nc.scalar.activation(xeT[:, p, :, :], bank[p][:, :].rearrange("p (k t) -> p k t", t=P), ACT.Copy)\
                    .then_inc(xeT_rd, 1)

            def weigh_expert(e, j, i):
                p = j % 2
                wait(act, dne_ps, e + 1)
                wait(act, wcol_rd, e + 1)
                wait(act, add_st, 16 * (e - 1))
                nc.scalar.activation(ob[p][:, :], bank[4 + p][:, :], ACT.Copy, scale=wcol[:, p:p + 1]).then_inc(ob_rd, 1)

            def expert(e, j, i):
                wait(act, gue_ps, e + 1)
                wait(act, he_rd, e)
                nc.scalar.activation(te[:, :], bank[2 + j % 2][:, 0:F], ACT.Tanh, scale=0.5).then_inc(te_rd, 1)
                if not (isinstance(e, int) and e + 1 >= EXPERTS):
                    turn_expert(e + 1, (j + 1) % NBUF, i)
                if not (isinstance(e, int) and e < 1):
                    weigh_expert(e - 1, (j - 1) % NBUF, i)

            turn_expert(0, 0, 0)
            run_experts(act, expert)
            weigh_expert(EXPERTS - 1, NBUF - 1, EXPERTS // NBUF - 1)

        @block.vector
        def _(dve):
            COUNT = 3

            def spread_of(c):
                wait(dve, x_ld[c.p], 16 * c.h + 16)
                nc.vector.bn_stats(stat[:, :], x2i[:, c.p, :]).then_inc(n_own, 1)
                wait(dve, n_own, c.n + 1)
                nc.vector.memset(carrier[:, :], 0.0)
                nc.vector.bn_aggr(mv[:, :], stat[:, :]).then_inc(var_rd, 1)

            def norm(c):
                wait(dve, rstd_rd, c.n + 1)
                wait(dve, var_rd, c.n + 1)
                wait(dve, xnT_ps, c.n - 1)
                wait(dve, xn_st[c.p], 16 * c.h)
                nc.vector.tensor_scalar(xn[:, c.p, :], x2i[:, c.p, :], mv[:, 0:1], rstd[:, 0:1],
                                        ALU.subtract, ALU.mult).then_inc(xn_rd, 1)

            def choose(c, own):
                wait(dve, tl_rd, c.n + 1)
                own.then(nc.vector.tensor_scalar(score[:, :], tl[:, :], 0.5, 0.5, ALU.mult, ALU.add))
                own.then(nc.vector.tensor_tensor(sc[:, :], score[:, :], gbias[:, :], ALU.add))
                nc.vector.memset(carrier[:, :], 0.0)
                for g in range(GROUPS):
                    ins = nc.vector.max(top8[:, g, :], sc[:, g * GE:(g + 1) * GE])
                own.then(ins)
                own.then(nc.vector.tensor_tensor(gsum[:, :], top8[:, :, 0], top8[:, :, 1], ALU.add))
                other = gsum[:, :].unsqueeze(1).to_broadcast([P, GROUPS, GROUPS])
                mine = gsum[:, :].unsqueeze(2).to_broadcast([P, GROUPS, GROUPS])
                nc.vector.tensor_tensor(above[:, :, :], other, mine, ALU.is_gt)
                own.then(nc.vector.tensor_tensor(ties[:, :, :], other, mine, ALU.is_equal))
                own.then(nc.vector.tensor_tensor(ties[:, :, :], ties[:, :, :], low[:, :, :], ALU.mult))
                own.then(nc.vector.tensor_tensor(above[:, :, :], above[:, :, :], ties[:, :, :], ALU.add))
                own.then(nc.vector.tensor_reduce(rank[:, :], above[:, :, :], AX.X, ALU.add))
                own.then(nc.vector.tensor_scalar(rank[:, :], rank[:, :], 2.0, None, ALU.is_lt))
                own.then(nc.vector.tensor_tensor(masked[:, :].rearrange("p (g e) -> p g e", e=GE),
                                                 sc[:, :].rearrange("p (g e) -> p g e", e=GE),
                                                 over_heads(rank[:, :], GE), ALU.mult))
                nc.vector.memset(carrier[:, :], 0.0)
                own.then(nc.vector.max(best8[:, :], masked[:, :]))
                fourth = best8[:, TOPK - 1:TOPK]
                nc.vector.tensor_scalar(gt[:, :], masked[:, :], fourth, None, ALU.is_gt)
                own.then(nc.vector.tensor_scalar(eq[:, :], masked[:, :], fourth, None, ALU.is_equal))
                nc.vector.tensor_reduce(need[:, :], gt[:, :], AX.X, ALU.add)
                own.then(nc.vector.tensor_tensor_scan(eqc[:, :], one32[:, :], eq[:, :], 0.0, ALU.mult, ALU.add))
                own.then(nc.vector.tensor_scalar(need[:, :], need[:, :], -1.0, float(TOPK), ALU.mult, ALU.add))
                own.then(nc.vector.scalar_tensor_tensor(out=eq[:, :], in0=eqc[:, :], scalar=need[:, 0:1], in1=eq[:, :],
                                                        op0=ALU.is_le, op1=ALU.mult))
                wait(dve, cnt_ps, c.n - 1)
                nc.vector.tensor_tensor(selb[:, c.p, :], gt[:, :], eq[:, :], ALU.add)
                own.then(nc.vector.tensor_tensor(sel[:, c.p, :], gt[:, :], eq[:, :], ALU.add))
                wait(dve, sel_rd, c.n)
                own.then(nc.vector.tensor_tensor(wt[:, :], score[:, :], sel[:, c.p, :], ALU.mult))
                own.then(nc.vector.tensor_reduce(wsum[:, :], wt[:, :], AX.X, ALU.add))
                own.then(nc.vector.tensor_scalar(wsum[:, :], wsum[:, :], 1e-20, None, ALU.add))
                own.then(nc.vector.reciprocal(wsum[:, :], wsum[:, :]))
                wait(dve, slot_ps, c.n - 1)
                nc.vector.tensor_scalar(column(c, 0), one32[:, :], tile_f[:, bass.ds(c.n, 1)], None, ALU.mult)
                nc.vector.tensor_scalar(wt[:, :], wt[:, :], wsum[:, 0:1], ROUTED_SCALE, ALU.mult, ALU.mult)\
                    .then_inc(wt_rd, 1)

            def count(c, own):
                wait(dve, cnt_ps, c.n + 1)
                own.then(nc.vector.tensor_tensor(incl[:, :], bank[5][:, 0:EXPERTS], base[:, :], ALU.add))
                nc.vector.tensor_tensor(base[:, :], bank[5][:, EXPERTS:2 * EXPERTS], base[:, :], ALU.add)
                own.then(nc.vector.tensor_tensor(incl[:, :], incl[:, :], sel[:, c.p, :], ALU.mult))
                own.then(nc.vector.tensor_scalar(posb[:, 0, :], incl[:, :], -1.0, None, ALU.add))
                wait(dve, slot_ps, c.n)
                nc.vector.tensor_tensor(onehot[:, :, :], slot_b[:, :, :], posb[:, :, :].to_broadcast([P, CAP, EXPERTS]),
                                        ALU.is_equal).then_inc(oh_rd, 1)
                wait(dve, oh_rd, c.n + 1)

            def step(cur, prev, nxt):
                if nxt:
                    spread_of(nxt)
                if prev:
                    wait(dve, tg_rd, prev.n + 1)
                    nc.vector.scalar_tensor_tensor(out=tg[:, :], in0=tg[:, :], scalar=1.0, in1=bank[1][:, :],
                                                   op0=ALU.add, op1=ALU.mult).then_inc(v_h, 1)
                    wait(dve, v_h, prev.n + 1)
                    wait(dve, dn_ps, prev.n)
                    nc.vector.scalar_tensor_tensor(out=hT[:, :, :].rearrange("p k t -> p (k t)"), in0=tg[:, :],
                                                   scalar=0.5, in1=bank[2][:, :], op0=ALU.mult, op1=ALU.mult)\
                        .then_inc(h_rd, 1)
                    count(prev, Own(dve, v_cnt, COUNT, prev.n))
                if nxt:
                    norm(nxt)
                if cur:
                    own = Own(dve, v_own, CHOICE, cur.n)
                    choose(cur, own)
                    own.close()

            CHOICE = 20
            dve.wait_ge(gw_ps, 1)
            nc.vector.tensor_copy(gwT[:, :, :], bank[0][:, 0:KH * EXPERTS].rearrange("p (k e) -> p k e", e=EXPERTS))\
                .then_inc(gwT_rd, 1)
            dve.wait_ge(par_ld, 32)
            spread_of(Chunk(0, 0, 0))
            norm(Chunk(0, 0, 0))
            dve.wait_ge(g_set2, 7)
            nc.vector.tensor_copy(tri[:, :], tri_f[:, :]).then_inc(v_set, 1)
            nc.vector.memset(ones[:, :], 1.0).then_inc(v_set, 1)
            nc.vector.memset(zb6[:, :], 0.0).then_inc(v_set, 1)
            nc.vector.tensor_copy(slot_b[:, :, :], over_heads(slot_i[:, :], EXPERTS)).then_inc(v_set, 1)
            nc.vector.tensor_copy(tile_f[:, :], tile_i[:, :]).then_inc(v_set, 1)
            nc.vector.tensor_copy(row_f[:, :], row_i[:, :]).then_inc(v_set, 1)
            nc.vector.memset(one32[:, :], 1.0).then_inc(v_set, 1)
            nc.vector.memset(base[:, :], 0.0).then_inc(v_set, 1)
            dve.wait_ge(v_set, 8)
            nc.vector.tensor_scalar(dump[:, :], row_f[:, :], float(TOKENS), None, ALU.add).then_inc(v_set, 1)
            for p in range(2):
                nc.vector.memset(R[:, p, :, 2:3], 1.0).then_inc(v_set, 1)
                nc.vector.tensor_scalar(R[:, p, :, 1:2].rearrange("p e c -> p (e c)"), one32[:, :], row_f[:, 0:1],
                                        None, ALU.mult).then_inc(v_set, 1)
            dve.wait_ge(v_set, 13)
            dve.wait_ge(gwT_rd, 1)
            run_steps(dve, step)

            dve.wait_ge(slot_ps, CHUNKS)
            nc.vector.tensor_copy(table[:, :, :],
                                  bank[SLOT_BANK][:, 0:EXPERTS * IDC].rearrange("p (e c) -> p e c", c=IDC))\
                .then_inc(fin, 1)
            dve.wait_ge(fin, 1)
            cell = [table[:, :, a:a + 1].rearrange("p e c -> p (e c)") for a in range(IDC)]
            nc.vector.scalar_tensor_tensor(out=tok[:, :], in0=cell[0], scalar=float(P), in1=cell[1],
                                           op0=ALU.mult, op1=ALU.add)
            nc.vector.tensor_scalar(unused[:, :], cell[2], -1.0, 1.0, ALU.mult, ALU.add)
            nc.vector.tensor_tensor(wslot[:, :], cell[3], cell[4], ALU.add).then_inc(fin, 1)
            dve.wait_ge(fin, 2)
            nc.vector.tensor_tensor(wslot[:, :], wslot[:, :], cell[5], ALU.add)
            nc.vector.scalar_tensor_tensor(out=dest[:, :], in0=unused[:, :], scalar=dump[:, 0:1], in1=tok[:, :],
                                           op0=ALU.mult, op1=ALU.add).then_inc(fin, 1)
            dve.wait_ge(fin, 3)

            def source(e, j, i):
                p = j % 2
                wait(dve, xe_ld[p], 16 * turns(e, j, i))
                nc.vector.tensor_scalar(src_ix[p][:, :], tok[:, bass.ds(e, 1)], 1.0, None, ALU.mult).then_inc(ix_rd, 1)

            def target(e, j, i):
                p = j % 2
                wait(dve, add_st, 16 * (e - 1))
                nc.vector.tensor_scalar(dst_ix[p][:, :], dest[:, bass.ds(e, 1)], 1.0, None, ALU.mult)
                nc.vector.tensor_scalar(wcol[:, p:p + 1], wslot[:, bass.ds(e, 1)], 1.0, None, ALU.mult)\
                    .then_inc(wcol_rd, 1)

            def expert(e, j, i):
                b = bank[2 + j % 2]
                if not (isinstance(e, int) and e + 2 >= EXPERTS):
                    source(e + 2, (j + 2) % NBUF, i if j < NBUF - 2 else i + 1)
                wait(dve, te_rd, e + 1)
                nc.vector.scalar_tensor_tensor(out=ae[:, :], in0=te[:, :], scalar=1.0, in1=b[:, 0:F],
                                               op0=ALU.add, op1=ALU.mult).then_inc(v_he, 1)
                wait(dve, v_he, e + 1)
                wait(dve, dne_ps, e - 1)
                nc.vector.scalar_tensor_tensor(out=hTe[:, j % 2, :, :].rearrange("p k t -> p (k t)"), in0=ae[:, :],
                                               scalar=0.5, in1=b[:, F:2 * F], op0=ALU.mult, op1=ALU.mult)\
                    .then_inc(he_rd, 1)
                target(e, j, i)

            source(0, 0, 0)
            source(1, 1, 0)
            run_experts(dve, expert)

        @block.tensor
        def _(pe):
            pe.wait_ge(g_set2, 2)
            pe.wait_ge(par_ld, 32)
            for k in range(KH):
                ins = nc.tensor.transpose(bank[0][:, k * EXPERTS:(k + 1) * EXPERTS], gw[:, k * P:(k + 1) * P],
                                          ident[0:EXPERTS, 0:EXPERTS])
            ins.then_inc(gw_ps, 1)
            pe.wait_ge(gwT_rd, 1)

            def turn_xn(c):
                wait(pe, xn_rd, c.n + 1)
                wait(pe, xnT_rd, c.n)
                for k in range(KH):
                    ins = nc.tensor.transpose(bank[0][:, k * P:(k + 1) * P], xn[:, c.p, k * P:(k + 1) * P],
                                              ident[:, :])
                ins.then_inc(xnT_ps, 1)

            def step(cur, prev, nxt):
                if cur:
                    n = cur.n
                if prev:
                    m = prev.n
                    wait(pe, sel_rd, m + 1)
                    wait(pe, oh_rd, m)
                    nc.tensor.matmul(bank[5][:, 0:EXPERTS], tri[:, :], selb[:, prev.p, :], start=True, stop=True)
                    nc.tensor.matmul(bank[5][:, EXPERTS:2 * EXPERTS], ones[:, :], selb[:, prev.p, :],
                                     start=True, stop=True).then_inc(cnt_ps, 1)
                if cur:
                    wait(pe, xnT_rd, n + 1)
                    wait(pe, tl_rd, n)
                    for k in range(KH):
                        ins = nc.tensor.matmul(bank[4][:, 0:EXPERTS], xnT[:, cur.p, k, :], gwT[:, k, :],
                                               start=(k == 0), stop=(k == KH - 1))
                    ins.then_inc(lg_ps, 1)
                    if isinstance(n, int) and n == 0:
                        pe.wait_ge(sh_ld, 48)
                if prev:
                    wait(pe, h_rd, m + 1)
                    wait(pe, dn_rd, m)
                    for f in range(KS):
                        ins = nc.tensor.matmul(bank[3][:, :], hT[:, f, :], sd[:, f, :],
                                               start=(f == 0), stop=(f == KS - 1))
                    ins.then_inc(dn_ps, 1)
                if cur:
                    wait(pe, h_rd, n)
                    for b, w in ((1, sg), (2, su)):
                        for f in range(KS):
                            for k in range(KH):
                                ins = nc.tensor.matmul(bank[b][:, f * P:(f + 1) * P], w[:, k, f * P:(f + 1) * P],
                                                       xnT[:, cur.p, k, :], start=(k == 0), stop=(k == KH - 1))
                    ins.then_inc(gu_ps, 1)
                if nxt:
                    turn_xn(nxt)
                if not prev:
                    pe.wait_ge(v_set, 13)
                    nc.tensor.matmul(bank[SLOT_BANK][:, 0:EXPERTS * IDC], ones[:, :], zb6[:, :], start=True, stop=True,
                                     skip_group_check=True)
                if prev:
                    wait(pe, oh_rd, m + 1)
                    for e in range(EXPERTS):
                        ins = nc.tensor.matmul(bank[SLOT_BANK][:, e * IDC:(e + 1) * IDC], onehot[:, :, e],
                                               R[:, prev.p, e, :], start=False, stop=True, skip_group_check=True)
                    ins.then_inc(slot_ps, 1)

            turn_xn(Chunk(0, 0, 0))
            run_steps(pe, step)

            def turn(e, j, i):
                p = j % 2
                wait(pe, xe_ld[p], 16 * turns(e, j, i) + 16)
                wait(pe, xeT_rd, e - 1)
                for k in range(KH):
                    ins = nc.tensor.transpose(bank[p][:, k * P:(k + 1) * P], xe[p][:, k * P:(k + 1) * P], ident[:, :])
                ins.then_inc(xeT_ps, 1)

            def down(e, j, i):
                p = j % 2
                wait(pe, he_rd, e + 1)
                wait(pe, ob_rd, e - 1)
                for f in range(KF):
                    ins = nc.tensor.matmul(bank[4 + p][:, :], hTe[:, p, f, :], w2s[:, j, f, :],
                                           start=(f == 0), stop=(f == KF - 1))
                ins.then_inc(dne_ps, 1)

            def expert(e, j, i):
                p = j % 2
                wait(pe, w_ld[j], 48 * i)
                wait(pe, xeT_rd, e + 1)
                wait(pe, he_rd, e - 1)
                for b, w in ((0, w1s), (F, w3s)):
                    for f in range(KF):
                        for k in range(KH):
                            ins = nc.tensor.matmul(bank[2 + p][:, b + f * P:b + (f + 1) * P],
                                                   w[:, j, k, f * P:(f + 1) * P], xeT[:, p, k, :],
                                                   start=(k == 0), stop=(k == KH - 1))
                ins.then_inc(gue_ps, 1)
                if not (isinstance(e, int) and e + 1 >= EXPERTS):
                    turn(e + 1, (j + 1) % NBUF, i if j < NBUF - 1 else i + 1)
                if not (isinstance(e, int) and e < 1):
                    down(e - 1, (j - 1) % NBUF, i)

            pe.wait_ge(first_ld, 48 * NBUF)
            pe.wait_ge(o_rd, CHUNKS)
            pe.wait_ge(fin, 1)
            turn(0, 0, 0)
            run_experts(pe, expert)
            down(EXPERTS - 1, NBUF - 1, EXPERTS // NBUF - 1)


def build(nc, x, W_in, b_in, conv_w, conv_b, A_log, dt_bias, D_param, norm_w, W_out, b_out,
          gate_w, gate_bias, w1, w2, w3, shared_gate, shared_up, shared_down, out):
    cum_dram = nc.dram_tensor("cum_rows", (2, HEADS, P), F32, kind="Internal").ap()
    ecum_dram = nc.dram_tensor("ecum_rows", (2, HEADS, P), F32, kind="Internal").ap()
    x2_dram = nc.dram_tensor("x2_rows", (TOKENS, HID), F32, kind="Internal").ap()
    xn2_dram = nc.dram_tensor("xn2_rows", (TOKENS, HID), F32, kind="Internal").ap()
    mamba_stage(nc, x, W_in, b_in, conv_w, conv_b, A_log, dt_bias, D_param, norm_w, W_out, b_out,
                cum_dram, ecum_dram, x2_dram)
    moe_stage(nc, x2_dram, xn2_dram, gate_w, gate_bias, w1, w2, w3, shared_gate, shared_up, shared_down, out)


_INS = ["L0_attn_x", "L0_attn_W_in", "L0_attn_b_in", "L0_attn_conv_w", "L0_attn_conv_b", "L0_attn_A_log",
        "L0_attn_dt_bias", "L0_attn_D_param", "L0_attn_norm_w", "L0_attn_W_out", "L0_attn_b_out",
        "L0_ffn_gate_w", "L0_ffn_gate_bias", "L0_ffn_w1", "L0_ffn_w2", "L0_ffn_w3",
        "L0_ffn_shared_gate", "L0_ffn_shared_up", "L0_ffn_shared_down"]


def kernel(**inputs):
    import numpy as np
    import concourse.bacc as bacc
    from concourse.bass_utils import run_bass_kernel_spmd

    nc = bacc.Bacc("TRN2", target_bir_lowering=False, num_devices=1)
    arrays, args = {}, []
    for name in _INS:
        a = np.ascontiguousarray(inputs[name])
        arrays[f"in_{name}"] = a
        args.append(nc.dram_tensor(f"in_{name}", a.shape, mybir.dt.from_np(a.dtype), kind="ExternalInput").ap())
    out = nc.dram_tensor("out_0", (TOKENS + P, HID), F32, kind="ExternalOutput").ap()
    build(nc, *args, out)
    r = run_bass_kernel_spmd(nc, [arrays], core_ids=[0])
    got = r.results[0]["out_0"]
    return got[:TOKENS].reshape(4, 512, 512)
```
